# Optimizing a Trainium2 kernel written in Bass

```python
import numpy as np
import jax
import jax.numpy as jnp

def _softmax(x, axis=-1):
    return jax.nn.softmax(x, axis=axis)

def _gelu(x):
    return jax.nn.gelu(x, approximate=True)

def _silu(x):
    return jax.nn.silu(x)

def _sigmoid(x):
    return jax.nn.sigmoid(x)

def _layernorm(x, axis=-1, eps=1e-05):
    m = jnp.mean(x, axis=axis, keepdims=True)
    v = jnp.var(x, axis=axis, keepdims=True)
    return (x - m) / jnp.sqrt(v + eps)

def _scatter_add(tgt, idx, src, axis=0):
    return tgt.at[idx].add(src)

def _segment_sum(src, seg, n):
    return jax.ops.segment_sum(src, seg, n)
kernel_name = 'mk_metaformer_d4_conv_nhwc256_r2_9624d7'

def setup_inputs(seed: int=0):
    np.random.seed(seed)
    _w = jnp.asarray

    def _rec_inputs():
        import jax
        import jax.numpy as jnp
        _gk = jax.random.key(seed)
        x = 7.22e-05 + 1 * jax.random.normal(jax.random.fold_in(_gk, 1), (8, 32, 32, 128), jnp.float32)
        return x
    x = _rec_inputs()

    def _L0_conv_setup():
        import jax, jax.numpy as jnp
        import numpy as np
        from jax import lax
        B, H, W, C = (8, 32, 32, 128)
        MAX_SCALE = 4
        R_RED = 8
        SCALES = [2 ** i for i in range(1, MAX_SCALE + 1)]
        EPS = 1e-07
        BN_EPS = 0.001

        def _box_sum(x, k):
            c = x.shape[-1]
            ker = jnp.ones((k, k, 1, c), x.dtype)
            return lax.conv_general_dilated(x, ker, window_strides=(1, 1), padding='SAME', dimension_numbers=('NHWC', 'HWIO', 'NHWC'), feature_group_count=c)
        key = jax.random.key(seed)
        ks = jax.random.split(key, 3)
        Cr = C // R_RED
        return {'x': jax.random.normal(ks[0], (B, H, W, C), jnp.float32), 'w1': jax.random.normal(ks[1], (C, Cr), jnp.float32) * 0.05, 'b1': jnp.zeros((Cr,), jnp.float32), 'w2': jax.random.normal(ks[2], (Cr, C), jnp.float32) * 0.05, 'b2': jnp.zeros((C,), jnp.float32), 'gamma': jnp.ones((C,), jnp.float32), 'beta': jnp.zeros((C,), jnp.float32), 'moving_mean': jnp.zeros((C,), jnp.float32), 'moving_var': jnp.ones((C,), jnp.float32)}
    _L0_conv_all = _L0_conv_setup()
    _L0_conv_in = {k: v for k, v in _L0_conv_all.items() if k in ('w1', 'b1', 'w2', 'b2', 'gamma', 'beta', 'moving_mean', 'moving_var')}
    del _L0_conv_all

    def _L0_ffn_setup():
        import math
        import jax, jax.numpy as jnp
        import numpy as np
        CAPACITY_FACTOR = 1.25
        key = jax.random.key(seed)
        ks = jax.random.split(key, 5)
        B, L, D, F, E = (8, 4096, 128, 512, 8)
        h = jax.random.normal(ks[0], (B, L, D), dtype=jnp.float32)
        gate_w = jax.random.normal(ks[1], (D, E), dtype=jnp.float32) * 0.02
        gate_b = jnp.zeros((E,), dtype=jnp.float32)
        w1 = jax.random.normal(ks[2], (E, D, F), dtype=jnp.float32) * (1.0 / math.sqrt(D))
        b1 = jnp.zeros((E, F), dtype=jnp.float32)
        w2 = jax.random.normal(ks[3], (E, F, D), dtype=jnp.float32) * (1.0 / math.sqrt(F))
        b2 = jnp.zeros((E, D), dtype=jnp.float32)
        return {'h': h, 'gate_w': gate_w, 'gate_b': gate_b, 'w1': w1, 'b1': b1, 'w2': w2, 'b2': b2}
    _L0_ffn_all = _L0_ffn_setup()
    _L0_ffn_in = {k: v for k, v in _L0_ffn_all.items() if k in ('gate_w', 'gate_b', 'w1', 'b1', 'w2', 'b2')}
    del _L0_ffn_all

    def _L1_conv_setup():
        import jax, jax.numpy as jnp
        import numpy as np
        K = 3
        FILTERS = 128
        GC = 16
        G = FILTERS // GC
        key = jax.random.key(seed)
        ks = jax.random.split(key, 5)
        B, H, W, C = (8, 32, 32, FILTERS)
        red = FILTERS // 4
        x = jax.random.normal(ks[0], (B, H, W, C), dtype=jnp.float32)
        W1 = jax.random.normal(ks[1], (C, red), dtype=jnp.float32) * 0.05
        b1 = jnp.zeros((red,), dtype=jnp.float32)
        W2 = jax.random.normal(ks[2], (red, K * K * G), dtype=jnp.float32) * 0.05
        b2 = jnp.zeros((K * K * G,), dtype=jnp.float32)
        return {'x': x, 'W1': W1, 'b1': b1, 'W2': W2, 'b2': b2}
    _L1_conv_all = _L1_conv_setup()
    _L1_conv_in = {k: v for k, v in _L1_conv_all.items() if k in ('W1', 'b1', 'W2', 'b2')}
    del _L1_conv_all

    def _L1_ffn_setup():
        import jax, jax.numpy as jnp
        import numpy as np
        TOP_K = 2
        key = jax.random.key(seed)
        ks = jax.random.split(key, 4)
        B, L, D, H, E = (8, 2048, 128, 512, 8)
        s = 0.02
        return {'x': jax.random.normal(ks[0], (B, L, D), jnp.float32), 'Wg': jax.random.normal(ks[1], (D, E), jnp.float32) * s, 'bg': jnp.zeros((E,), jnp.float32), 'W1': jax.random.normal(ks[2], (E, D, H), jnp.float32) * s, 'b1': jnp.zeros((E, H), jnp.float32), 'W2': jax.random.normal(ks[3], (E, H, D), jnp.float32) * s, 'b2': jnp.zeros((E, D), jnp.float32)}
    _L1_ffn_all = _L1_ffn_setup()
    _L1_ffn_in = {k: v for k, v in _L1_ffn_all.items() if k in ('Wg', 'bg', 'W1', 'b1', 'W2', 'b2')}
    del _L1_ffn_all

    def _L2_conv_setup():
        import jax, jax.numpy as jnp
        import numpy as np
        IN_F, OUT_F = (128, 128)
        GRID, ORDER = (5, 3)
        K = GRID + ORDER + 1
        EPS_MINMAX = 1e-07
        EPS_BN = 0.001

        def _bn(z, gamma, beta, mean, var):
            return gamma * (z - mean) * jax.lax.rsqrt(var + EPS_BN) + beta
        key = jax.random.key(seed)
        ks = jax.random.split(key, 4)
        x = jax.random.normal(ks[0], (32, 32, 32, IN_F), dtype=jnp.float32)
        he = lambda k, shape, fan_in: jax.random.normal(k, shape, jnp.float32) * np.sqrt(2.0 / fan_in)
        base_weight = he(ks[1], (IN_F, OUT_F), IN_F)
        spline_weight = he(ks[2], (OUT_F, IN_F, K), IN_F * K)
        spline_scaler = jnp.ones((OUT_F, IN_F), jnp.float32)
        return {'x': x, 'base_weight': base_weight, 'spline_weight': spline_weight, 'spline_scaler': spline_scaler, 'bn_base_gamma': jnp.ones((OUT_F,), jnp.float32), 'bn_base_beta': jnp.zeros((OUT_F,), jnp.float32), 'bn_base_mean': jnp.zeros((OUT_F,), jnp.float32), 'bn_base_var': jnp.ones((OUT_F,), jnp.float32), 'bn_spline_gamma': jnp.ones((OUT_F,), jnp.float32), 'bn_spline_beta': jnp.zeros((OUT_F,), jnp.float32), 'bn_spline_mean': jnp.zeros((OUT_F,), jnp.float32), 'bn_spline_var': jnp.ones((OUT_F,), jnp.float32)}
    _L2_conv_all = _L2_conv_setup()
    _L2_conv_in = {k: v for k, v in _L2_conv_all.items() if k in ('base_weight', 'spline_weight', 'spline_scaler', 'bn_base_gamma', 'bn_base_beta', 'bn_base_mean', 'bn_base_var', 'bn_spline_gamma', 'bn_spline_beta', 'bn_spline_mean', 'bn_spline_var')}
    del _L2_conv_all

    def _L2_ffn_setup():
        import jax, jax.numpy as jnp
        import numpy as np
        B, T, D, H, E = (16, 2048, 128, 256, 8)
        key = jax.random.key(seed)
        ks = jax.random.split(key, 5)
        x = jax.random.normal(ks[0], (B, T, D), dtype=jnp.float32)
        gate_w = jax.random.normal(ks[1], (D, E), dtype=jnp.float32) * 0.02
        gate_b = jnp.zeros((E,), dtype=jnp.float32)
        W1 = jax.random.normal(ks[2], (E, D, H), dtype=jnp.float32) * 0.02
        b1 = jnp.zeros((E, H), dtype=jnp.float32)
        W2 = jax.random.normal(ks[3], (E, H, D), dtype=jnp.float32) * 0.02
        b2 = jnp.zeros((E, D), dtype=jnp.float32)
        return {'x': x, 'gate_w': gate_w, 'gate_b': gate_b, 'W1': W1, 'b1': b1, 'W2': W2, 'b2': b2}
    _L2_ffn_all = _L2_ffn_setup()
    _L2_ffn_in = {k: v for k, v in _L2_ffn_all.items() if k in ('gate_w', 'gate_b', 'W1', 'b1', 'W2', 'b2')}
    del _L2_ffn_all

    def _L3_conv_setup():
        import jax, jax.numpy as jnp
        import numpy as np
        GAMMA = 2.0
        EPS = 1e-12
        key = jax.random.key(seed)
        k1, k2 = jax.random.split(key)
        B, H, W_, C = (8, 56, 56, 128)
        x = jax.random.normal(k1, (B, H, W_, C), dtype=jnp.float32)
        W = jax.random.normal(k2, (C, C), dtype=jnp.float32) * 0.05
        return {'x': x, 'W': W}
    _L3_conv_all = _L3_conv_setup()
    _L3_conv_in = {k: v for k, v in _L3_conv_all.items() if k in ('W',)}
    del _L3_conv_all

    def _L3_ffn_setup():
        import jax, jax.numpy as jnp
        import numpy as np
        D_MODEL = 128
        N_EXPERTS = 16
        HIDDEN = 256
        SCALE = 0.02
        key = jax.random.key(seed)
        ks = jax.random.split(key, 5)
        x = jax.random.normal(ks[0], (4, 4096, D_MODEL), dtype=jnp.float32)
        gate_w = jax.random.normal(ks[1], (D_MODEL, N_EXPERTS), dtype=jnp.float32) * SCALE
        gate_b = jnp.zeros((N_EXPERTS,), dtype=jnp.float32)
        w1 = jax.random.normal(ks[2], (N_EXPERTS, D_MODEL, HIDDEN), dtype=jnp.float32) * SCALE
        w2 = jax.random.normal(ks[3], (N_EXPERTS, D_MODEL, HIDDEN), dtype=jnp.float32) * SCALE
        w3 = jax.random.normal(ks[4], (N_EXPERTS, HIDDEN, D_MODEL), dtype=jnp.float32) * SCALE
        return {'x': x, 'gate_w': gate_w, 'gate_b': gate_b, 'w1': w1, 'w2': w2, 'w3': w3}
    _L3_ffn_all = _L3_ffn_setup()
    _L3_ffn_in = {k: v for k, v in _L3_ffn_all.items() if k in ('gate_w', 'gate_b', 'w1', 'w2', 'w3')}
    del _L3_ffn_all
    return {'x': x, 'L0_conv_w1': _L0_conv_in['w1'], 'L0_conv_b1': _L0_conv_in['b1'], 'L0_conv_w2': _L0_conv_in['w2'], 'L0_conv_b2': _L0_conv_in['b2'], 'L0_conv_gamma': _L0_conv_in['gamma'], 'L0_conv_beta': _L0_conv_in['beta'], 'L0_conv_moving_mean': _L0_conv_in['moving_mean'], 'L0_conv_moving_var': _L0_conv_in['moving_var'], 'L0_ffn_gate_w': _L0_ffn_in['gate_w'], 'L0_ffn_gate_b': _L0_ffn_in['gate_b'], 'L0_ffn_w1': _L0_ffn_in['w1'], 'L0_ffn_b1': _L0_ffn_in['b1'], 'L0_ffn_w2': _L0_ffn_in['w2'], 'L0_ffn_b2': _L0_ffn_in['b2'], 'L1_conv_W1': _L1_conv_in['W1'], 'L1_conv_b1': _L1_conv_in['b1'], 'L1_conv_W2': _L1_conv_in['W2'], 'L1_conv_b2': _L1_conv_in['b2'], 'L1_ffn_Wg': _L1_ffn_in['Wg'], 'L1_ffn_bg': _L1_ffn_in['bg'], 'L1_ffn_W1': _L1_ffn_in['W1'], 'L1_ffn_b1': _L1_ffn_in['b1'], 'L1_ffn_W2': _L1_ffn_in['W2'], 'L1_ffn_b2': _L1_ffn_in['b2'], 'L2_conv_base_weight': _L2_conv_in['base_weight'], 'L2_conv_spline_weight': _L2_conv_in['spline_weight'], 'L2_conv_spline_scaler': _L2_conv_in['spline_scaler'], 'L2_conv_bn_base_gamma': _L2_conv_in['bn_base_gamma'], 'L2_conv_bn_base_beta': _L2_conv_in['bn_base_beta'], 'L2_conv_bn_base_mean': _L2_conv_in['bn_base_mean'], 'L2_conv_bn_base_var': _L2_conv_in['bn_base_var'], 'L2_conv_bn_spline_gamma': _L2_conv_in['bn_spline_gamma'], 'L2_conv_bn_spline_beta': _L2_conv_in['bn_spline_beta'], 'L2_conv_bn_spline_mean': _L2_conv_in['bn_spline_mean'], 'L2_conv_bn_spline_var': _L2_conv_in['bn_spline_var'], 'L2_ffn_gate_w': _L2_ffn_in['gate_w'], 'L2_ffn_gate_b': _L2_ffn_in['gate_b'], 'L2_ffn_W1': _L2_ffn_in['W1'], 'L2_ffn_b1': _L2_ffn_in['b1'], 'L2_ffn_W2': _L2_ffn_in['W2'], 'L2_ffn_b2': _L2_ffn_in['b2'], 'L3_conv_W': _L3_conv_in['W'], 'L3_ffn_gate_w': _L3_ffn_in['gate_w'], 'L3_ffn_gate_b': _L3_ffn_in['gate_b'], 'L3_ffn_w1': _L3_ffn_in['w1'], 'L3_ffn_w2': _L3_ffn_in['w2'], 'L3_ffn_w3': _L3_ffn_in['w3']}

def reference(x, L0_conv_w1, L0_conv_b1, L0_conv_w2, L0_conv_b2, L0_conv_gamma, L0_conv_beta, L0_conv_moving_mean, L0_conv_moving_var, L0_ffn_gate_w, L0_ffn_gate_b, L0_ffn_w1, L0_ffn_b1, L0_ffn_w2, L0_ffn_b2, L1_conv_W1, L1_conv_b1, L1_conv_W2, L1_conv_b2, L1_ffn_Wg, L1_ffn_bg, L1_ffn_W1, L1_ffn_b1, L1_ffn_W2, L1_ffn_b2, L2_conv_base_weight, L2_conv_spline_weight, L2_conv_spline_scaler, L2_conv_bn_base_gamma, L2_conv_bn_base_beta, L2_conv_bn_base_mean, L2_conv_bn_base_var, L2_conv_bn_spline_gamma, L2_conv_bn_spline_beta, L2_conv_bn_spline_mean, L2_conv_bn_spline_var, L2_ffn_gate_w, L2_ffn_gate_b, L2_ffn_W1, L2_ffn_b1, L2_ffn_W2, L2_ffn_b2, L3_conv_W, L3_ffn_gate_w, L3_ffn_gate_b, L3_ffn_w1, L3_ffn_w2, L3_ffn_w3):
    import jax
    import jax.numpy as jnp

    def _L0_conv_ref(x, w1, b1, w2, b2, gamma, beta, moving_mean, moving_var):
        import jax, jax.numpy as jnp
        import numpy as np
        from jax import lax
        B, H, W, C = (8, 32, 32, 128)
        MAX_SCALE = 4
        R_RED = 8
        SCALES = [2 ** i for i in range(1, MAX_SCALE + 1)]
        EPS = 1e-07
        BN_EPS = 0.001

        def _box_sum(x, k):
            c = x.shape[-1]
            ker = jnp.ones((k, k, 1, c), x.dtype)
            return lax.conv_general_dilated(x, ker, window_strides=(1, 1), padding='SAME', dimension_numbers=('NHWC', 'HWIO', 'NHWC'), feature_group_count=c)
        xmin = jnp.min(x, axis=(1, 2, 3), keepdims=True)
        xmax = jnp.max(x, axis=(1, 2, 3), keepdims=True)
        x = (x - xmin) / (xmax - xmin + EPS)
        measures = jnp.stack([_box_sum(x, k) for k in SCALES], axis=-1)
        log_r = jnp.log(jnp.asarray(SCALES, jnp.float32))
        log_m = jnp.log(measures + EPS)
        lr_c = log_r - log_r.mean()
        alphas = jnp.einsum('bhwcs,s->bhwc', log_m, lr_c) / jnp.sum(lr_c ** 2)
        squeeze = alphas.mean(axis=(1, 2))
        excite = jax.nn.sigmoid(jax.nn.relu(squeeze @ w1 + b1) @ w2 + b2)
        ols_est = alphas[..., None] * log_r
        a = log_m - log_m.mean(axis=-1, keepdims=True)
        b = ols_est - ols_est.mean(axis=-1, keepdims=True)
        sim = (a * b).sum(-1) / (jnp.linalg.norm(a, axis=-1) * jnp.linalg.norm(b, axis=-1) + EPS)
        alpha_norm = (alphas - moving_mean) / jnp.sqrt(moving_var + BN_EPS) * gamma + beta
        x = x * excite[:, None, None, :]
        return sim * jax.nn.sigmoid(alpha_norm) + (1.0 - sim) * x

    def _L0_ffn_ref(h, gate_w, gate_b, w1, b1, w2, b2):
        import math
        import jax, jax.numpy as jnp
        import numpy as np
        CAPACITY_FACTOR = 1.25
        B, L, D = h.shape
        E = gate_w.shape[1]
        T = B * L
        C = max(1, math.ceil(CAPACITY_FACTOR * T / E))
        x = h.reshape(T, D)
        logits = x @ gate_w + gate_b
        probs = jax.nn.softmax(logits, axis=-1)
        idx = jnp.argmax(probs, axis=-1)
        prb = jnp.take_along_axis(probs, idx[:, None], axis=1)[:, 0]
        one_hot = jax.nn.one_hot(idx, E, dtype=jnp.float32)
        pos = (jnp.cumsum(one_hot, axis=0) * one_hot).sum(-1).astype(jnp.int32) - 1
        kept = pos < C
        pos_safe = jnp.where(kept, pos, C)
        buf = jnp.zeros((E, C, D), dtype=h.dtype).at[idx, pos_safe].set(x, mode='drop')
        hmid = jax.nn.relu(jnp.einsum('ecd,edf->ecf', buf, w1) + b1[:, None, :])
        ybuf = jnp.einsum('ecf,efd->ecd', hmid, w2) + b2[:, None, :]
        pos_g = jnp.minimum(pos, C - 1)
        y_tok = ybuf[idx, pos_g] * (prb * kept)[:, None]
        y = y_tok.reshape(B, L, D)
        y = jnp.nan_to_num(y, nan=0.0, posinf=10000.0, neginf=-10000.0)
        return y

    def _L1_conv_ref(x, W1, b1, W2, b2):
        import jax, jax.numpy as jnp
        import numpy as np
        K = 3
        FILTERS = 128
        GC = 16
        G = FILTERS // GC
        b, h, w, c = x.shape
        kk = K * K
        wgt = jnp.einsum('bhwc,cd->bhwd', x, W1) + b1
        wgt = jnp.einsum('bhwd,de->bhwe', wgt, W2) + b2
        wgt = wgt.transpose(0, 3, 1, 2).reshape(b, G, 1, kk, h, w)
        pad = (K - 1) // 2
        xp = jnp.pad(x, ((0, 0), (pad, K - 1 - pad), (pad, K - 1 - pad), (0, 0)))
        patches = jnp.stack([xp[:, i:i + h, j:j + w, :] for i in range(K) for j in range(K)], axis=3)
        out = patches.reshape(b, h, w, kk * c).transpose(0, 3, 1, 2).reshape(b, G, GC, kk, h, w)
        out = jnp.einsum('bgokhw,bgckhw->bgchw', wgt, out)
        out = out.reshape(b, FILTERS, h, w).transpose(0, 2, 3, 1)
        return out

    def _L1_ffn_ref(x, Wg, bg, W1, b1, W2, b2):
        import jax, jax.numpy as jnp
        import numpy as np
        TOP_K = 2
        B, L, D = x.shape
        E = W1.shape[0]
        xf = x.reshape(-1, D)
        gate_logits = xf @ Wg + bg
        top_w, top_i = jax.lax.top_k(gate_logits, TOP_K)
        top_w = jax.nn.softmax(top_w, axis=-1)
        w_dense = jnp.sum(jax.nn.one_hot(top_i, E, dtype=xf.dtype) * top_w[..., None], axis=1)
        out = jnp.zeros_like(xf)
        for e in range(E):
            h = jax.nn.gelu(xf @ W1[e] + b1[e], approximate=False)
            out = out + w_dense[:, e:e + 1] * (h @ W2[e] + b2[e])
        return out.reshape(B, L, D)

    def _L2_conv_ref(x, base_weight, spline_weight, spline_scaler, bn_base_gamma, bn_base_beta, bn_base_mean, bn_base_var, bn_spline_gamma, bn_spline_beta, bn_spline_mean, bn_spline_var):
        import jax, jax.numpy as jnp
        import numpy as np
        IN_F, OUT_F = (128, 128)
        GRID, ORDER = (5, 3)
        K = GRID + ORDER + 1
        EPS_MINMAX = 1e-07
        EPS_BN = 0.001

        def _bn(z, gamma, beta, mean, var):
            return gamma * (z - mean) * jax.lax.rsqrt(var + EPS_BN) + beta
        B, H, W, _ = x.shape
        xf = x.reshape(-1, IN_F)
        base = xf @ base_weight
        base = jax.nn.silu(_bn(base, bn_base_gamma, bn_base_beta, bn_base_mean, bn_base_var))
        x_min = jnp.min(xf, axis=0, keepdims=True)
        x_max = jnp.max(xf, axis=0, keepdims=True)
        xn = (xf - x_min) / (x_max - x_min + EPS_MINMAX)
        knots = jnp.linspace(-1.0, 1.0, K, dtype=jnp.float32)
        basis = jnp.maximum(0.0, 1.0 - jnp.abs(xn[:, :, None] - knots[None, None, :]))
        w = (spline_weight * spline_scaler[:, :, None]).reshape(OUT_F, IN_F * K)
        spline = basis.reshape(-1, IN_F * K) @ w.T
        spline = _bn(spline, bn_spline_gamma, bn_spline_beta, bn_spline_mean, bn_spline_var)
        out = base + spline
        return out.reshape(B, H, W, OUT_F)

    def _L2_ffn_ref(x, gate_w, gate_b, W1, b1, W2, b2):
        import jax, jax.numpy as jnp
        import numpy as np
        B, T, D, H, E = (16, 2048, 128, 256, 8)
        Bb, Tt, Dd = x.shape
        Ee = gate_w.shape[1]
        xf = x.reshape(-1, Dd)
        N = xf.shape[0]
        logits = xf @ gate_w + gate_b
        probs = jax.nn.softmax(logits, axis=-1)
        top2_vals, top2_idx = jax.lax.top_k(probs, 2)
        cw = jnp.zeros((N, Ee), dtype=xf.dtype).at[jnp.arange(N)[:, None], top2_idx].add(top2_vals)

        def step(acc, params):
            w1, bb1, w2, bb2, we = params
            h = jax.nn.gelu(xf @ w1 + bb1, approximate=False)
            y = h @ w2 + bb2
            return (acc + we[:, None] * y, None)
        out, _ = jax.lax.scan(step, jnp.zeros_like(xf), (W1, b1, W2, b2, cw.T))
        return out.reshape(Bb, Tt, Dd)

    def _L3_conv_ref(x, W):
        import jax, jax.numpy as jnp
        import numpy as np
        GAMMA = 2.0
        EPS = 1e-12
        B, H, Wd, C = x.shape
        hw = H * Wd
        t = jnp.einsum('bhwc,cd->bhwd', x, W).reshape(B, hw, C)
        xf = x.reshape(B, hw, C)
        inv_norm = jax.lax.rsqrt(jnp.maximum(jnp.sum(xf * xf, axis=-1, keepdims=True), EPS))
        xn = xf * inv_norm
        sim = jnp.einsum('bic,bjc->bij', xn, xn)
        sim = jnp.power(jax.nn.relu(sim), GAMMA)
        y = jnp.einsum('bij,bjc->bic', sim, t)
        return y.reshape(B, H, Wd, C)

    def _L3_ffn_ref(x, gate_w, gate_b, w1, w2, w3):
        import jax, jax.numpy as jnp
        import numpy as np
        D_MODEL = 128
        N_EXPERTS = 16
        HIDDEN = 256
        SCALE = 0.02
        n_experts = w1.shape[0]
        logits = jnp.einsum('bsd,de->bse', x, gate_w) + gate_b
        probs = jax.nn.softmax(logits, axis=-1)
        top_probs, top_idx = jax.lax.top_k(probs, 2)
        top_probs = top_probs / jnp.sum(top_probs, axis=-1, keepdims=True)
        dispatch = jnp.sum(jax.nn.one_hot(top_idx, n_experts, dtype=x.dtype) * top_probs[..., None], axis=-2)
        h1 = jnp.einsum('bsd,edh->bseh', x, w1)
        h2 = jnp.einsum('bsd,edh->bseh', x, w2)
        hidden = jax.nn.silu(h1) * h2
        expert_out = jnp.einsum('bseh,eho->bseo', hidden, w3)
        return jnp.einsum('bseo,bse->bso', expert_out, dispatch)

    def _gn(v, G=32, eps=1e-05):
        B_, H_, W_, C_ = v.shape
        g = v.reshape(B_, H_, W_, G, C_ // G)
        m = jnp.mean(g, axis=(1, 2, 4), keepdims=True)
        s = jnp.var(g, axis=(1, 2, 4), keepdims=True)
        return ((g - m) / jnp.sqrt(s + eps)).reshape(v.shape)

    def _ln_c(v, eps=1e-06):
        m = jnp.mean(v, axis=-1, keepdims=True)
        s = jnp.var(v, axis=-1, keepdims=True)
        return (v - m) / jnp.sqrt(s + eps)

    def _ln_t(v, eps=1e-05):
        m = jnp.mean(v, axis=-1, keepdims=True)
        s = jnp.var(v, axis=-1, keepdims=True)
        return (v - m) / jnp.sqrt(s + eps)

    def _to_tokens(v):
        B_, H_, W_, C_ = v.shape
        return v.reshape(B_, H_ * W_, C_)

    def _from_tokens(t, like):
        return t.reshape(like.shape)
    x = x + _L0_conv_ref(_ln_c(x), L0_conv_w1, L0_conv_b1, L0_conv_w2, L0_conv_b2, L0_conv_gamma, L0_conv_beta, L0_conv_moving_mean, L0_conv_moving_var)
    t = _to_tokens(x)
    t = t + _L0_ffn_ref(_ln_t(t), L0_ffn_gate_w, L0_ffn_gate_b, L0_ffn_w1, L0_ffn_b1, L0_ffn_w2, L0_ffn_b2)
    x = _from_tokens(t, x)
    x = x + _L1_conv_ref(_ln_c(x), L1_conv_W1, L1_conv_b1, L1_conv_W2, L1_conv_b2)
    t = _to_tokens(x)
    t = t + _L1_ffn_ref(_ln_t(t), L1_ffn_Wg, L1_ffn_bg, L1_ffn_W1, L1_ffn_b1, L1_ffn_W2, L1_ffn_b2)
    x = _from_tokens(t, x)
    x = x + _L2_conv_ref(_ln_c(x), L2_conv_base_weight, L2_conv_spline_weight, L2_conv_spline_scaler, L2_conv_bn_base_gamma, L2_conv_bn_base_beta, L2_conv_bn_base_mean, L2_conv_bn_base_var, L2_conv_bn_spline_gamma, L2_conv_bn_spline_beta, L2_conv_bn_spline_mean, L2_conv_bn_spline_var)
    t = _to_tokens(x)
    t = t + _L2_ffn_ref(_ln_t(t), L2_ffn_gate_w, L2_ffn_gate_b, L2_ffn_W1, L2_ffn_b1, L2_ffn_W2, L2_ffn_b2)
    x = _from_tokens(t, x)
    x = x + _L3_conv_ref(_ln_c(x), L3_conv_W)
    t = _to_tokens(x)
    t = t + _L3_ffn_ref(_ln_t(t), L3_ffn_gate_w, L3_ffn_gate_b, L3_ffn_w1, L3_ffn_w2, L3_ffn_w3)
    x = _from_tokens(t, x)
    return x

_drawn_inputs = setup_inputs


def setup_inputs(seed=0):
    import zlib

    import numpy as np

    out = dict(_drawn_inputs(seed))
    spreads = {'L0_conv_b1': (0.0, 2.0),
     'L0_conv_b2': (0.0, 2.0),
     'L0_conv_gamma': (1.0, 0.2),
     'L0_conv_beta': (0.0, 0.365),
     'L0_conv_moving_mean': (0.0, 0.338),
     'L0_conv_moving_var': (1.0, 0.2),
     'L0_ffn_gate_b': (0.0, 0.1),
     'L0_ffn_b1': (0.0, 0.8),
     'L0_ffn_b2': (0.0, 0.615),
     'L1_conv_b1': (0.0, 0.1),
     'L1_conv_b2': (0.0, 0.1),
     'L1_ffn_bg': (0.0, 0.1),
     'L1_ffn_b1': (0.0, 0.472),
     'L1_ffn_b2': (0.0, 0.1),
     'L2_conv_spline_scaler': (1.0, 0.2),
     'L2_conv_bn_base_gamma': (1.0, 0.2),
     'L2_conv_bn_base_beta': (0.0, 0.1),
     'L2_conv_bn_base_mean': (0.0, 0.1),
     'L2_conv_bn_base_var': (1.0, 0.2),
     'L2_conv_bn_spline_gamma': (1.0, 0.2),
     'L2_conv_bn_spline_beta': (0.0, 0.1),
     'L2_conv_bn_spline_mean': (0.0, 0.1),
     'L2_conv_bn_spline_var': (1.0, 0.2),
     'L2_ffn_gate_b': (0.0, 0.656),
     'L2_ffn_b1': (0.0, 0.8),
     'L2_ffn_b2': (0.0, 0.296),
     'L3_ffn_gate_b': (0.0, 0.8)}
    factors = {'L0_conv_w1': 63.644,
     'L0_conv_w2': 61.486,
     'L1_ffn_W1': 3.768,
     'L2_ffn_gate_w': 4.346,
     'L2_ffn_W1': 8.0,
     'L2_ffn_W2': 8.0,
     'L3_ffn_gate_w': 8.0,
     'L3_ffn_w1': 8.0,
     'L3_ffn_w2': 8.0,
     'L3_ffn_w3': 8.0}
    for name, (base, spread) in spreads.items():
        noise = np.random.default_rng([zlib.crc32(name.encode()), seed]).standard_normal(out[name].shape)
        drawn = base * np.exp(spread * noise) if base else spread * noise
        out[name] = jnp.asarray(drawn.astype(out[name].dtype))
    for name, factor in factors.items():
        out[name] = (out[name] * factor).astype(out[name].dtype)
    return out
```

```python
from contextlib import ExitStack

import numpy as np

import concourse.bass as bass
from concourse import mybir

ALU = mybir.AluOpType
ACT = mybir.ActivationFunctionType
AX = mybir.AxisListType
F32 = mybir.dt.float32
BF16 = mybir.dt.bfloat16
I32 = mybir.dt.int32

P = 128
C = 128
B, HH, WW = 8, 32, 32
IMG = HH * WW
N = B * IMG
NT = N // P
TPB = IMG // P
BANK = 512
ROW = C + 2
REGION = N + P
NOWHERE = 1 << 20
EMAX = 16
LN2 = float(np.log(2.0))

FFN = [
    dict(E=8, F=512, K=1, over_chosen=False, act=ACT.Relu, gated=False, capacity=1280, guard=True),
    dict(E=8, F=512, K=2, over_chosen=True, act=ACT.Gelu, gated=False, capacity=None, guard=False),
    dict(E=8, F=256, K=2, over_chosen=False, act=ACT.Gelu, gated=False, capacity=None, guard=False),
    dict(E=16, F=256, K=2, over_chosen=True, act=ACT.Silu, gated=True, capacity=None, guard=False),
]


class Sem:

    def __init__(self, handle):
        self.h = handle
        self.base = 0


class Chain:

    def __init__(self, eng, sem, before):
        self.eng, self.sem, self.before, self.n = eng, sem, before, 0

    def note(self, ins):
        self.n += 1
        ins.then_inc(self.sem.h, 1)

    def settle(self):
        self.eng.wait_ge(self.sem.h, self.before + self.n)

    def link(self, ins):
        self.note(ins)
        self.settle()


def past(i, k):
    return not isinstance(i, int) or i >= k


def steps(eng, n, unroll, body):
    for u in range(unroll):
        body(u, u)
    if n > unroll:
        with eng.Fori(1, n // unroll) as g:
            for u in range(unroll):
                body(g * unroll + u, u)


def spelled_out(n, unroll, body):
    for i in range(n):
        body(i, i % unroll)


class Core:

    def __init__(self, nc, ctx, ins, out):
        self.nc, self.ctx, self.ins, self.out = nc, ctx, ins, out
        self.sems = {}

        def sb(name, shape, dt=F32):
            return ctx.enter_context(nc.sbuf_tensor(name, shape, dt))

        self.sb = sb
        self.x = sb("residual", [P, NT, C])
        self.ch = sb("channel_major", [P, B * 34 * 34])
        self.rows0 = sb("rows_first_choice", [P, NT, ROW])
        self.rows1 = sb("rows_second_choice", [P, NT, ROW])
        self.wts = sb("expert_weights", [P, 12288])
        self.ps = ctx.enter_context(nc.psum_tensor("psum", [P, 8, BANK], F32))
        self.xn = self.flat(self.rows0)[:, 0:N].rearrange("p (t c) -> p t c", c=C)
        self.mixed = self.flat(self.rows1)[:, 0:N]

        self.ident = sb("identity", [P, P])
        self.tri = sb("upper_triangle", [P, P], BF16)
        self.ones = sb("ones_square", [P, P], BF16)
        self.rank = sb("expert_rank", [P, EMAX])
        self.region = sb("region_start", [P, EMAX])
        self.partition = sb("partition_index", [P, 1])
        self.tile_no = sb("tile_number", [P, 144])
        self.token_id = sb("token_id", [P, NT, 2], I32)
        self.token_id1 = sb("token_id_one_choice", [P, NT], I32)
        self.pad_rows = sb("pad_rows", [P, ROW])
        self.zeros = sb("zeros", [P, C])
        self.eps = sb("epsilons", [P, 4])
        self.eps3, self.eps5, self.eps6, self.eps7 = (self.eps[:, j:j + 1] for j in range(4))
        self.stats = sb("bn_stats", [P, NT, 6])
        self.mean = sb("mean", [P, NT])
        self.var4 = sb("four_variances", [P, NT])
        self.rstd = sb("rstd", [P, NT])
        self.counts = sb("expert_counts", [P, EMAX])
        self.tile_expert = sb("tile_expert", [1, 144], I32)
        self.tile_row = sb("tile_row", [1, 144], I32)

        self.dispatched = nc.dram_tensor("dispatched", (EMAX * REGION + P, ROW), F32, kind="Internal").ap()
        self.returned = nc.dram_tensor("returned", (N * 2, C), F32, kind="Internal").ap()

    @staticmethod
    def flat(t):
        return t[:].rearrange("p t c -> p (t c)")

    def sem(self, name):
        if name not in self.sems:
            self.sems[name] = Sem(self.ctx.enter_context(self.nc.semaphore(name)))
        return self.sems[name]

    def advance(self, **counts):
        for name, n in counts.items():
            self.sems[name].base += n


def constants(k):
    nc = k.nc
    s_set = k.sem("const_set")
    s_made = k.sem("const_made")
    s_x = k.sem("x_loaded")
    x_dram = k.ins["x"].rearrange("b h w c -> (b h w) c").rearrange("(t p) c -> p t c", p=P)
    with ExitStack() as ctx, nc.Block() as block:
        int_rank = ctx.enter_context(nc.sbuf_tensor("int_rank", [P, EMAX], I32))
        int_region = ctx.enter_context(nc.sbuf_tensor("int_region", [P, EMAX], I32))
        int_part = ctx.enter_context(nc.sbuf_tensor("int_part", [P, 1], I32))
        int_tile = ctx.enter_context(nc.sbuf_tensor("int_tile", [P, 144], I32))

        @block.sync
        def _(sp):
            for b in range(B):
                sp.dma_start(k.x[:, b * TPB:(b + 1) * TPB, :], x_dram[:, b * TPB:(b + 1) * TPB, :]).then_inc(s_x.h, 16)
            sp.wait_ge(s_x.h, 16 * B)
            sp.wait_ge(s_made.h, 4)
            sp.dma_start(k.dispatched[EMAX * REGION:EMAX * REGION + P, :], k.pad_rows[:]).then_inc(s_x.h, 16)
            sp.dma_start(k.dispatched[8 * REGION:8 * REGION + P, :], k.pad_rows[:]).then_inc(s_x.h, 16)
            sp.wait_ge(s_x.h, 16 * (B + 2))

        @block.vector
        def _(dve):
            dve.memset(k.ident[:], 0.0).then_inc(s_set.h, 1)
            dve.memset(k.tri[:], 1.0).then_inc(s_set.h, 1)
            dve.memset(k.ones[:], 1.0).then_inc(s_set.h, 1)
            dve.memset(k.pad_rows[:], 0.0).then_inc(s_set.h, 1)
            dve.memset(k.zeros[:], 0.0).then_inc(s_set.h, 1)
            for j, value in enumerate((1e-3, 1e-5, 1e-6, 1e-7)):
                dve.memset(k.eps[:, j:j + 1], value)
            dve.wait_ge(s_made.h, 8)
            dve.tensor_copy(k.rank[:], int_rank[:])
            dve.tensor_copy(k.region[:], int_region[:])
            dve.tensor_copy(k.partition[:], int_part[:])
            dve.tensor_copy(k.tile_no[:], int_tile[:])

        @block.gpsimd
        def _(pool):
            pool.wait_ge(s_set.h, 4)
            pool.affine_select(out=k.ident[:], in_=k.ident[:], compare_op=ALU.not_equal, fill=1.0, base=0,
                               pattern=[[-1, P]], channel_multiplier=1).then_inc(s_made.h, 1)
            pool.affine_select(out=k.tri[:], in_=k.tri[:], compare_op=ALU.is_ge, fill=0.0, base=0,
                               pattern=[[1, P]], channel_multiplier=-1).then_inc(s_made.h, 1)
            pool.iota(k.pad_rows[:].bitcast(I32)[:, C:C + 1], pattern=[[0, 1]], base=NOWHERE,
                      channel_multiplier=0).then_inc(s_made.h, 1)
            pool.iota(int_rank[:], pattern=[[-1, EMAX]], base=EMAX, channel_multiplier=0).then_inc(s_made.h, 1)
            pool.iota(int_region[:], pattern=[[REGION, EMAX]], base=-1, channel_multiplier=0).then_inc(s_made.h, 1)
            pool.iota(int_part[:], pattern=[[0, 1]], base=0, channel_multiplier=1).then_inc(s_made.h, 1)
            pool.iota(int_tile[:], pattern=[[1, 144]], base=0, channel_multiplier=0).then_inc(s_made.h, 1)
            pool.iota(k.token_id[:], pattern=[[2 * P, NT], [1, 2]], base=0, channel_multiplier=2).then_inc(s_made.h, 1)
            pool.iota(k.token_id1[:], pattern=[[P, NT]], base=0, channel_multiplier=1)
    k.advance(const_set=5, const_made=8, x_loaded=16 * (B + 2))


STAT_OPS = 6


def finish_stats(dve, k, ch):
    def col(j):
        return k.stats[:, :, j:j + 1].rearrange("p t a -> p (t a)")
    ch.note(dve.tensor_tensor(k.mean[:], col(1), col(4), ALU.add))
    ch.note(dve.tensor_tensor(k.var4[:], col(1), col(4), ALU.subtract))
    ch.note(dve.tensor_tensor(k.rstd[:], col(2), col(5), ALU.add))
    ch.settle()
    ch.note(dve.tensor_scalar(k.mean[:], k.mean[:], 0.5, None, ALU.mult))
    ch.link(dve.tensor_tensor(k.var4[:], k.var4[:], k.var4[:], ALU.mult))
    ch.link(dve.scalar_tensor_tensor(out=k.var4[:], in0=k.rstd[:], scalar=4.0 / C, in1=k.var4[:], op0=ALU.mult, op1=ALU.add))


def norm_mixer(k, layer):
    nc = k.nc
    choices = FFN[layer - 1]["K"] if layer else 0
    s_y, s_v = k.sem("rows_back0"), k.sem("vector_step")
    s_y1 = k.sem("rows_back1")
    s_root, s_rstd = k.sem("root_ready"), k.sem("rstd_ready")
    s_norm, s_turned, s_evac = k.sem("norm_ready"), k.sem("turned"), k.sem("turned_copied")
    s_pad = k.sem("border_cleared")
    padded = layer == 1
    per = choices + TPB
    norm3 = layer == 3
    ch4 = k.ch[:].rearrange("p (b h w) -> p b h w", b=B, h=34)
    with ExitStack() as ctx, nc.Block() as block:
        back = ctx.enter_context(nc.sbuf_tensor(f"back_{layer}", [P, 2, TPB, max(choices, 1) * C], F32)) if choices else None
        src = k.returned[0:N * choices, :].rearrange("(t p k) c -> p t (k c)", p=P, k=choices) if choices else None

        if choices:
            @block.sync
            def _(sp):
                def load(b, u):
                    if past(b, 2):
                        sp.wait_ge(s_v.h, s_v.base + (b - 2) * per + choices)
                    sp.dma_start(back[:, u], src[:, bass.ds(b * TPB, TPB), :]).then_inc((s_y, s_y1)[u].h, 16)
                spelled_out(B, 2, load)

        @block.vector
        def _(dve):
            def first(b, u):
                ch = Chain(dve, s_v, s_v.base + b * per)
                tiles = bass.ds(b * TPB, TPB)
                if choices:
                    dve.wait_ge((s_y, s_y1)[u].h, (s_y, s_y1)[u].base + (b - u) * 8 + 16)
                    for c in range(choices):
                        ins = dve.tensor_tensor(k.x[:, tiles, :], k.x[:, tiles, :], back[:, u, :, c * C:(c + 1) * C], ALU.add)
                        ch.link(ins)
                for t in range(TPB):
                    one = bass.ds(b * TPB + t, 1)
                    ch.note(dve.bn_stats(k.stats[:, one, :].rearrange("p a c -> p (a c)"),
                                         k.x[:, one, :].rearrange("p a c -> p (a c)")))
            spelled_out(B, 2, first)
            ch = Chain(dve, s_v, s_v.base + B * per)
            ch.settle()
            finish_stats(dve, k, ch)
            dve.wait_ge(s_root.h, s_root.base + 1)
            dve.reciprocal(k.rstd[:], k.rstd[:]).then_inc(s_rstd.h, 1)
            dve.wait_ge(s_rstd.h, s_rstd.base + 1)
            if padded:
                dve.memset(k.ch[:], 0.0).then_inc(s_pad.h, 1)

            def second(b, u):
                for t in range(TPB):
                    one = bass.ds(b * TPB + t, 1)
                    ins = dve.tensor_scalar(k.xn[:, one, :].rearrange("p a c -> p (a c)"),
                                            k.x[:, one, :].rearrange("p a c -> p (a c)"),
                                            k.mean[:, one], k.rstd[:, one],
                                            ALU.subtract, ALU.mult)
                ins.then_inc(s_norm.h, 1)
            spelled_out(B, 2, second)

        @block.tensor
        def _(pe):
            def turn(b, u):
                pe.wait_ge(s_norm.h, s_norm.base + b + 1)
                if past(b, 2):
                    pe.wait_ge(s_evac.h, s_evac.base + b - 1)
                for t in range(TPB):
                    bank, at = 2 * u + t // 4, (t % 4) * P
                    ins = pe.transpose(k.ps[:, bank, at:at + P],
                                       k.xn[:, bass.ds(b * TPB + t, 1), :].rearrange("p a c -> p (a c)"), k.ident[:])
                ins.then_inc(s_turned.h, 1)
            spelled_out(B, 2, turn)

        @block.scalar
        def _(act):
            act.wait_ge(s_v.h, s_v.base + B * per + STAT_OPS)
            act.activation(k.rstd[:], k.var4[:], ACT.Sqrt, bias=k.eps6, scale=0.25).then_inc(s_root.h, 1)
            if padded:
                act.wait_ge(s_pad.h, s_pad.base + 1)

            def evac(b, u):
                act.wait_ge(s_turned.h, s_turned.base + b + 1)
                src_ps = k.ps[:, 2 * u:2 * u + 2, :]
                if padded:
                    dst = ch4[:, bass.ds(b, 1), 1:33, 1:33].rearrange("p a h w -> p (a h) w")
                    ins = act.activation(dst, src_ps.rearrange("p a (h w) -> p (a h) w", w=WW), ACT.Copy)
                else:
                    ins = act.activation(k.ch[:, bass.ds(b * IMG, IMG)], src_ps.rearrange("p a n -> p (a n)"), ACT.Copy)
                ins.then_inc(s_evac.h, 1)
            spelled_out(B, 2, evac)
    k.advance(vector_step=B * per + STAT_OPS, root_ready=1, rstd_ready=1, norm_ready=B, turned=B, turned_copied=B)
    if choices:
        k.advance(rows_back0=16 * B // 2, rows_back1=16 * B // 2)
    if padded:
        k.advance(border_cleared=1)


def ffn_inputs(k, layer):
    i = k.ins
    if layer == 0:
        return i["L0_ffn_gate_w"], i["L0_ffn_gate_b"], i["L0_ffn_w1"], i["L0_ffn_b1"], i["L0_ffn_w2"], i["L0_ffn_b2"]
    if layer == 1:
        return i["L1_ffn_Wg"], i["L1_ffn_bg"], i["L1_ffn_W1"], i["L1_ffn_b1"], i["L1_ffn_W2"], i["L1_ffn_b2"]
    if layer == 2:
        return i["L2_ffn_gate_w"], i["L2_ffn_gate_b"], i["L2_ffn_W1"], i["L2_ffn_b1"], i["L2_ffn_W2"], i["L2_ffn_b2"]
    return i["L3_ffn_gate_w"], i["L3_ffn_gate_b"], i["L3_ffn_w1"], i["L3_ffn_w2"], i["L3_ffn_w3"], None


def norm_router(k, layer):
    nc, f = k.nc, FFN[layer]
    E, K, F = f["E"], f["K"], f["F"]
    T = N * K // P + E
    G = E + (1 if K == 2 else 0)
    route_ops = 15 + 4 * bool(f["capacity"]) if K == 1 else 25
    gate_w, gate_b, w1, b1, w2, b2 = ffn_inputs(k, layer)
    names = ("vector_step", "root_ready", "rstd_ready", "norm_ready", "turned", "turned_copied",
             "mix_turned", "mix_added", "gate_loaded", "logits_ready", "shifted", "exp_ready", "chosen", "ranked",
             "slots_ready", "rows_sent", "rows_copied", "counts_final", "pads_ready", "weights_loaded", "plan_step")
    s = {n: k.sem(n) for n in names}
    per1 = 1 + TPB
    stats_done = B * per1 + STAT_OPS

    def wait(eng, name, n):
        eng.wait_ge(s[name].h, s[name].base + n)

    with ExitStack() as ctx, nc.Block() as block:
        def sb(name, shape, dt=F32):
            return ctx.enter_context(nc.sbuf_tensor(f"{name}_{layer}", shape, dt))

        gw = sb("gate_w", [P, E])
        gb = sb("gate_b", [P, E])
        turned = sb("turned_rows", [P, 2, IMG])
        lg = sb("logits", [P, TPB, E])
        lg2 = sb("logits_rest", [P, TPB, E])
        oh = [sb("choice0", [P, TPB, E]), sb("choice1", [P, TPB, E])]
        top = sb("top", [P, 4, TPB])
        ex = sb("exponents", [P, TPB, G])
        exo = sb("exponentials", [P, TPB, G])
        msk = sb("chosen_mask", [P, TPB + 1, E], BF16)
        pos = sb("position", [P, TPB, E])
        posr = sb("position_row", [P, TPB, E])
        tmp = sb("routing_tmp", [P, TPB, E])
        wsum = sb("weight_sum", [P, 3, TPB])
        slotf = sb("slot_float", [P, 2, TPB])
        slot = sb("slot", [P, 2, 2, TPB], I32)
        padf = sb("pad_slot_float", [P, E])
        padi = sb("pad_slot", [P, E], I32)
        nti = sb("tiles_int", [P, E], I32)
        ntf = sb("tiles", [P, 3, E])
        acc = sb("plan", [P, 3, 144])
        rows = [k.rows0, k.rows1]

        @block.sync
        def _(sp):
            sp.dma_start(gw[:], gate_w).then_inc(s["gate_loaded"].h, 16)
            sp.dma_start(gb[:], gate_b.partition_broadcast(P)).then_inc(s["gate_loaded"].h, 16)
            for dst, src in expert_weight_loads(k, layer):
                sp.dma_start(dst, src).then_inc(s["weights_loaded"].h, 16)

        @block.vector
        def _(dve):
            def first(b, u):
                ch = Chain(dve, s["vector_step"], s["vector_step"].base + b * per1)
                tiles = bass.ds(b * TPB, TPB)
                wait(dve, "mix_turned", b + 1)
                xs = k.x[:, tiles, :].rearrange("p t c -> p (t c)")
                ch.link(dve.tensor_tensor(xs, xs, k.ps[:, 2 * u:2 * u + 2, :].rearrange("p a n -> p (a n)"), ALU.add))
                for t in range(TPB):
                    one = bass.ds(b * TPB + t, 1)
                    ins = dve.bn_stats(k.stats[:, one, :].rearrange("p a c -> p (a c)"),
                                       k.x[:, one, :].rearrange("p a c -> p (a c)"))
                    ch.note(ins)
            spelled_out(B, 2, first)
            ch = Chain(dve, s["vector_step"], s["vector_step"].base + B * per1)
            ch.settle()
            finish_stats(dve, k, ch)
            wait(dve, "root_ready", 1)
            dve.reciprocal(k.rstd[:], k.rstd[:]).then_inc(s["rstd_ready"].h, 1)
            dve.memset(k.counts[:], 0.0).then_inc(s["rstd_ready"].h, 1)
            dve.memset(msk[:], 0.0).then_inc(s["rstd_ready"].h, 1)
            wait(dve, "rstd_ready", 3)
            wait(dve, "gate_loaded", 32)

            base = s["vector_step"].base + stats_done

            def second(b, u):
                ch = Chain(dve, s["vector_step"], base + b * route_ops)
                tiles = bass.ds(b * TPB, TPB)
                for t in range(TPB):
                    one = bass.ds(b * TPB + t, 1)
                    ins = dve.tensor_scalar(k.rows0[:, one, 0:C].rearrange("p a c -> p (a c)"),
                                            k.x[:, one, :].rearrange("p a c -> p (a c)"),
                                            k.mean[:, one], k.rstd[:, one],
                                            ALU.subtract, ALU.mult)
                ins.then_inc(s["norm_ready"].h, 1)
                ids = k.token_id1[:, tiles] if K == 1 else None
                for c in range(K):
                    src = k.token_id1[:, tiles] if K == 1 else k.token_id[:, tiles, c:c + 1].rearrange("p t a -> p (t a)")
                    ch.note(dve.tensor_copy(rows[c][:].bitcast(I32)[:, tiles, C:C + 1].rearrange("p t a -> p (t a)"), src))

                def over_e(v):
                    return v.unsqueeze(2).to_broadcast([P, TPB, E])

                def over_t(v):
                    return v.unsqueeze(1).to_broadcast([P, TPB, E])

                def choose(logits, c):
                    best, tie = top[:, 2 * c, :], top[:, 2 * c + 1, :]
                    ch.link(dve.tensor_reduce(best, logits, AX.X, ALU.max))
                    ch.link(dve.tensor_tensor(oh[c][:], logits, over_e(best), ALU.is_equal))
                    ch.link(dve.tensor_tensor(oh[c][:], oh[c][:], over_t(k.rank[:, 0:E]), ALU.mult))
                    ch.link(dve.tensor_reduce(tie, oh[c][:], AX.X, ALU.max))
                    ch.link(dve.tensor_tensor(oh[c][:], oh[c][:], over_e(tie), ALU.is_equal))

                wait(dve, "logits_ready", b + 1)
                pl = k.ps[:, 6, 0:TPB * E].rearrange("p (t e) -> p t e", e=E)
                ch.link(dve.tensor_tensor(lg[:], pl, over_t(gb[:]), ALU.add))
                choose(lg[:], 0)
                if K == 2:
                    ch.link(dve.scalar_tensor_tensor(out=lg2[:], in0=oh[0][:], scalar=-1e30, in1=lg[:],
                                                     op0=ALU.mult, op1=ALU.add))
                    choose(lg2[:], 1)
                    dve.tensor_tensor(msk[:, 0:TPB, :], oh[0][:], oh[1][:], ALU.add).then_inc(s["chosen"].h, 1)
                else:
                    dve.tensor_copy(msk[:, 0:TPB, :], oh[0][:]).then_inc(s["chosen"].h, 1)
                ins = dve.tensor_tensor(ex[:, :, 0:E], lg[:], over_e(top[:, 0, :]), ALU.subtract)
                if K == 2:
                    ins.then_inc(s["shifted"].h, 1)
                    ins = dve.tensor_tensor(ex[:, :, E:E + 1], top[:, 2, :].unsqueeze(2), top[:, 0, :].unsqueeze(2), ALU.subtract)
                ins.then_inc(s["shifted"].h, 1)
                wait(dve, "ranked", b + 1)
                pr = k.ps[:, 7, 0:(TPB + 1) * E].rearrange("p (t e) -> p t e", e=E)
                ch.link(dve.tensor_tensor(pos[:], pr[:, 0:TPB, :], over_t(k.counts[:, 0:E]), ALU.add))
                ch.note(dve.tensor_tensor(k.counts[:, 0:E], k.counts[:, 0:E], pr[:, TPB, :], ALU.add))
                ch.link(dve.tensor_tensor(posr[:], pos[:], over_t(k.region[:, 0:E]), ALU.add))
                for c in range(K):
                    ch.link(dve.tensor_tensor(tmp[:], posr[:], oh[c][:], ALU.mult))
                    ch.link(dve.tensor_reduce(slotf[:, c, :], tmp[:], AX.X, ALU.add))
                    if past(b, 2):
                        wait(dve, "rows_sent", 16 * TPB * K * (b - 1))
                    ch.link(dve.tensor_copy(slot[:, u, c, :], slotf[:, c, :]))
                wait(dve, "exp_ready", b + 1)
                w0 = wsum[:, 1, :]
                if f["over_chosen"]:
                    ch.link(dve.tensor_scalar(wsum[:, 0, :], exo[:, :, E:E + 1].rearrange("p t a -> p (t a)"), 1.0, None, ALU.add))
                else:
                    ch.link(dve.tensor_reduce(wsum[:, 0, :], exo[:, :, 0:E], AX.X, ALU.add))
                ch.link(dve.reciprocal(w0, wsum[:, 0, :]))
                if f["capacity"]:
                    ch.link(dve.tensor_tensor(tmp[:], pos[:], oh[0][:], ALU.mult))
                    ch.link(dve.tensor_reduce(wsum[:, 2, :], tmp[:], AX.X, ALU.add))
                    ch.link(dve.tensor_scalar(wsum[:, 2, :], wsum[:, 2, :], float(f["capacity"]), None, ALU.is_le))
                    ch.link(dve.tensor_tensor(w0, w0, wsum[:, 2, :], ALU.mult))
                col = slice(C + 1, C + 2)
                dve.tensor_copy(k.rows0[:, tiles, col].rearrange("p t a -> p (t a)"), w0).then_inc(s["slots_ready"].h, 1)
                if K == 2:
                    dve.tensor_tensor(k.rows1[:, tiles, col].rearrange("p t a -> p (t a)"), w0,
                                      exo[:, :, E:E + 1].rearrange("p t a -> p (t a)"),
                                      ALU.mult).then_inc(s["slots_ready"].h, 1)
                assert ch.n == route_ops, ch.n
            spelled_out(B, 2, second)

            ch = Chain(dve, s["plan_step"], s["plan_step"].base)
            wait(dve, "vector_step", stats_done + B * route_ops)
            cnt, reg = k.counts[:, 0:E], k.region[:, 0:E]
            ch.link(dve.tensor_tensor(padf[:], cnt, reg, ALU.add))
            ch.link(dve.tensor_scalar(padf[:], padf[:], k.partition[:, 0:1], 1.0, ALU.add, ALU.add))
            dve.tensor_copy(padi[:], padf[:]).then_inc(s["pads_ready"].h, 1)
            ch.link(dve.tensor_scalar(ntf[:, 0, :], cnt, float(P - 1), None, ALU.add))
            ch.link(dve.tensor_copy(nti[:], ntf[:, 0, :]))
            ch.link(dve.tensor_scalar(nti[:], nti[:], 7, None, ALU.logical_shift_right))
            ch.link(dve.tensor_copy(ntf[:, 0, :], nti[:]))
            ch.link(dve.memset(ntf[:, 1, :], 1.0))
            ch.link(dve.tensor_tensor_scan(ntf[:, 2, :], ntf[:, 1, :], ntf[:, 0, :], 0.0, ALU.mult, ALU.add))
            ch.link(dve.tensor_scalar(ntf[:, 1, :], ntf[:, 0, :], float(-P), float(REGION), ALU.mult, ALU.add))
            ch.note(dve.memset(acc[0:1, 0, 0:T], 0.0))
            ch.link(dve.tensor_scalar(acc[0:1, 1, 0:T], k.tile_no[0:1, 0:T], float(P), None, ALU.mult))
            for e in range(E):
                end, skip = ntf[0:1, 2, e:e + 1], ntf[0:1, 1, e:e + 1]
                ch.link(dve.tensor_scalar(acc[0:1, 2, 0:T], k.tile_no[0:1, 0:T], end, None, ALU.is_ge))
                ch.note(dve.tensor_tensor(acc[0:1, 0, 0:T], acc[0:1, 0, 0:T], acc[0:1, 2, 0:T], ALU.add))
                ch.link(dve.scalar_tensor_tensor(out=acc[0:1, 1, 0:T], in0=acc[0:1, 2, 0:T], scalar=skip,
                                                 in1=acc[0:1, 1, 0:T], op0=ALU.mult, op1=ALU.add))
            ch.link(dve.tensor_scalar(acc[0:1, 0, 0:T], acc[0:1, 0, 0:T], float(E - 1), None, ALU.min))
            ch.link(dve.tensor_scalar(acc[0:1, 1, 0:T], acc[0:1, 1, 0:T], float(E * REGION), None, ALU.min))
            ch.note(dve.tensor_copy(k.tile_expert[0:1, 0:T], acc[0:1, 0, 0:T]))
            ch.link(dve.tensor_copy(k.tile_row[0:1, 0:T], acc[0:1, 1, 0:T]))
            k.plan_ops = ch.n

        @block.tensor
        def _(pe):
            def back(b, u):
                if past(b, 2):
                    wait(pe, "vector_step", (b - 2) * per1 + 1)
                for t in range(TPB):
                    bank, at = 2 * u + t // 4, (t % 4) * P
                    ins = pe.transpose(k.ps[:, bank, at:at + P], k.mixed[:, bass.ds(b * IMG + t * P, P)], k.ident[:])
                ins.then_inc(s["mix_turned"].h, 1)
            spelled_out(B, 2, back)
            wait(pe, "gate_loaded", 32)
            wait(pe, "rstd_ready", 3)

            def route(b, u):
                wait(pe, "norm_ready", b + 1)
                for t in range(TPB):
                    bank, at = 2 * u + t // 4, (t % 4) * P
                    ins = pe.transpose(k.ps[:, bank, at:at + P],
                                       k.rows0[:, bass.ds(b * TPB + t, 1), 0:C].rearrange("p a c -> p (a c)"), k.ident[:])
                ins.then_inc(s["turned"].h, 1)
                wait(pe, "turned_copied", b + 1)
                if past(b, 1):
                    wait(pe, "chosen", b)
                for t in range(TPB):
                    ins = pe.matmul(k.ps[:, 6, t * E:(t + 1) * E], turned[:, u, t * P:(t + 1) * P], gw[:],
                                    start=True, stop=True)
                ins.then_inc(s["logits_ready"].h, 1)
                wait(pe, "chosen", b + 1)
                if past(b, 1):
                    wait(pe, "slots_ready", K * b)
                pe.matmul(k.ps[:, 7, 0:(TPB + 1) * E], k.tri[:], msk[:].rearrange("p t e -> p (t e)"), start=True, stop=True)
                for t in range(TPB):
                    later = k.ps[:, 7, (t + 1) * E:(TPB + 1) * E].rearrange("p (t e) -> p t e", e=E)
                    ins = pe.matmul(later, k.ones[:], msk[:, t:t + 1, :].to_broadcast([P, TPB - t, E]),
                                    start=False, stop=True, skip_group_check=True)
                ins.then_inc(s["ranked"].h, 1)
            spelled_out(B, 2, route)

        @block.scalar
        def _(act):
            wait(act, "vector_step", stats_done)
            act.activation(k.rstd[:], k.var4[:], ACT.Sqrt, bias=k.eps5, scale=0.25).then_inc(s["root_ready"].h, 1)

            def step(b, u):
                tiles = bass.ds(b * TPB, TPB)
                wait(act, "turned", b + 1)
                act.activation(turned[:, u, :], k.ps[:, 2 * u:2 * u + 2, :].rearrange("p a n -> p (a n)"),
                               ACT.Copy).then_inc(s["turned_copied"].h, 1)
                if K == 2:
                    act.activation(k.rows1[:, tiles, 0:C], k.rows0[:, tiles, 0:C], ACT.Copy).then_inc(s["rows_copied"].h, 1)
                wait(act, "shifted", K * (b + 1))
                act.activation(exo[:], ex[:], ACT.Exp).then_inc(s["exp_ready"].h, 1)
            spelled_out(B, 2, step)

        @block.gpsimd
        def _(pool):
            def send(b, u):
                wait(pool, "slots_ready", K * (b + 1))
                if K == 2:
                    wait(pool, "rows_copied", b + 1)
                for t in range(TPB):
                    for c in range(K):
                        pool.indirect_dma_start(
                            out=k.dispatched, out_offset=bass.IndirectOffsetOnAxis(ap=slot[:, u, c, t:t + 1], axis=0),
                            in_=rows[c][:, bass.ds(b * TPB + t, 1), :].rearrange("p a c -> p (a c)"),
                            in_offset=None).then_inc(s["rows_sent"].h, 16)
                wait(pool, "rows_sent", 16 * TPB * K * (b + 1))
            spelled_out(B, 2, send)
            wait(pool, "pads_ready", 1)
            for e in range(E):
                pool.indirect_dma_start(
                    out=k.dispatched, out_offset=bass.IndirectOffsetOnAxis(ap=padi[:, e:e + 1], axis=0),
                    in_=k.pad_rows[:], in_offset=None).then_inc(s["rows_sent"].h, 16)
            wait(pool, "rows_sent", 16 * (NT * K + E))

    k.advance(vector_step=stats_done + B * route_ops, root_ready=1, rstd_ready=3, norm_ready=B,
              turned=B, turned_copied=B, mix_turned=B, gate_loaded=32, logits_ready=B, shifted=K * B, exp_ready=B,
              chosen=B, ranked=B, slots_ready=K * B, rows_sent=16 * (NT * K + E), rows_copied=B if K == 2 else 0,
              pads_ready=1, plan_step=k.plan_ops)


def expert_weight_loads(k, layer):
    f = FFN[layer]
    E, F = f["E"], f["F"]
    _, _, w1, b1, w2, b2 = ffn_inputs(k, layer)
    first, second = expert_weight_views(k, layer)
    if not f["gated"]:
        return [(first, w1.rearrange("e c f -> c e f")),
                (second, w2.rearrange("e (j h) c -> h e j c", h=P))]
    w3 = w2
    return [(first[:, :, 0:F], w1.rearrange("e c f -> c e f")),
            (first[:, :, F:2 * F], b1.rearrange("e c f -> c e f")),
            (second, w3.rearrange("e (j h) c -> h e j c", h=P))]


def expert_weight_views(k, layer):
    f = FFN[layer]
    E, F = f["E"], f["F"]
    wide = 2 * F if f["gated"] else F
    first = k.wts[:, 0:E * wide].rearrange("p (e f) -> p e f", e=E)
    second = k.wts[:, E * wide:E * wide + E * F].rearrange("p (e j c) -> p e j c", e=E, j=F // P)
    return first, second


RING = 8


def experts(k, layer):
    nc, f = k.nc, FFN[layer]
    E, K, F = f["E"], f["K"], f["F"]
    T = N * K // P + E
    J = F // P
    gated = f["gated"]
    wide = 2 * F if gated else F
    _, _, w1, b1, w2, b2 = ffn_inputs(k, layer)
    first, second = expert_weight_views(k, layer)
    names = ("x_turned", "x_copied", "w_copied", "hidden_ready", "act_ready", "gated_ready",
             "y_ready", "y_scaled", "bias_split", "bias_turned", "bias_kept", "guard_step", "bias_loaded")
    s = {n: k.sem(n) for n in names}
    s_row = [k.sem(f"slot_rows{r}") for r in range(RING)]
    s_out = [k.sem(f"results_sent{r}") for r in range(RING)]
    loads = 16 * len(expert_weight_loads(k, layer))
    PSX, PSH, PSY = 0, 2, 4
    HB = 4

    def wait(eng, name, n):
        eng.wait_ge(s[name].h, s[name].base + n)

    with ExitStack() as ctx, nc.Block() as block:
        def sb(name, shape, dt=F32):
            return ctx.enter_context(nc.sbuf_tensor(f"{name}_{layer}", shape, dt))

        sizes = (RING * ROW, RING * C, 2 * C, 2 * wide, HB * F, HB * F)
        starts = [sum(sizes[:j]) for j in range(len(sizes))]

        def room(j, n):
            return k.ch[:, starts[j]:starts[j] + sizes[j]].rearrange("p (a n) -> p a n", n=n)

        rt, ys, xt, wc, hs = room(0, ROW), room(1, C), room(2, C), room(3, wide), room(4, F)
        gs = room(5, F) if gated else hs
        if f["guard"]:
            gm = sb("guard", [P, 3, C])
            carry = sb("guard_carry", [P, 2])
        if b2 is not None:
            brows = sb("bias_rows", [E * J, P])
            bcol = sb("bias_columns", [P, E * J])
            n2 = E * C
            bp2 = sb("bias_parts", [3, E, C], BF16)
            brow = k.flat(k.rows1)[0:1, 0:n2]
            bpart = k.flat(k.rows0).bitcast(BF16)[0:1, 0:3 * n2].rearrange("p (a n) -> p a n", a=3)

        @block.sync
        def _(sp):
            if b2 is not None:
                sp.dma_start(brows[:], b1.rearrange("e (j h) -> (e j) h", h=P)).then_inc(s["bias_loaded"].h, 16)
                sp.dma_start(brow, b2.rearrange("(a e) f -> a (e f)", a=1)).then_inc(s["bias_loaded"].h, 16)
                wait(sp, "bias_split", 5)
                for part in range(3):
                    sp.dma_start(bp2[part:part + 1, :, :].rearrange("p e c -> p (e c)"),
                                 bpart[0:1, part, :]).then_inc(s["bias_loaded"].h, 16)

            def load(t, u):
                row = sp.value_load(k.tile_row[0:1, bass.ds(t, 1)], min_val=0, max_val=E * REGION)
                if past(t, RING):
                    sp.wait_ge(s_out[u].h, s_out[u].base + (t - u) * (16 // RING))
                sp.dma_start(rt[:, u, :], k.dispatched[bass.ds(row, P), :]).then_inc(s_row[u].h, 16)
            steps(sp, T, RING, load)

        @block.tensor
        def _(pe):
            if b2 is not None:
                wait(pe, "bias_loaded", 16 * 5)
                pe.transpose(k.ps[:, PSY, 0:E * J], brows[:], k.ident[0:E * J, 0:E * J]).then_inc(s["bias_turned"].h, 1)
                wait(pe, "bias_kept", 1)
            pe.wait_ge(k.sem("weights_loaded").h, k.sem("weights_loaded").base + loads)

            def turn_rows(t, u):
                pe.wait_ge(s_row[u].h, s_row[u].base + (t - u) * (16 // RING) + 16)
                pe.transpose(k.ps[:, PSX + u % 2, 0:P], rt[:, u, 0:C], k.ident[:]).then_inc(s["x_turned"].h, 1)

            def hidden(t, u):
                wait(pe, "x_copied", t + 1)
                wait(pe, "w_copied", t + 1)
                if past(t, 2):
                    wait(pe, "gated_ready" if gated else "act_ready", t - 1)
                for j in range(wide // P):
                    ins = pe.matmul(k.ps[:, PSH + u % 2, j * P:(j + 1) * P], wc[:, u % 2, j * P:(j + 1) * P],
                                    xt[:, u % 2, :], start=True, stop=True)
                ins.then_inc(s["hidden_ready"].h, 1)

            def result(t, u):
                e = pe.value_load(k.tile_expert[0:1, bass.ds(t, 1)], min_val=0, max_val=E - 1)
                wait(pe, "gated_ready" if gated else "act_ready", t + 1)
                if past(t, 4):
                    wait(pe, "y_scaled", t - 3)
                bank = k.ps[:, PSY + u % 4, 0:C]
                if b2 is not None:
                    pe.matmul(bank, k.ones[0:3, :], bp2[:, bass.ds(e, 1), :].rearrange("p a f -> p (a f)"),
                              start=True, stop=False)
                for j in range(J):
                    ins = pe.matmul(bank, gs[:, u % HB, j * P:(j + 1) * P],
                                    second[:, bass.ds(e, 1), j, :].rearrange("p a c -> p (a c)"),
                                    start=(b2 is None and j == 0), stop=(j == J - 1))
                ins.then_inc(s["y_ready"].h, 1)

            turn_rows(0, 0)

            def step(t, u, last=False):
                if not last:
                    turn_rows(t + 1, (u + 1) % RING)
                hidden(t, u)
                if past(t, 2):
                    result(t - 2, (u - 2) % RING)

            for u in range(RING):
                step(u, u)
            with pe.Fori(1, T // RING - 1) as g:
                for u in range(RING):
                    step(g * RING + u, u)
            for u in range(RING):
                step(T - RING + u, u, last=(u == RING - 1))
            result(T - 2, (T - 2) % RING)
            result(T - 1, (T - 1) % RING)

        @block.scalar
        def _(act):
            if b2 is not None:
                wait(act, "bias_turned", 1)
                act.activation(bcol[:], k.ps[:, PSY, 0:E * J], ACT.Copy).then_inc(s["bias_kept"].h, 1)
                wait(act, "bias_kept", 1)
            act.wait_ge(k.sem("weights_loaded").h, k.sem("weights_loaded").base + loads)

            def copy_weights(t, u):
                e = act.value_load(k.tile_expert[0:1, bass.ds(t, 1)], min_val=0, max_val=E - 1)
                if past(t, 2):
                    wait(act, "hidden_ready", t - 1)
                act.activation(wc[:, u % 2, :], first[:, bass.ds(e, 1), :].rearrange("p a f -> p (a f)"),
                               ACT.Copy).then_inc(s["w_copied"].h, 1)

            def activate(t, u):
                if not gated:
                    e = act.value_load(k.tile_expert[0:1, bass.ds(t, 1)], min_val=0, max_val=E - 1)
                wait(act, "hidden_ready", t + 1)
                if gated:
                    if past(t, HB):
                        wait(act, "gated_ready", t - HB + 1)
                    act.activation(hs[:, u % HB, :], k.ps[:, PSH + u % 2, 0:F], f["act"]).then_inc(s["act_ready"].h, 1)
                    return
                if past(t, HB):
                    wait(act, "y_ready", t - HB + 1)
                for j in range(J):
                    cols = slice(j * P, (j + 1) * P)
                    ins = act.activation(hs[:, u % HB, cols], k.ps[:, PSH + u % 2, cols], f["act"],
                                         bias=bcol[:, bass.ds(e * J + j, 1)])
                ins.then_inc(s["act_ready"].h, 1)

            def step(t, u, last=False):
                if not last:
                    copy_weights(t + 1, (u + 1) % RING)
                activate(t, u)

            copy_weights(0, 0)
            for u in range(RING):
                step(u, u)
            with act.Fori(1, T // RING - 1) as g:
                for u in range(RING):
                    step(g * RING + u, u)
            for u in range(RING):
                step(T - RING + u, u, last=(u == RING - 1))

        @block.vector
        def _(dve):
            if b2 is not None:
                wait(dve, "bias_loaded", 32)
                ch = Chain(dve, s["bias_split"], s["bias_split"].base)
                for part in range(3):
                    ch.link(dve.tensor_copy(bpart[0:1, part, :], brow))
                    if part < 2:
                        ch.link(dve.tensor_tensor(brow, brow, bpart[0:1, part, :], ALU.subtract))

            def copy_rows(t, u):
                wait(dve, "x_turned", t + 1)
                if past(t, 2):
                    wait(dve, "hidden_ready", t - 1)
                dve.tensor_copy(xt[:, u % 2, :], k.ps[:, PSX + u % 2, 0:P]).then_inc(s["x_copied"].h, 1)

            def gate(t, u):
                wait(dve, "act_ready", t + 1)
                if past(t, HB):
                    wait(dve, "y_ready", t - HB + 1)
                dve.tensor_tensor(gs[:, u % HB, :], hs[:, u % HB, :], k.ps[:, PSH + u % 2, F:2 * F],
                                  ALU.mult).then_inc(s["gated_ready"].h, 1)

            def scale(t, u):
                wait(dve, "y_ready", t + 1)
                if past(t, RING):
                    dve.wait_ge(s_out[u].h, s_out[u].base + (t - u) * (16 // RING))
                y = ys[:, u, :]
                weight = rt[:, u, C + 1:C + 2]
                if not f["guard"]:
                    dve.tensor_scalar(y, k.ps[:, PSY + u % 4, 0:C], weight, None, ALU.mult).then_inc(s["y_scaled"].h, 1)
                    return
                ch = Chain(dve, s["guard_step"], s["guard_step"].base + t * 7)
                ch.link(dve.tensor_scalar(y, k.ps[:, PSY + u % 4, 0:C], weight, None, ALU.mult))
                ch.note(dve.tensor_scalar(gm[:, 0, :], y, 1e4, -1e4, ALU.min, ALU.max))
                ch.note(dve.scalar_tensor_tensor(out=gm[:, 1, :], in0=y, scalar=0.0, in1=k.zeros[:],
                                                 op0=ALU.mult, op1=ALU.not_equal))
                ch.note(dve.tensor_tensor(gm[:, 2, :], y, y, ALU.not_equal))
                ch.settle()
                ch.note(dve.tensor_copy(carry[:, 0:1], k.zeros[:, 0:1]))
                ch.link(dve.copy_predicated(y, gm[:, 1, :].bitcast(I32), gm[:, 0, :]))
                ch.note(dve.tensor_copy(carry[:, 1:2], k.zeros[:, 0:1]))
                dve.copy_predicated(y, gm[:, 2, :].bitcast(I32), k.zeros[:]).then_inc(s["y_scaled"].h, 1)

            copy_rows(0, 0)

            def step(t, u, last=False):
                if not last:
                    copy_rows(t + 1, (u + 1) % RING)
                if gated:
                    gate(t, u)
                if past(t, 2):
                    scale(t - 2, (u - 2) % RING)

            for u in range(RING):
                step(u, u)
            with dve.Fori(1, T // RING - 1) as g:
                for u in range(RING):
                    step(g * RING + u, u)
            for u in range(RING):
                step(T - RING + u, u, last=(u == RING - 1))
            scale(T - 2, (T - 2) % RING)
            scale(T - 1, (T - 1) % RING)

        @block.gpsimd
        def _(pool):
            last = pool.to_reg(N * K - 1)

            def send(t, u):
                wait(pool, "y_scaled", t + 1)
                pool.indirect_dma_start(
                    out=k.returned[0:N * K, :],
                    out_offset=bass.IndirectOffsetOnAxis(ap=rt[:, u, C:C + 1].bitcast(I32), axis=0),
                    in_=ys[:, u, :], in_offset=None, bounds_check=last, oob_is_err=False).then_inc(s_out[u].h, 16)
            spelled_out(T, RING, send)
            for u in range(RING):
                pool.wait_ge(s_out[u].h, s_out[u].base + 16 * T // RING)

    k.advance(x_turned=T, x_copied=T, w_copied=T, hidden_ready=T, act_ready=T,
              y_ready=T, y_scaled=T, weights_loaded=loads)
    if gated:
        k.advance(gated_ready=T)
    if f["guard"]:
        k.advance(guard_step=7 * T)
    if b2 is not None:
        k.advance(bias_split=5, bias_loaded=16 * 5, bias_turned=1, bias_kept=1)
    for r in range(RING):
        s_row[r].base += 16 * T // RING
        s_out[r].base += 16 * T // RING


def load_columns(sp, sem, dst, vectors):
    for j, v in enumerate(vectors):
        sp.dma_start(dst[:, j:j + 1], v.rearrange("(c a) -> c a", a=1)).then_inc(sem.h, 16)


def mixer_fractal(k):
    nc, i = k.nc, k.ins
    RED = i["L0_conv_w1"].shape[1]
    names = ("mix_loaded", "mix_v", "mix_range", "mix_allmax", "mix_pad", "mix_boxes", "mix_logs", "mix_pool",
             "mix_slope", "mix_squares", "mix_energy", "mix_sq1", "mix_sq2", "mix_prep", "mix_mm", "mix_excite",
             "mix_root", "mix_sig", "mix_sim", "mix_out", "mix_pool2", "mix_used")
    s = {n: k.sem(n) for n in names}

    def wait(eng, name, n):
        eng.wait_ge(s[name].h, s[name].base + n)

    SIDE = 47
    slope_scale = 0.1 / LN2
    norm_scale = slope_scale * float(np.sqrt(5.0) * LN2)
    xch = k.ch[:, 0:N].rearrange("p (b n) -> p b n", b=B)
    slope = k.flat(k.rows0)[:, 0:N].rearrange("p (b n) -> p b n", b=B)
    energy = k.mixed.rearrange("p (b n) -> p b n", b=B)
    with ExitStack() as ctx, nc.Block() as block:
        def sb(name, shape, dt=F32):
            return ctx.enter_context(nc.sbuf_tensor(name, shape, dt))

        w = k.wts[:]
        pad = w[:, 0:SIDE * SIDE].rearrange("p (h w) -> p h w", w=SIDE)
        tmp = w[:, 2210:2210 + 47 * 46]
        s2 = w[:, 4372:4372 + 46 * 46].rearrange("p (h w) -> p h w", w=46)
        s4 = w[:, 6488:6488 + 44 * 44].rearrange("p (h w) -> p h w", w=44)
        s8 = w[:, 8424:8424 + 40 * 40].rearrange("p (h w) -> p h w", w=40)
        logs = sb("logs", [P, 4, IMG])
        s16 = logs[:, 3, :].rearrange("p (h w) -> p h w", w=WW)
        con = [w[:, 10024:11048], w[:, 11048:12072], k.ch[:, N:N + IMG]]
        vec = sb("mix_vectors", [P, 8])
        w1 = sb("squeeze_w", [P, RED])
        w2 = sb("excite_w", [RED, P])
        b1 = sb("squeeze_b", [RED, 1])
        rng = sb("range", [P, 2, B])
        rngall = sb("range_all", [P, 2, B])
        inv = sb("range_inverse", [P, B])
        lowest = sb("lowest", [P, B])
        sums = sb("slope_sums", [P, B])
        sq = sb("squeezed", [P, B])
        hid = sb("squeeze_hidden", [RED, B])
        exc = sb("excite", [P, B])
        gain = sb("gain", [P, B])
        bn = sb("bn_scale", [P, 4])

        @block.sync
        def _(sp):
            load_columns(sp, s["mix_loaded"], vec, [i["L0_conv_b2"], i["L0_conv_gamma"], i["L0_conv_beta"],
                                                    i["L0_conv_moving_mean"], i["L0_conv_moving_var"]])
            sp.dma_start(w1[:], i["L0_conv_w1"]).then_inc(s["mix_loaded"].h, 16)
            sp.dma_start(w2[:], i["L0_conv_w2"]).then_inc(s["mix_loaded"].h, 16)
            sp.dma_start(b1[:], i["L0_conv_b1"].rearrange("(c a) -> c a", a=1)).then_inc(s["mix_loaded"].h, 16)
            wait(sp, "mix_loaded", 16 * 8)

        BOX = 10

        @block.vector
        def _(dve):
            ch = Chain(dve, s["mix_v"], s["mix_v"].base)
            ch.note(dve.memset(pad, 0.0))
            ch.note(dve.tensor_reduce(rng[:, 0, :], xch, AX.X, ALU.max))
            ch.link(dve.tensor_reduce(rng[:, 1, :], xch, AX.X, ALU.min))
            dve.tensor_scalar(rng[:, 1, :], rng[:, 1, :], -1.0, None, ALU.mult).then_inc(s["mix_range"].h, 1)
            wait(dve, "mix_allmax", 1)
            ch.link(dve.tensor_tensor(inv[:], rngall[:, 0, :], rngall[:, 1, :], ALU.add))
            ch.link(dve.tensor_scalar(inv[:], inv[:], 1e-7, None, ALU.add))
            ch.link(dve.reciprocal(inv[:], inv[:]))
            ch.link(dve.tensor_scalar(lowest[:], rngall[:, 1, :], -1.0, None, ALU.mult))
            pre = k.fractal_pre = ch.n

            def boxes(b, u):
                ch = Chain(dve, s["mix_v"], s["mix_v"].base + pre + b * BOX)
                one = bass.ds(b, 1)
                src = xch[:, one, :].rearrange("p a (h w) -> p (a h) w", w=WW)
                ch.link(dve.tensor_scalar(pad[:, 7:39, 7:39], src, lowest[:, one], inv[:, one], ALU.subtract, ALU.mult))
                if past(b, 1):
                    wait(dve, "mix_logs", b)

                def double(out, src, rows, cols, shift):
                    t = tmp[:, 0:rows * (cols - shift)].rearrange("p (h w) -> p h w", h=rows)
                    ch.link(dve.tensor_tensor(t, src[:, :, 0:cols - shift], src[:, :, shift:cols], ALU.add))
                    ins = dve.tensor_tensor(out, t[:, 0:rows - shift, :], t[:, shift:rows, :], ALU.add)
                    ch.link(ins)

                double(s2, pad, 47, 47, 1)
                double(s4, s2, 46, 46, 2)
                double(s8, s4, 44, 44, 4)
                if past(b, 1):
                    wait(dve, "mix_pool", 5 * b)
                double(s16, s8, 40, 40, 8)
                wait(dve, "mix_pool", b * 5 + 2)
                ch.link(dve.scalar_tensor_tensor(out=slope[:, one, :].rearrange("p a n -> p (a n)"), in0=con[0],
                                                 scalar=3.0, in1=con[1], op0=ALU.mult, op1=ALU.add,
                                                 accum_out=sums[:, one]))
            spelled_out(B, 1, boxes)

            ch = Chain(dve, s["mix_prep"], s["mix_prep"].base)
            wait(dve, "mix_v", pre + B * BOX)
            wait(dve, "mix_loaded", 16 * 8)
            ch.note(dve.tensor_scalar(sq[:], sums[:], slope_scale / IMG, None, ALU.mult))
            dve.wait_ge(s["mix_prep"].h, s["mix_prep"].base + 1)
            wait(dve, "mix_sq1", 1)
            ch.link(dve.reciprocal(bn[:, 1:2], bn[:, 0:1]))
            ch.link(dve.tensor_tensor(bn[:, 1:2], bn[:, 1:2], vec[:, 1:2], ALU.mult))
            ch.link(dve.tensor_tensor(bn[:, 2:3], bn[:, 1:2], vec[:, 3:4], ALU.mult))
            ch.link(dve.tensor_tensor(bn[:, 2:3], vec[:, 2:3], bn[:, 2:3], ALU.subtract))
            ch.link(dve.tensor_scalar(bn[:, 3:4], bn[:, 1:2], slope_scale, None, ALU.mult))
            wait(dve, "mix_excite", 2)
            ch.link(dve.tensor_tensor(gain[:], inv[:], exc[:], ALU.mult))

            def blend(b, u):
                one = bass.ds(b, 1)
                at = energy[:, one, :].rearrange("p a n -> p (a n)")
                wait(dve, "mix_root", 2 * (b + 1))
                c2 = Chain(dve, s["mix_sim"], s["mix_sim"].base + b * 6)
                c2.link(dve.tensor_scalar(logs[:, 0, :], at, 1e-7, None, ALU.add))
                c2.link(dve.reciprocal(logs[:, 0, :], logs[:, 0, :]))
                c2.note(dve.tensor_tensor(logs[:, 0, :], con[2], logs[:, 0, :], ALU.mult))
                c2.link(dve.tensor_scalar(logs[:, 1, :], xch[:, one, :].rearrange("p a n -> p (a n)"), lowest[:, one],
                                          gain[:, one], ALU.subtract, ALU.mult))
                wait(dve, "mix_sig", b + 1)
                c2.link(dve.tensor_tensor(logs[:, 2, :], logs[:, 1, :], con[0], ALU.subtract))
                c2.link(dve.tensor_tensor(logs[:, 3, :], logs[:, 0, :], logs[:, 2, :], ALU.mult))
                dve.tensor_tensor(at, logs[:, 1, :], logs[:, 3, :], ALU.subtract).then_inc(s["mix_used"].h, 1)
            spelled_out(B, 1, blend)

        @block.gpsimd
        def _(pool):
            wait(pool, "mix_range", 1)
            pool.partition_all_reduce(rngall[:].rearrange("p a b -> p (a b)"), rng[:].rearrange("p a b -> p (a b)"), P,
                                      bass.bass_isa.ReduceOp.max).then_inc(s["mix_allmax"].h, 1)

            def contrasts(b, u):
                ch = Chain(pool, s["mix_pool"], s["mix_pool"].base + b * 5)
                wait(pool, "mix_logs", b + 1)
                if past(b, 1):
                    wait(pool, "mix_squares", 4 * b)
                L = [logs[:, j, :] for j in range(4)]
                ch.note(pool.tensor_tensor(con[0], L[3], L[0], ALU.subtract))
                ch.note(pool.tensor_tensor(con[1], L[2], L[1], ALU.subtract))
                ch.note(pool.tensor_tensor(L[3], L[3], L[0], ALU.add))
                ch.note(pool.tensor_tensor(L[2], L[2], L[1], ALU.add))
                ch.settle()
                ch.note(pool.tensor_tensor(con[2], L[3], L[2], ALU.subtract))
                at = energy[:, bass.ds(b, 1), :].rearrange("p a n -> p (a n)")
                c2 = Chain(pool, s["mix_energy"], s["mix_energy"].base + b * 3)
                wait(pool, "mix_squares", 4 * (b + 1))
                c2.link(pool.tensor_tensor(con[0], con[0], con[1], ALU.add))
                c2.link(pool.tensor_tensor(con[0], con[0], con[2], ALU.add))
                c2.link(pool.tensor_tensor(at, con[0], at, ALU.mult))
            spelled_out(B, 1, contrasts)

        @block.scalar
        def _(act):
            def logs_of(b, u):
                one = bass.ds(b, 1)
                act.wait_ge(s["mix_v"].h, s["mix_v"].base + k.fractal_pre + b * BOX + BOX - 1)
                if past(b, 1):
                    wait(act, "mix_pool", 5 * b)
                for j, view in enumerate((s2[:, 7:39, 7:39], s4[:, 6:38, 6:38], s8[:, 4:36, 4:36], s16)):
                    ins = act.activation(logs[:, j, :].rearrange("p (h w) -> p h w", w=WW), view, ACT.Ln, bias=k.eps7)
                ins.then_inc(s["mix_logs"].h, 1)
                wait(act, "mix_pool", 5 * (b + 1))
                act.wait_ge(s["mix_v"].h, s["mix_v"].base + k.fractal_pre + (b + 1) * BOX)
                for j, scale in ((0, 0.5 ** 0.5), (1, 0.5 ** 0.5), (2, 0.5)):
                    act.activation(con[j], con[j], ACT.Square, scale=scale).then_inc(s["mix_squares"].h, 1)
                act.activation(energy[:, one, :].rearrange("p a n -> p (a n)"), slope[:, one, :].rearrange("p a n -> p (a n)"), ACT.Square,
                               scale=norm_scale).then_inc(s["mix_squares"].h, 1)
            spelled_out(B, 1, logs_of)
            wait(act, "mix_loaded", 16 * 8)
            act.activation(bn[:, 0:1], vec[:, 4:5], ACT.Sqrt, bias=k.eps3).then_inc(s["mix_sq1"].h, 1)
            wait(act, "mix_mm", 1)
            act.activation(hid[:], k.ps[0:RED, 0, 0:B], ACT.Relu, bias=b1[:]).then_inc(s["mix_excite"].h, 1)
            wait(act, "mix_mm", 2)
            act.activation(exc[:], k.ps[:, 1, 0:B], ACT.Sigmoid, bias=vec[:, 0:1]).then_inc(s["mix_excite"].h, 1)
            wait(act, "mix_energy", 3 * B)
            wait(act, "mix_prep", 6)

            def roots(b, u):
                one = bass.ds(b, 1)
                at = energy[:, one, :].rearrange("p a n -> p (a n)")
                sl = slope[:, one, :].rearrange("p a n -> p (a n)")
                if past(b, 1):
                    wait(act, "mix_used", b)
                act.activation(at, at, ACT.Sqrt).then_inc(s["mix_root"].h, 1)
                act.activation(con[2], sl, ACT.Square, scale=norm_scale).then_inc(s["mix_root"].h, 1)
                act.activation(con[0], sl, ACT.Sigmoid, scale=bn[:, 3:4], bias=bn[:, 2:3]).then_inc(s["mix_sig"].h, 1)
            spelled_out(B, 1, roots)

        @block.tensor
        def _(pe):
            wait(pe, "mix_loaded", 16 * 8)
            wait(pe, "mix_prep", 1)
            pe.matmul(k.ps[0:RED, 0, 0:B], w1[:], sq[:], start=True, stop=True).then_inc(s["mix_mm"].h, 1)
            wait(pe, "mix_excite", 1)
            pe.matmul(k.ps[:, 1, 0:B], w2[:], hid[:], start=True, stop=True).then_inc(s["mix_mm"].h, 1)


def mixer_involution(k):
    nc, i = k.nc, k.ins
    RED = i["L1_conv_W1"].shape[1]
    TAPS = 9
    GROUPS = i["L1_conv_W2"].shape[1] // TAPS
    GC = C // GROUPS
    PER = 2 * TAPS
    names = ("inv_loaded", "inv_prep", "inv_bias", "inv_ones", "inv_hidden", "inv_biased", "inv_kernel", "inv_product",
             "inv_sum", "inv_stored")
    s = {n: k.sem(n) for n in names}
    loads = 16 * (4 * 2 + 2)

    def wait(eng, name, n):
        eng.wait_ge(s[name].h, s[name].base + n)

    ch4 = k.ch[:].rearrange("p (b h w) -> p b h w", b=B, h=34)
    with ExitStack() as ctx, nc.Block() as block:
        def sb(name, shape, dt=F32):
            return ctx.enter_context(nc.sbuf_tensor(name, shape, dt))

        room = k.flat(k.rows0)[:, 0:6 * BANK].rearrange("p (a n) -> p a n", n=BANK)
        hid, prod = room[:, 0:2, :], room[:, 2:6, :]
        wide = k.wts[:, 0:3 * TAPS * C].rearrange("p (a n) -> p a n", a=3)
        w2x = wide[:, 0, :]
        gather = wide[:, 1, :].rearrange("p (t c) -> p t c", t=TAPS)
        bias_row = wide[0:1, 2, :]
        w1 = sb("reduce_w", [P, RED])
        w1r = sb("reduce_w_four_times", [P, 4, RED])
        w2 = sb("span_w", [P, GROUPS * TAPS])
        b2row = sb("span_b_row", [1, GROUPS * TAPS])
        b1 = sb("reduce_b", [P, 1])
        b2 = sb("span_b", [P, TAPS])

        @block.sync
        def _(sp):
            for g in range(4):
                rows = slice(RED * g, RED * (g + 1))
                sp.dma_start(w2[rows, :], i["L1_conv_W2"]).then_inc(s["inv_loaded"].h, 16)
                sp.dma_start(b1[rows, :], i["L1_conv_b1"].rearrange("(c a) -> c a", a=1)).then_inc(s["inv_loaded"].h, 16)
            sp.dma_start(w1[:], i["L1_conv_W1"]).then_inc(s["inv_loaded"].h, 16)
            sp.dma_start(b2row[:], i["L1_conv_b2"].rearrange("(a c) -> a c", a=1)).then_inc(s["inv_loaded"].h, 16)
            wait(sp, "inv_loaded", loads)

        def window(b, half, dy, dx):
            return ch4[:, bass.ds(b, 1), 16 * half + dy:16 * half + dy + 16, dx:dx + WW].rearrange("p a h w -> p (a h) w")

        @block.gpsimd
        def _(pool):
            pool.memset(gather, 1.0).then_inc(s["inv_ones"].h, 1)
            wait(pool, "inv_ones", 1)
            pool.affine_select(out=gather, in_=gather, compare_op=ALU.is_ge, fill=0.0, base=0,
                               pattern=[[P, TAPS], [-TAPS, C]], channel_multiplier=1).then_inc(s["inv_ones"].h, 1)
            wait(pool, "inv_ones", 2)
            pool.affine_select(out=gather, in_=gather, compare_op=ALU.is_ge, fill=0.0, base=TAPS - 1,
                               pattern=[[-P, TAPS], [TAPS, C]], channel_multiplier=-1).then_inc(s["inv_ones"].h, 1)

        @block.tensor
        def _(pe):
            wait(pe, "inv_prep", 3)
            for tap in range(TAPS):
                ins = pe.matmul(k.ps[:, 7, tap:tap + 1], bias_row[:, tap * P:(tap + 1) * P], k.ident[0:1, 0:1],
                                start=True, stop=True)
            ins.then_inc(s["inv_bias"].h, 1)
            wait(pe, "inv_ones", 3)
            wait(pe, "inv_prep", 4)

            def image(b, u):
                for half in range(2):
                    if past(b, 1):
                        wait(pe, "inv_biased", 2 * b + half - 1)
                    pe.matmul(k.ps[:, half, :].rearrange("p (h w) -> p h w", w=WW), w1r[:].rearrange("p a r -> p (a r)"),
                              window(b, half, 1, 1), start=True, stop=True).then_inc(s["inv_hidden"].h, 1)

                def kernel_entries(n):
                    half, tap = n // TAPS, n % TAPS
                    if tap == 0:
                        wait(pe, "inv_biased", 2 * b + half + 1)
                    if past(b, 1) or n >= 4:
                        wait(pe, "inv_product", b * PER + n - 3)
                    rows = slice(RED * (tap % 4), RED * (tap % 4 + 1))
                    pe.matmul(k.ps[:, 2 + (u * PER + n) % 4, :], w2x[rows, tap * P:(tap + 1) * P], hid[rows, half, :],
                              start=True, stop=True).then_inc(s["inv_kernel"].h, 1)

                def add_up(n):
                    half, tap = n // TAPS, n % TAPS
                    if tap == 0 and past(b, 1):
                        wait(pe, "inv_stored", 2 * b + half - 1)
                    wait(pe, "inv_product", b * PER + n + 1)
                    pe.matmul(k.ps[:, 6 + half, :], gather[:, tap, :], prod[:, (u * PER + n) % 4, :], start=(tap == 0),
                              stop=(tap == TAPS - 1)).then_inc(s["inv_sum"].h, 1)

                for n in range(PER):
                    kernel_entries(n)
                    if n >= 2:
                        add_up(n - 2)
                add_up(PER - 2)
                add_up(PER - 1)
            steps(pe, B, 2, image)

        @block.scalar
        def _(act):
            wait(act, "inv_loaded", loads)

            def image(b, u):
                for half in range(2):
                    wait(act, "inv_hidden", 2 * b + half + 1)
                    if past(b, 1):
                        wait(act, "inv_kernel", b * PER + (half - 1) * TAPS)
                    act.activation(hid[:, half, :], k.ps[:, half, :], ACT.Identity, bias=b1[:]).then_inc(s["inv_biased"].h, 1)
                for half in range(2):
                    wait(act, "inv_sum", b * PER + (half + 1) * TAPS)
                    act.activation(k.mixed[:, bass.ds(b * IMG + half * BANK, BANK)], k.ps[:, 6 + half, :],
                                   ACT.Copy).then_inc(s["inv_stored"].h, 1)
            steps(act, B, 1, image)

        @block.vector
        def _(dve):
            wait(dve, "inv_loaded", loads)
            dve.tensor_copy(w1r[:], w1[:].unsqueeze(1).to_broadcast([P, 4, RED])).then_inc(s["inv_prep"].h, 1)
            for p, dst, src in ((P, w2x, w2[:]), (1, bias_row, b2row[:])):
                for g in range(GROUPS):
                    ins = dve.tensor_copy(
                        dst[:, g * GC * TAPS:(g + 1) * GC * TAPS].rearrange("p (c t) -> p c t", t=TAPS),
                        src[:, g * TAPS:(g + 1) * TAPS].unsqueeze(1).to_broadcast([p, GC, TAPS]))
                ins.then_inc(s["inv_prep"].h, 1)
            wait(dve, "inv_bias", 1)
            dve.tensor_copy(b2[:], k.ps[:, 7, 0:TAPS]).then_inc(s["inv_prep"].h, 1)
            wait(dve, "inv_prep", 4)

            def image(b, u):
                for n in range(PER):
                    half, tap = n // TAPS, n % TAPS
                    wait(dve, "inv_kernel", b * PER + n + 1)
                    if past(b, 1) or n >= 4:
                        wait(dve, "inv_sum", b * PER + n - 3)
                    m = (u * PER + n) % 4
                    dve.scalar_tensor_tensor(
                        out=prod[:, m, :].rearrange("p (h w) -> p h w", w=WW),
                        in0=k.ps[:, 2 + m, :].rearrange("p (h w) -> p h w", w=WW), scalar=b2[:, tap:tap + 1],
                        in1=window(b, half, tap // 3, tap % 3), op0=ALU.add, op1=ALU.mult).then_inc(s["inv_product"].h, 1)
            steps(dve, B, 2, image)


def mixer_spline(k):
    nc, i = k.nc, k.ins
    KN = i["L2_conv_spline_weight"].shape[2]
    knots = [float(v) for v in np.linspace(-1.0, 1.0, KN, dtype=np.float32)]
    CHUNKS = N // BANK
    names = ("spl_loaded", "spl_v", "spl_scaled", "spl_wturned", "spl_wcopied", "spl_root", "spl_abs", "spl_basis",
             "spl_base", "spl_basis_used", "spl_silu", "spl_bn", "spl_out", "spl_range")
    s = {n: k.sem(n) for n in names}

    def wait(eng, name, n):
        eng.wait_ge(s[name].h, s[name].base + n)

    with ExitStack() as ctx, nc.Block() as block:
        def sb(name, shape, dt=F32):
            return ctx.enter_context(nc.sbuf_tensor(name, shape, dt))

        base_w = sb("base_w", [P, C])
        spw = sb("spline_w", [P, C, KN])
        scl = sb("spline_scaler", [P, C])
        spt = sb("spline_w_turned", [P, KN, C])
        vec = sb("spline_vectors", [P, 8])
        bn = sb("spline_bn", [P, 2, 4])
        rng = sb("channel_range", [P, 3])
        room = k.flat(k.rows0)[:, 0:12 * BANK].rearrange("p (a n) -> p a n", n=BANK)
        xu, dist, hat, silu, spo = (room[:, a:b, :] for a, b in ((0, 2), (2, 5), (5, 8), (8, 10), (10, 12)))
        kn = sb("minus_knots", [P, KN])

        @block.sync
        def _(sp):
            load_columns(sp, s["spl_loaded"], vec, [i[f"L2_conv_bn_{a}_{b}"] for a in ("base", "spline")
                                                    for b in ("gamma", "beta", "mean", "var")])
            sp.dma_start(base_w[:], i["L2_conv_base_weight"]).then_inc(s["spl_loaded"].h, 16)
            sp.dma_start(spw[:], i["L2_conv_spline_weight"]).then_inc(s["spl_loaded"].h, 16)
            sp.dma_start(scl[:], i["L2_conv_spline_scaler"]).then_inc(s["spl_loaded"].h, 16)
            wait(sp, "spl_loaded", 16 * 11)

        @block.vector
        def _(dve):
            ch = Chain(dve, s["spl_v"], s["spl_v"].base)
            for j, v in enumerate(knots):
                ins = dve.memset(kn[:, j:j + 1], -v)
            ins.then_inc(s["spl_range"].h, 1)
            wait(dve, "spl_loaded", 16 * 11)
            dve.tensor_tensor(spw[:], spw[:], scl[:].unsqueeze(2).to_broadcast([P, C, KN]),
                              ALU.mult).then_inc(s["spl_scaled"].h, 1)
            ch.note(dve.tensor_reduce(rng[:, 0:1], k.ch[:, 0:N], AX.X, ALU.min))
            ch.link(dve.tensor_reduce(rng[:, 1:2], k.ch[:, 0:N], AX.X, ALU.max))
            ch.link(dve.tensor_tensor(rng[:, 1:2], rng[:, 1:2], rng[:, 0:1], ALU.subtract))
            ch.link(dve.tensor_scalar(rng[:, 1:2], rng[:, 1:2], 1e-7, None, ALU.add))
            ch.link(dve.reciprocal(rng[:, 2:3], rng[:, 1:2]))
            wait(dve, "spl_root", 2)
            for j in range(2):
                g, bt, mn = (vec[:, 4 * j + a:4 * j + a + 1] for a in range(3))
                ch.link(dve.reciprocal(bn[:, j, 1:2], bn[:, j, 0:1]))
                ch.link(dve.tensor_tensor(bn[:, j, 1:2], bn[:, j, 1:2], g, ALU.mult))
                ch.link(dve.tensor_tensor(bn[:, j, 2:3], bn[:, j, 1:2], mn, ALU.mult))
                ch.link(dve.tensor_tensor(bn[:, j, 2:3], bt, bn[:, j, 2:3], ALU.subtract))
                ch.link(dve.tensor_scalar(bn[:, j, 3:4], bn[:, j, 1:2], -1.0, None, ALU.mult))

            k.spline_pre = ch.n

            def chunk(c, u):
                if past(c, 2):
                    wait(dve, "spl_abs", KN * (c - 1))
                dve.tensor_scalar(xu[:, u, :], k.ch[:, bass.ds(c * BANK, BANK)], rng[:, 0:1], rng[:, 2:3],
                                  ALU.subtract, ALU.mult).then_inc(s["spl_v"].h, 1)
                for j in range(KN):
                    wait(dve, "spl_abs", c * KN + j + 1)
                    if past(c, 1) or j >= 3:
                        wait(dve, "spl_basis_used", c * KN + j - 2)
                    dve.tensor_scalar(hat[:, j % 3, :], dist[:, j % 3, :], 1.0, 1.0, ALU.min,
                                      ALU.subtract).then_inc(s["spl_basis"].h, 1)
                wait(dve, "spl_basis_used", (c + 1) * KN)
                wait(dve, "spl_silu", 2 * (c + 1))
                dve.scalar_tensor_tensor(out=k.mixed[:, bass.ds(c * BANK, BANK)], in0=k.ps[:, 2 + u, :],
                                         scalar=bn[:, 1, 3:4], in1=silu[:, u, :], op0=ALU.mult,
                                         op1=ALU.add).then_inc(s["spl_bn"].h, 1)
            steps(dve, CHUNKS, 2, chunk)

        @block.scalar
        def _(act):
            wait(act, "spl_loaded", 16 * 11)
            for j in range(2):
                act.activation(bn[:, j, 0:1], vec[:, 4 * j + 3:4 * j + 4], ACT.Sqrt, bias=k.eps3).then_inc(s["spl_root"].h, 1)
            for t in range(KN):
                wait(act, "spl_wturned", t + 1)
                act.activation(spt[:, t, :], k.ps[:, 4 + t % 2, 0:P], ACT.Copy).then_inc(s["spl_wcopied"].h, 1)
            wait(act, "spl_range", 1)

            def chunk(c, u):
                act.wait_ge(s["spl_v"].h, s["spl_v"].base + k.spline_pre + c + 1)
                for j in range(KN):
                    if past(c, 1) or j >= 3:
                        wait(act, "spl_basis", c * KN + j - 2)
                    act.activation(dist[:, j % 3, :], xu[:, u, :], ACT.Abs, bias=kn[:, j:j + 1]).then_inc(s["spl_abs"].h, 1)
                wait(act, "spl_base", c + 1)
                if past(c, 2):
                    wait(act, "spl_bn", c - 1)
                act.activation(silu[:, u, :], k.ps[:, u, :], ACT.Silu, scale=bn[:, 0, 1:2],
                               bias=bn[:, 0, 2:3]).then_inc(s["spl_silu"].h, 1)
                wait(act, "spl_silu", 2 * c + 1)
                act.activation(silu[:, u, :], silu[:, u, :], ACT.Identity, bias=bn[:, 1, 2:3]).then_inc(s["spl_silu"].h, 1)
            steps(act, CHUNKS, 2, chunk)

        @block.tensor
        def _(pe):
            wait(pe, "spl_scaled", 1)
            for t in range(KN):
                if t >= 2:
                    wait(pe, "spl_wcopied", t - 1)
                pe.transpose(k.ps[:, 4 + t % 2, 0:P], spw[:, :, t], k.ident[:]).then_inc(s["spl_wturned"].h, 1)
            wait(pe, "spl_wcopied", KN)

            def chunk(c, u):
                if past(c, 2):
                    wait(pe, "spl_silu", 2 * (c - 1))
                pe.matmul(k.ps[:, u, :], base_w[:], k.ch[:, bass.ds(c * BANK, BANK)], start=True,
                          stop=True).then_inc(s["spl_base"].h, 1)
                if past(c, 2):
                    wait(pe, "spl_bn", c - 1)
                for j in range(KN):
                    wait(pe, "spl_basis", c * KN + j + 1)
                    ins = pe.matmul(k.ps[:, 2 + u, :], spt[:, j, :], hat[:, j % 3, :], start=(j == 0), stop=(j == KN - 1))
                    ins.then_inc(s["spl_basis_used"].h, 1)
            steps(pe, CHUNKS, 2, chunk)


def mixer_attention(k):
    nc, i = k.nc, k.ins
    names = ("att_loaded", "att_sq", "att_norm", "att_root", "att_unit", "att_turned", "att_copied", "att_value",
             "att_vcopied", "att_sim", "att_relu", "att_square", "att_y", "att_out", "att_xt")
    s = {n: k.sem(n) for n in names}

    def wait(eng, name, n):
        eng.wait_ge(s[name].h, s[name].base + n)

    xft = k.ch[:, 0:N]
    with ExitStack() as ctx, nc.Block() as block:
        def sb(name, shape, dt=F32):
            return ctx.enter_context(nc.sbuf_tensor(name, shape, dt))

        w = sb("att_w", [P, C])
        ssq = sb("att_norms", [P, NT])
        val = k.wts[:, 0:N].rearrange("p (t c) -> p t c", c=C)
        rel = sb("att_relu_buf", [P, 2, BANK])
        r2 = sb("att_weights", [P, 2, BANK])

        @block.sync
        def _(sp):
            sp.dma_start(w[:], i["L3_conv_W"]).then_inc(s["att_loaded"].h, 16)
            wait(sp, "att_loaded", 16)

        HALVES = 2 * B
        KEYS = TPB

        @block.scalar
        def _(act):
            def norms(t, u):
                one = bass.ds(t, 1)
                act.activation(k.mixed[:, bass.ds(t * P, P)], k.xn[:, one, :].rearrange("p a c -> p (a c)"), ACT.Square,
                               accum_out=ssq[:, one]).then_inc(s["att_sq"].h, 1)
            steps(act, NT, 2, norms)
            act.wait_ge(s["att_norm"].h, s["att_norm"].base + 1)
            act.activation(ssq[:], ssq[:], ACT.Sqrt).then_inc(s["att_root"].h, 1)

            def values(b, u):
                wait(act, "att_value", b + 1)
                act.activation(val[:, bass.ds(b * TPB, TPB), :].rearrange("p t c -> p (t c)"),
                               k.ps[:, 4 + 2 * u:6 + 2 * u, :].rearrange("p a n -> p (a n)"),
                               ACT.Copy).then_inc(s["att_vcopied"].h, 1)
                wait(act, "att_turned", b + 1)
                act.activation(xft[:, bass.ds(b * IMG, IMG)], k.ps[:, 2 * u:2 * u + 2, :].rearrange("p a n -> p (a n)"),
                               ACT.Copy).then_inc(s["att_copied"].h, 1)
            steps(act, B, 2, values)

            def relus(b, u):
                for h in range(2):
                    for j in range(KEYS):
                        n = h * KEYS + j
                        wait(act, "att_sim", b * 2 * KEYS + n + 1)
                        if past(b, 1) or n >= 2:
                            wait(act, "att_square", b * 2 * KEYS + n - 1)
                        act.activation(rel[:, n % 2, :], k.ps[:, n % 4, :], ACT.Relu).then_inc(s["att_relu"].h, 1)
            steps(act, B, 1, relus)

        @block.vector
        def _(dve):
            wait(dve, "att_sq", NT)
            dve.tensor_scalar(ssq[:], ssq[:], 1e-12, None, ALU.max).then_inc(s["att_norm"].h, 1)
            wait(dve, "att_root", 1)
            dve.reciprocal(ssq[:], ssq[:]).then_inc(s["att_norm"].h, 1)
            wait(dve, "att_norm", 2)

            def unit(b, u):
                for t in range(TPB):
                    one = bass.ds(b * TPB + t, 1)
                    v = k.xn[:, one, :].rearrange("p a c -> p (a c)")
                    ins = dve.tensor_scalar(v, v, ssq[:, one], None, ALU.mult)
                ins.then_inc(s["att_unit"].h, 1)
            steps(dve, B, 1, unit)

            def squares(b, u):
                for h in range(2):
                    for j in range(KEYS):
                        n = h * KEYS + j
                        wait(dve, "att_relu", b * 2 * KEYS + n + 1)
                        if past(b, 1) or n >= 2:
                            wait(dve, "att_y", b * 2 * KEYS + n - 1)
                        dve.tensor_tensor(r2[:, n % 2, :], rel[:, n % 2, :], rel[:, n % 2, :],
                                          ALU.mult).then_inc(s["att_square"].h, 1)
                    wait(dve, "att_y", b * 2 * KEYS + (h + 1) * KEYS)
                    dve.tensor_copy(k.mixed[:, bass.ds(b * IMG + h * BANK, BANK)],
                                    k.ps[:, 4 + h, :]).then_inc(s["att_out"].h, 1)
            steps(dve, B, 1, squares)

        @block.tensor
        def _(pe):
            wait(pe, "att_loaded", 16)

            def values(b, u):
                if past(b, 2):
                    wait(pe, "att_copied", b - 1)
                for t in range(TPB):
                    bank, at = 4 + 2 * u + t // 4, (t % 4) * P
                    ins = pe.matmul(k.ps[:, bank, at:at + P], xft[:, bass.ds(b * IMG + t * P, P)], w[:],
                                    start=True, stop=True)
                ins.then_inc(s["att_value"].h, 1)
                wait(pe, "att_unit", b + 1)
                for t in range(TPB):
                    bank, at = 2 * u + t // 4, (t % 4) * P
                    ins = pe.transpose(k.ps[:, bank, at:at + P],
                                       k.xn[:, bass.ds(b * TPB + t, 1), :].rearrange("p a c -> p (a c)"), k.ident[:])
                ins.then_inc(s["att_turned"].h, 1)
            spelled_out(B, 2, values)
            wait(pe, "att_copied", B)

            def attend(b, u):
                def sim(n):
                    h, j = n // KEYS, n % KEYS
                    if past(b, 1) or n >= 4:
                        wait(pe, "att_relu", b * 2 * KEYS + n - 3)
                    pe.matmul(k.ps[:, n % 4, :], xft[:, bass.ds(b * IMG + j * P, P)],
                              xft[:, bass.ds(b * IMG + h * BANK, BANK)], start=True, stop=True).then_inc(s["att_sim"].h, 1)

                def gather(n):
                    h, j = n // KEYS, n % KEYS
                    wait(pe, "att_square", b * 2 * KEYS + n + 1)
                    if j == 0 and past(b, 1):
                        wait(pe, "att_out", 2 * b + h - 1)
                    pe.matmul(k.ps[:, 4 + h, :], val[:, bass.ds(b * TPB + j, 1), :].rearrange("p a c -> p (a c)"),
                              r2[:, n % 2, :], start=(j == 0), stop=(j == KEYS - 1)).then_inc(s["att_y"].h, 1)

                sim(0)
                sim(1)
                for n in range(2 * KEYS):
                    if n + 2 < 2 * KEYS:
                        sim(n + 2)
                    gather(n)
            spelled_out(B, 1, attend)


def finish(k):
    nc = k.nc
    s_in, s_add, s_out = k.sem("last_rows"), k.sem("last_added"), k.sem("stored")
    src = k.returned[:].rearrange("(t p k) c -> p t (k c)", p=P, k=2)
    dst = k.out.rearrange("b h w c -> (b h w) c").rearrange("(t p) c -> p t c", p=P)
    with ExitStack() as ctx, nc.Block() as block:
        buf = [k.flat(k.rows0)[:, 0:4 * TPB * 2 * C].rearrange("p (b t c) -> p b t c", b=4, t=TPB),
               k.flat(k.rows1)[:, 0:4 * TPB * 2 * C].rearrange("p (b t c) -> p b t c", b=4, t=TPB)]
        s_each = [k.sem(f"last_rows{b}") for b in range(B)]

        @block.sync
        def _(sp):
            for b in range(B):
                sp.dma_start(buf[b // 4][:, b % 4], src[:, b * TPB:(b + 1) * TPB, :]).then_inc(s_each[b].h, 16)
            for b in range(B):
                sp.wait_ge(s_add.h, 2 * (b + 1))
                sp.dma_start(dst[:, b * TPB:(b + 1) * TPB, :], k.x[:, b * TPB:(b + 1) * TPB, :]).then_inc(s_out.h, 16)
            sp.wait_ge(s_out.h, 16 * B)

        @block.vector
        def _(dve):
            for b in range(B):
                dve.wait_ge(s_each[b].h, 16)
                xs = k.x[:, b * TPB:(b + 1) * TPB, :]
                for c in range(2):
                    dve.tensor_tensor(xs, xs, buf[b // 4][:, b % 4, :, c * C:(c + 1) * C], ALU.add).then_inc(s_add.h, 1)
                    dve.wait_ge(s_add.h, 2 * b + c + 1)


def build(nc, ins, out, upto=99):
    with ExitStack() as ctx:
        k = Core(nc, ctx, ins, out)
        constants(k)
        mixers = [mixer_fractal, mixer_involution, mixer_spline, mixer_attention]
        for layer in range(4):
            norm_mixer(k, layer)
            mixers[layer](k)
            norm_router(k, layer)
            experts(k, layer)
        finish(k)



NAMES = ["x",
         "L0_conv_w1", "L0_conv_b1", "L0_conv_w2", "L0_conv_b2", "L0_conv_gamma", "L0_conv_beta",
         "L0_conv_moving_mean", "L0_conv_moving_var",
         "L0_ffn_gate_w", "L0_ffn_gate_b", "L0_ffn_w1", "L0_ffn_b1", "L0_ffn_w2", "L0_ffn_b2",
         "L1_conv_W1", "L1_conv_b1", "L1_conv_W2", "L1_conv_b2",
         "L1_ffn_Wg", "L1_ffn_bg", "L1_ffn_W1", "L1_ffn_b1", "L1_ffn_W2", "L1_ffn_b2",
         "L2_conv_base_weight", "L2_conv_spline_weight", "L2_conv_spline_scaler",
         "L2_conv_bn_base_gamma", "L2_conv_bn_base_beta", "L2_conv_bn_base_mean", "L2_conv_bn_base_var",
         "L2_conv_bn_spline_gamma", "L2_conv_bn_spline_beta", "L2_conv_bn_spline_mean", "L2_conv_bn_spline_var",
         "L2_ffn_gate_w", "L2_ffn_gate_b", "L2_ffn_W1", "L2_ffn_b1", "L2_ffn_W2", "L2_ffn_b2",
         "L3_conv_W", "L3_ffn_gate_w", "L3_ffn_gate_b", "L3_ffn_w1", "L3_ffn_w2", "L3_ffn_w3"]


def kernel(**inputs):
    import concourse.bacc as bacc
    from concourse.bass_utils import run_bass_kernel_spmd

    nc = bacc.Bacc("TRN2", target_bir_lowering=False, num_devices=1)
    arrays, ins = {}, {}
    for name in NAMES:
        a = np.ascontiguousarray(inputs[name])
        arrays[f"in_{name}"] = a
        ins[name] = nc.dram_tensor(f"in_{name}", a.shape, F32, kind="ExternalInput").ap()
    out = nc.dram_tensor("out", (B, HH, WW, C), F32, kind="ExternalOutput").ap()
    build(nc, ins, out)
    r = run_bass_kernel_spmd(nc, [arrays], core_ids=[0])
    return r.results[0]["out"]
```

```python
from contextlib import ExitStack

import numpy as np

import concourse.bass as bass
from concourse import mybir

ALU = mybir.AluOpType
ACT = mybir.ActivationFunctionType
AX = mybir.AxisListType
F32 = mybir.dt.float32
BF16 = mybir.dt.bfloat16
I32 = mybir.dt.int32

P = 128
C = 128
B, HH, WW = 8, 32, 32
IMG = HH * WW
N = B * IMG
NT = N // P
TPB = IMG // P
BANK = 512
ROW = C + 2
REGION = N + P
NOWHERE = 1 << 20
EMAX = 16
LN2 = float(np.log(2.0))

FFN = [
    dict(E=8, F=512, K=1, over_chosen=False, act=ACT.Relu, gated=False, capacity=1280, guard=True),
    dict(E=8, F=512, K=2, over_chosen=True, act=ACT.Gelu, gated=False, capacity=None, guard=False),
    dict(E=8, F=256, K=2, over_chosen=False, act=ACT.Gelu, gated=False, capacity=None, guard=False),
    dict(E=16, F=256, K=2, over_chosen=True, act=ACT.Silu, gated=True, capacity=None, guard=False),
]


class Sem:

    def __init__(self, handle):
        self.h = handle
        self.base = 0


class Chain:

    def __init__(self, eng, sem, before):
        self.eng, self.sem, self.before, self.n = eng, sem, before, 0

    def note(self, ins):
        self.n += 1
        ins.then_inc(self.sem.h, 1)

    def settle(self):
        self.eng.wait_ge(self.sem.h, self.before + self.n)

    def link(self, ins):
        self.note(ins)
        self.settle()


def past(i, k):
    return not isinstance(i, int) or i >= k


def steps(eng, n, unroll, body):
    for u in range(unroll):
        body(u, u)
    if n // unroll > 1:
        with eng.Fori(1, n // unroll) as g:
            for u in range(unroll):
                body(g * unroll + u, u)
    for i in range(n // unroll * unroll, n):
        body(i, i % unroll)


def pipelined(eng, n, unroll, body):
    for u in range(unroll):
        body(u, u, False)
    with eng.Fori(1, n // unroll - 1) as g:
        for u in range(unroll):
            body(g * unroll + u, u, False)
    for i in range((n // unroll - 1) * unroll, n):
        body(i, i % unroll, i == n - 1)


def spelled_out(n, unroll, body):
    for i in range(n):
        body(i, i % unroll)


class Core:

    def __init__(self, nc, ctx, ins, out):
        self.nc, self.ctx, self.ins, self.out = nc, ctx, ins, out
        self.sems = {}

        def sb(name, shape, dt=F32):
            return ctx.enter_context(nc.sbuf_tensor(name, shape, dt))

        self.sb = sb
        self.x = sb("residual", [P, NT, C])
        self.ch = sb("channel_major", [P, B * 34 * 34])
        self.rows0 = sb("rows_first_choice", [P, NT, ROW])
        self.rows1 = sb("rows_second_choice", [P, NT, ROW])
        self.wts = sb("expert_weights", [P, 12288])
        self.ps = ctx.enter_context(nc.psum_tensor("psum", [P, 8, BANK], F32))
        self.xn = self.flat(self.rows0)[:, 0:N].rearrange("p (t c) -> p t c", c=C)
        self.mixed = self.flat(self.rows1)[:, 0:N]

        self.ident = sb("identity", [P, P])
        self.tri = sb("upper_triangle", [P, P], BF16)
        self.ones = sb("ones_square", [P, P], BF16)
        self.rank = sb("expert_rank", [P, EMAX])
        self.region = sb("region_start", [P, EMAX])
        self.partition = sb("partition_index", [P, 1])
        self.tile_no = sb("tile_number", [P, 144])
        self.token_id = sb("token_id", [P, NT, 2], I32)
        self.token_id1 = sb("token_id_one_choice", [P, NT], I32)
        self.pad_rows = sb("pad_rows", [P, ROW])
        self.zeros = sb("zeros", [P, C])
        self.eps = sb("epsilons", [P, 4])
        self.eps3, self.eps5, self.eps6, self.eps7 = (self.eps[:, j:j + 1] for j in range(4))
        self.stats = sb("bn_stats", [P, NT, 6])
        self.mean = sb("mean", [P, NT])
        self.var4 = sb("four_variances", [P, NT])
        self.rstd = sb("rstd", [P, NT])
        self.counts = sb("expert_counts", [P, EMAX])
        self.tile_expert = sb("tile_expert", [1, 144], I32)
        self.tile_row = sb("tile_row", [1, 144], I32)

        self.dispatched = nc.dram_tensor("dispatched", (EMAX * REGION + P, ROW), F32, kind="Internal").ap()
        self.returned = nc.dram_tensor("returned", (N * 2, C), F32, kind="Internal").ap()

    @staticmethod
    def flat(t):
        return t[:].rearrange("p t c -> p (t c)")

    def sem(self, name):
        if name not in self.sems:
            self.sems[name] = Sem(self.ctx.enter_context(self.nc.semaphore(name)))
        return self.sems[name]

    def advance(self, **counts):
        for name, n in counts.items():
            self.sems[name].base += n


def constants(k):
    nc = k.nc
    s_set = k.sem("const_set")
    s_made = k.sem("const_made")
    s_x = k.sem("x_loaded")
    x_dram = k.ins["x"].rearrange("b h w c -> (b h w) c").rearrange("(t p) c -> p t c", p=P)
    with ExitStack() as ctx, nc.Block() as block:
        int_rank = ctx.enter_context(nc.sbuf_tensor("int_rank", [P, EMAX], I32))
        int_region = ctx.enter_context(nc.sbuf_tensor("int_region", [P, EMAX], I32))
        int_part = ctx.enter_context(nc.sbuf_tensor("int_part", [P, 1], I32))
        int_tile = ctx.enter_context(nc.sbuf_tensor("int_tile", [P, 144], I32))

        @block.sync
        def _(sp):
            for b in range(B):
                sp.dma_start(k.x[:, b * TPB:(b + 1) * TPB, :], x_dram[:, b * TPB:(b + 1) * TPB, :]).then_inc(s_x.h, 16)
            sp.wait_ge(s_x.h, 16 * B)
            sp.wait_ge(s_made.h, 4)
            sp.dma_start(k.dispatched[EMAX * REGION:EMAX * REGION + P, :], k.pad_rows[:]).then_inc(s_x.h, 16)
            sp.dma_start(k.dispatched[8 * REGION:8 * REGION + P, :], k.pad_rows[:]).then_inc(s_x.h, 16)
            sp.wait_ge(s_x.h, 16 * (B + 2))

        @block.vector
        def _(dve):
            dve.memset(k.ident[:], 0.0).then_inc(s_set.h, 1)
            dve.memset(k.tri[:], 1.0).then_inc(s_set.h, 1)
            dve.memset(k.ones[:], 1.0).then_inc(s_set.h, 1)
            dve.memset(k.pad_rows[:], 0.0).then_inc(s_set.h, 1)
            dve.memset(k.zeros[:], 0.0).then_inc(s_set.h, 1)
            for j, value in enumerate((1e-3, 1e-5, 1e-6, 1e-7)):
                dve.memset(k.eps[:, j:j + 1], value)
            dve.wait_ge(s_made.h, 8)
            dve.tensor_copy(k.rank[:], int_rank[:])
            dve.tensor_copy(k.region[:], int_region[:])
            dve.tensor_copy(k.partition[:], int_part[:])
            dve.tensor_copy(k.tile_no[:], int_tile[:])

        @block.gpsimd
        def _(pool):
            pool.wait_ge(s_set.h, 4)
            pool.affine_select(out=k.ident[:], in_=k.ident[:], compare_op=ALU.not_equal, fill=1.0, base=0,
                               pattern=[[-1, P]], channel_multiplier=1).then_inc(s_made.h, 1)
            pool.affine_select(out=k.tri[:], in_=k.tri[:], compare_op=ALU.is_ge, fill=0.0, base=0,
                               pattern=[[1, P]], channel_multiplier=-1).then_inc(s_made.h, 1)
            pool.iota(k.pad_rows[:].bitcast(I32)[:, C:C + 1], pattern=[[0, 1]], base=NOWHERE,
                      channel_multiplier=0).then_inc(s_made.h, 1)
            pool.iota(int_rank[:], pattern=[[-1, EMAX]], base=EMAX, channel_multiplier=0).then_inc(s_made.h, 1)
            pool.iota(int_region[:], pattern=[[REGION, EMAX]], base=-1, channel_multiplier=0).then_inc(s_made.h, 1)
            pool.iota(int_part[:], pattern=[[0, 1]], base=0, channel_multiplier=1).then_inc(s_made.h, 1)
            pool.iota(int_tile[:], pattern=[[1, 144]], base=0, channel_multiplier=0).then_inc(s_made.h, 1)
            pool.iota(k.token_id[:], pattern=[[2 * P, NT], [1, 2]], base=0, channel_multiplier=2).then_inc(s_made.h, 1)
            pool.iota(k.token_id1[:], pattern=[[P, NT]], base=0, channel_multiplier=1)
    k.advance(const_set=5, const_made=8, x_loaded=16 * (B + 2))


STAT_OPS = 6


def finish_stats(dve, k, ch, tiles=slice(0, NT)):
    mean, var4, spare = k.mean[:, tiles], k.var4[:, tiles], k.rstd[:, tiles]

    def col(j):
        return k.stats[:, tiles, j]
    ch.note(dve.tensor_tensor(mean, col(1), col(4), ALU.add))
    ch.note(dve.tensor_tensor(var4, col(1), col(4), ALU.subtract))
    ch.note(dve.tensor_tensor(spare, col(2), col(5), ALU.add))
    ch.settle()
    ch.note(dve.tensor_scalar(mean, mean, 0.5, None, ALU.mult))
    ch.link(dve.tensor_tensor(var4, var4, var4, ALU.mult))
    ch.link(dve.scalar_tensor_tensor(out=var4, in0=spare, scalar=4.0 / C, in1=var4, op0=ALU.mult, op1=ALU.add))


def norm_mixer(k, layer):
    nc = k.nc
    choices = FFN[layer - 1]["K"] if layer else 0
    s_y, s_v = k.sem("rows_back0"), k.sem("vector_step")
    s_y1 = k.sem("rows_back1")
    s_root, s_rstd = k.sem("root_ready"), k.sem("rstd_ready")
    s_norm, s_turned, s_evac = k.sem("norm_ready"), k.sem("turned"), k.sem("turned_copied")
    s_pad = k.sem("border_cleared")
    padded = layer == 1
    per = choices + TPB
    norm3 = layer == 3
    ch4 = k.ch[:].rearrange("p (b h w) -> p b h w", b=B, h=34)
    with ExitStack() as ctx, nc.Block() as block:
        back = ctx.enter_context(nc.sbuf_tensor(f"back_{layer}", [P, 2, TPB, max(choices, 1) * C], F32)) if choices else None
        src = k.returned[0:N * choices, :].rearrange("(t p k) c -> p t (k c)", p=P, k=choices) if choices else None

        if choices:
            @block.sync
            def _(sp):
                def load(b, u):
                    if past(b, 2):
                        sp.wait_ge(s_v.h, s_v.base + (b - 2) * per + choices)
                    sp.dma_start(back[:, u], src[:, bass.ds(b * TPB, TPB), :]).then_inc((s_y, s_y1)[u].h, 16)
                spelled_out(B, 2, load)

        @block.vector
        def _(dve):
            def first(b, u):
                ch = Chain(dve, s_v, s_v.base + b * per)
                tiles = bass.ds(b * TPB, TPB)
                if choices:
                    dve.wait_ge((s_y, s_y1)[u].h, (s_y, s_y1)[u].base + (b - u) * 8 + 16)
                    for c in range(choices):
                        ins = dve.tensor_tensor(k.x[:, tiles, :], k.x[:, tiles, :], back[:, u, :, c * C:(c + 1) * C], ALU.add)
                        ch.link(ins)
                for t in range(TPB):
                    one = bass.ds(b * TPB + t, 1)
                    ch.note(dve.bn_stats(k.stats[:, one, :].rearrange("p a c -> p (a c)"),
                                         k.x[:, one, :].rearrange("p a c -> p (a c)")))
            spelled_out(B, 2, first)
            ch = Chain(dve, s_v, s_v.base + B * per)
            ch.settle()
            finish_stats(dve, k, ch)
            dve.wait_ge(s_root.h, s_root.base + 1)
            dve.reciprocal(k.rstd[:], k.rstd[:]).then_inc(s_rstd.h, 1)
            dve.wait_ge(s_rstd.h, s_rstd.base + 1)
            if padded:
                dve.memset(k.ch[:], 0.0).then_inc(s_pad.h, 1)

            def second(b, u):
                for t in range(TPB):
                    one = bass.ds(b * TPB + t, 1)
                    ins = dve.tensor_scalar(k.xn[:, one, :].rearrange("p a c -> p (a c)"),
                                            k.x[:, one, :].rearrange("p a c -> p (a c)"),
                                            k.mean[:, one], k.rstd[:, one],
                                            ALU.subtract, ALU.mult)
                ins.then_inc(s_norm.h, 1)
            spelled_out(B, 2, second)

        @block.tensor
        def _(pe):
            def turn(b, u):
                pe.wait_ge(s_norm.h, s_norm.base + b + 1)
                if past(b, 2):
                    pe.wait_ge(s_evac.h, s_evac.base + b - 1)
                for t in range(TPB):
                    bank, at = 2 * u + t // 4, (t % 4) * P
                    ins = pe.transpose(k.ps[:, bank, at:at + P],
                                       k.xn[:, bass.ds(b * TPB + t, 1), :].rearrange("p a c -> p (a c)"), k.ident[:])
                ins.then_inc(s_turned.h, 1)
            spelled_out(B, 2, turn)

        @block.scalar
        def _(act):
            act.wait_ge(s_v.h, s_v.base + B * per + STAT_OPS)
            act.activation(k.rstd[:], k.var4[:], ACT.Sqrt, bias=k.eps6, scale=0.25).then_inc(s_root.h, 1)
            if padded:
                act.wait_ge(s_pad.h, s_pad.base + 1)

            def evac(b, u):
                act.wait_ge(s_turned.h, s_turned.base + b + 1)
                src_ps = k.ps[:, 2 * u:2 * u + 2, :]
                if padded:
                    dst = ch4[:, bass.ds(b, 1), 1:33, 1:33].rearrange("p a h w -> p (a h) w")
                    ins = act.activation(dst, src_ps.rearrange("p a (h w) -> p (a h) w", w=WW), ACT.Copy)
                else:
                    ins = act.activation(k.ch[:, bass.ds(b * IMG, IMG)], src_ps.rearrange("p a n -> p (a n)"), ACT.Copy)
                ins.then_inc(s_evac.h, 1)
            spelled_out(B, 2, evac)
    k.advance(vector_step=B * per + STAT_OPS, root_ready=1, rstd_ready=1, norm_ready=B, turned=B, turned_copied=B)
    if choices:
        k.advance(rows_back0=16 * B // 2, rows_back1=16 * B // 2)
    if padded:
        k.advance(border_cleared=1)


def ffn_inputs(k, layer):
    i = k.ins
    if layer == 0:
        return i["L0_ffn_gate_w"], i["L0_ffn_gate_b"], i["L0_ffn_w1"], i["L0_ffn_b1"], i["L0_ffn_w2"], i["L0_ffn_b2"]
    if layer == 1:
        return i["L1_ffn_Wg"], i["L1_ffn_bg"], i["L1_ffn_W1"], i["L1_ffn_b1"], i["L1_ffn_W2"], i["L1_ffn_b2"]
    if layer == 2:
        return i["L2_ffn_gate_w"], i["L2_ffn_gate_b"], i["L2_ffn_W1"], i["L2_ffn_b1"], i["L2_ffn_W2"], i["L2_ffn_b2"]
    return i["L3_ffn_gate_w"], i["L3_ffn_gate_b"], i["L3_ffn_w1"], i["L3_ffn_w2"], i["L3_ffn_w3"], None


ROUTE_STATS = 1 + TPB + STAT_OPS


class Router:

    BANK_A, BANK_B = 6, 7

    def __init__(self, k, layer, ctx, mixed, mixed_ready, room=None):
        nc, f = k.nc, FFN[layer]
        self.k, self.nc, self.layer, self.f = k, nc, layer, f
        self.mixed, self.mixed_ready = mixed, mixed_ready
        self.E, self.K = E, K = f["E"], f["K"]
        self.T = N * K // P + E
        self.G = E + K - 1
        self.choose_ops = 7 if K == 1 else 14
        self.place_ops = 3 + 3 * K + 2 + (4 if f["capacity"] else 0)
        names = ("mix_turned", "add_step", "route_root", "route_rstd", "rows_ready", "rows_turned", "rows_kept",
                 "rows_copied", "gate_loaded", "logits_ready", "choose_step", "chosen", "shifted", "exp_ready", "ranked",
                 "place_step", "slots_ready", "rows_sent", "pads_ready", "weights_loaded", "plan_step", "route_reset")
        self.s = {n: k.sem(n) for n in names}

        taken = 0

        def sb(name, shape, dt=F32):
            nonlocal taken
            size = int(np.prod(shape[1:]))
            if room is None or dt == BF16 or taken + size > room.shape[1]:
                return ctx.enter_context(nc.sbuf_tensor(f"{name}_{layer}", shape, dt))[:]
            view = room[:, taken:taken + size]
            taken += size
            view = view if dt == F32 else view.bitcast(dt)
            if len(shape) == 2:
                return view
            letters = "abc"[:len(shape) - 1]
            return view.rearrange(f"p ({' '.join(letters)}) -> p {' '.join(letters)}",
                                  **{x: n for x, n in zip(letters, shape[1:])})

        self.gw = sb("gate_w", [P, E])
        self.gb = sb("gate_b", [P, E])
        self.turned = sb("turned_rows", [P, IMG])
        self.lg = sb("logits", [P, TPB, E])
        self.lg2 = sb("logits_rest", [P, TPB, E])
        self.oh = [sb("choice0", [P, TPB, E]), sb("choice1", [P, TPB, E])]
        self.top = sb("top", [P, 4, TPB])
        self.ex = sb("exponents", [P, TPB, self.G])
        self.exo = sb("exponentials", [P, TPB, self.G])
        self.msk = sb("chosen_mask", [P, TPB + 1, E], BF16)
        self.pos = sb("position", [P, TPB, E])
        self.posr = sb("position_row", [P, TPB, E])
        self.tmp = sb("routing_tmp", [P, TPB, E])
        self.wsum = sb("weight_sum", [P, 3, TPB])
        self.slotf = sb("slot_float", [P, 2, TPB])
        self.slot = sb("slot", [P, 2, 2, TPB], I32)
        self.padf = sb("pad_slot_float", [P, E])
        self.padi = sb("pad_slot", [P, E], I32)
        self.nti = sb("tiles_int", [P, E], I32)
        self.ntf = sb("tiles", [P, 3, E])
        self.plan = self.turned[:, 0:3 * 144].rearrange("p (a n) -> p a n", a=3)
        self.rows = [k.rows0, k.rows1]

    def when(self, name, n):
        return self.s[name].h, self.s[name].base + n

    def over_e(self, v):
        return v.unsqueeze(2).to_broadcast([P, TPB, self.E])

    def over_t(self, v):
        return v.unsqueeze(1).to_broadcast([P, TPB, self.E])

    def load_gate(self, sp):
        gate_w, gate_b = ffn_inputs(self.k, self.layer)[:2]
        sp.dma_start(self.gw[:], gate_w).then_inc(self.s["gate_loaded"].h, 16)
        sp.dma_start(self.gb[:], gate_b.partition_broadcast(P)).then_inc(self.s["gate_loaded"].h, 16)
        sp.wait_ge(*self.when("gate_loaded", 32))

    def load_weights(self, sp):
        for dst, src in expert_weight_loads(self.k, self.layer):
            sp.dma_start(dst, src).then_inc(self.s["weights_loaded"].h, 16)

    def turn_back(self, pe, b):
        sem, n = self.mixed_ready(b)
        pe.wait_ge(sem.h, n)
        if b:
            pe.wait_ge(*self.when("place_step", b * self.place_ops))
        mixed = self.mixed(b)
        for t in range(TPB):
            bank, at = (self.BANK_A, self.BANK_B)[t // 4], (t % 4) * P
            ins = pe.transpose(self.k.ps[:, bank, at:at + P], mixed[:, t * P:(t + 1) * P], self.k.ident[:])
        ins.then_inc(self.s["mix_turned"].h, 1)

    def turn_rows(self, pe, b):
        pe.wait_ge(*self.when("rows_ready", b + 1))
        for t in range(TPB):
            bank, at = (self.BANK_A, self.BANK_B)[t // 4], (t % 4) * P
            ins = pe.transpose(self.k.ps[:, bank, at:at + P], self.k.rows0[:, b * TPB + t, 0:C], self.k.ident[:])
        ins.then_inc(self.s["rows_turned"].h, 1)

    def gate(self, pe, b):
        E = self.E
        if b == 0:
            pe.wait_ge(*self.when("gate_loaded", 32))
        pe.wait_ge(*self.when("rows_kept", b + 1))
        for t in range(TPB):
            ins = pe.matmul(self.k.ps[:, self.BANK_B, t * E:(t + 1) * E], self.turned[:, t * P:(t + 1) * P], self.gw[:],
                            start=True, stop=True)
        ins.then_inc(self.s["logits_ready"].h, 1)

    def rank(self, pe, b):
        E, msk = self.E, self.msk
        pe.wait_ge(*self.when("chosen", b + 1))
        pe.matmul(self.k.ps[:, self.BANK_B, 0:(TPB + 1) * E], self.k.tri[:], msk[:].rearrange("p t e -> p (t e)"),
                  start=True, stop=True)
        for t in range(TPB):
            later = self.k.ps[:, self.BANK_B, (t + 1) * E:(TPB + 1) * E].rearrange("p (t e) -> p t e", e=E)
            ins = pe.matmul(later, self.k.ones[:], msk[:, t:t + 1, :].to_broadcast([P, TPB - t, E]),
                            start=False, stop=True, skip_group_check=True)
        ins.then_inc(self.s["ranked"].h, 1)

    def reset(self, dve):
        dve.memset(self.k.counts[:], 0.0).then_inc(self.s["route_reset"].h, 1)
        dve.memset(self.msk[:], 0.0).then_inc(self.s["route_reset"].h, 1)
        dve.wait_ge(*self.when("route_reset", 2))

    def add(self, dve, b):
        k, tiles = self.k, slice(b * TPB, (b + 1) * TPB)
        ch = Chain(dve, self.s["add_step"], self.s["add_step"].base + b * ROUTE_STATS)
        dve.wait_ge(*self.when("mix_turned", b + 1))
        xs = k.x[:, tiles, :].rearrange("p t c -> p (t c)")
        both = k.ps[:, self.BANK_A:self.BANK_B + 1, :].rearrange("p a n -> p (a n)")
        ch.link(dve.tensor_tensor(xs, xs, both, ALU.add))
        for t in range(b * TPB, (b + 1) * TPB):
            ch.note(dve.bn_stats(k.stats[:, t, :], k.x[:, t, :]))
        ch.settle()
        finish_stats(dve, k, ch, tiles)
        assert ch.n == ROUTE_STATS

    def norm(self, dve, b):
        k, tiles = self.k, slice(b * TPB, (b + 1) * TPB)
        dve.wait_ge(*self.when("route_root", b + 1))
        dve.reciprocal(k.rstd[:, tiles], k.rstd[:, tiles]).then_inc(self.s["route_rstd"].h, 1)
        dve.wait_ge(*self.when("route_rstd", b + 1))
        for t in range(b * TPB, (b + 1) * TPB):
            ins = dve.tensor_scalar(k.rows0[:, t, 0:C], k.x[:, t, :], k.mean[:, t:t + 1], k.rstd[:, t:t + 1],
                                    ALU.subtract, ALU.mult)
        ins.then_inc(self.s["rows_ready"].h, 1)
        for c in range(self.K):
            src = k.token_id1[:, tiles] if self.K == 1 else k.token_id[:, tiles, c]
            dve.tensor_copy(self.rows[c][:].bitcast(I32)[:, tiles, C], src)

    def choose(self, dve, b):
        k, E, K = self.k, self.E, self.K
        lg, lg2, oh, top, ex, msk = self.lg, self.lg2, self.oh, self.top, self.ex, self.msk
        ch = Chain(dve, self.s["choose_step"], self.s["choose_step"].base + b * self.choose_ops)

        def best_of(logits, c):
            best, tie = top[:, 2 * c, :], top[:, 2 * c + 1, :]
            ch.link(dve.tensor_reduce(best, logits, AX.X, ALU.max))
            ch.link(dve.tensor_tensor(oh[c][:], logits, self.over_e(best), ALU.is_equal))
            ch.link(dve.tensor_tensor(oh[c][:], oh[c][:], self.over_t(k.rank[:, 0:E]), ALU.mult))
            ch.link(dve.tensor_reduce(tie, oh[c][:], AX.X, ALU.max))
            ch.link(dve.tensor_tensor(oh[c][:], oh[c][:], self.over_e(tie), ALU.is_equal))

        dve.wait_ge(*self.when("logits_ready", b + 1))
        if b == 0:
            dve.wait_ge(*self.when("gate_loaded", 32))
        logits = k.ps[:, self.BANK_B, 0:TPB * E].rearrange("p (t e) -> p t e", e=E)
        ch.link(dve.tensor_tensor(lg[:], logits, self.over_t(self.gb[:]), ALU.add))
        best_of(lg[:], 0)
        if K == 2:
            ch.link(dve.scalar_tensor_tensor(out=lg2[:], in0=oh[0][:], scalar=-1e30, in1=lg[:],
                                             op0=ALU.mult, op1=ALU.add))
            best_of(lg2[:], 1)
            dve.tensor_tensor(msk[:, 0:TPB, :], oh[0][:], oh[1][:], ALU.add).then_inc(self.s["chosen"].h, 1)
            ch.note(dve.tensor_tensor(ex[:, :, E], top[:, 2, :], top[:, 0, :], ALU.subtract))
        else:
            dve.tensor_copy(msk[:, 0:TPB, :], oh[0][:]).then_inc(self.s["chosen"].h, 1)
        ch.note(dve.tensor_tensor(ex[:, :, 0:E], lg[:], self.over_e(top[:, 0, :]), ALU.subtract))
        assert ch.n == self.choose_ops, ch.n

    def place(self, dve, b):
        k, E, K, f = self.k, self.E, self.K, self.f
        oh, pos, tmp, exo, wsum = self.oh, self.pos, self.tmp, self.exo, self.wsum
        tiles = slice(b * TPB, (b + 1) * TPB)
        ch = Chain(dve, self.s["place_step"], self.s["place_step"].base + b * self.place_ops)
        dve.wait_ge(*self.when("ranked", b + 1))
        ranks = k.ps[:, self.BANK_B, 0:(TPB + 1) * E].rearrange("p (t e) -> p t e", e=E)
        ch.link(dve.tensor_tensor(pos[:], ranks[:, 0:TPB, :], self.over_t(k.counts[:, 0:E]), ALU.add))
        ch.note(dve.tensor_tensor(k.counts[:, 0:E], k.counts[:, 0:E], ranks[:, TPB, :], ALU.add))
        ch.link(dve.tensor_tensor(self.posr[:], pos[:], self.over_t(k.region[:, 0:E]), ALU.add))
        for c in range(K):
            ch.link(dve.tensor_tensor(tmp[:], self.posr[:], oh[c][:], ALU.mult))
            ch.link(dve.tensor_reduce(self.slotf[:, c, :], tmp[:], AX.X, ALU.add))
            if b >= 2:
                dve.wait_ge(*self.when("rows_sent", 16 * TPB * K * (b - 1)))
            ch.link(dve.tensor_copy(self.slot[:, b % 2, c, :], self.slotf[:, c, :]))
        dve.wait_ge(*self.when("exp_ready", b + 1))
        w0 = wsum[:, 1, :]
        if f["over_chosen"]:
            ch.link(dve.tensor_scalar(wsum[:, 0, :], exo[:, :, E], 1.0, None, ALU.add))
        else:
            ch.link(dve.tensor_reduce(wsum[:, 0, :], exo[:, :, 0:E], AX.X, ALU.add))
        ch.link(dve.reciprocal(w0, wsum[:, 0, :]))
        if f["capacity"]:
            ch.link(dve.tensor_tensor(tmp[:], pos[:], oh[0][:], ALU.mult))
            ch.link(dve.tensor_reduce(wsum[:, 2, :], tmp[:], AX.X, ALU.add))
            ch.link(dve.tensor_scalar(wsum[:, 2, :], wsum[:, 2, :], float(f["capacity"]), None, ALU.is_le))
            ch.link(dve.tensor_tensor(w0, w0, wsum[:, 2, :], ALU.mult))
        dve.tensor_copy(k.rows0[:, tiles, C + 1], w0).then_inc(self.s["slots_ready"].h, 1)
        if K == 2:
            dve.tensor_tensor(k.rows1[:, tiles, C + 1], w0, exo[:, :, E], ALU.mult).then_inc(self.s["slots_ready"].h, 1)
        assert ch.n == self.place_ops, ch.n

    def make_plan(self, dve):
        k, E, T, ntf, acc = self.k, self.E, self.T, self.ntf, self.plan
        ch = Chain(dve, self.s["plan_step"], self.s["plan_step"].base)
        dve.wait_ge(*self.when("place_step", B * self.place_ops))
        cnt, reg = k.counts[:, 0:E], k.region[:, 0:E]
        ch.link(dve.tensor_tensor(self.padf[:], cnt, reg, ALU.add))
        ch.link(dve.tensor_scalar(self.padf[:], self.padf[:], k.partition[:, 0:1], 1.0, ALU.add, ALU.add))
        dve.tensor_copy(self.padi[:], self.padf[:]).then_inc(self.s["pads_ready"].h, 1)
        ch.link(dve.tensor_scalar(ntf[:, 0, :], cnt, float(P - 1), None, ALU.add))
        ch.link(dve.tensor_copy(self.nti[:], ntf[:, 0, :]))
        ch.link(dve.tensor_scalar(self.nti[:], self.nti[:], 7, None, ALU.logical_shift_right))
        ch.link(dve.tensor_copy(ntf[:, 0, :], self.nti[:]))
        ch.link(dve.memset(ntf[:, 1, :], 1.0))
        ch.link(dve.tensor_tensor_scan(ntf[:, 2, :], ntf[:, 1, :], ntf[:, 0, :], 0.0, ALU.mult, ALU.add))
        ch.link(dve.tensor_scalar(ntf[:, 1, :], ntf[:, 0, :], float(-P), float(REGION), ALU.mult, ALU.add))
        ch.note(dve.memset(acc[0:1, 0, 0:T], 0.0))
        ch.link(dve.tensor_scalar(acc[0:1, 1, 0:T], k.tile_no[0:1, 0:T], float(P), None, ALU.mult))
        for e in range(E):
            end, skip = ntf[0:1, 2, e:e + 1], ntf[0:1, 1, e:e + 1]
            ch.link(dve.tensor_scalar(acc[0:1, 2, 0:T], k.tile_no[0:1, 0:T], end, None, ALU.is_ge))
            ch.note(dve.tensor_tensor(acc[0:1, 0, 0:T], acc[0:1, 0, 0:T], acc[0:1, 2, 0:T], ALU.add))
            ch.link(dve.scalar_tensor_tensor(out=acc[0:1, 1, 0:T], in0=acc[0:1, 2, 0:T], scalar=skip,
                                             in1=acc[0:1, 1, 0:T], op0=ALU.mult, op1=ALU.add))
        ch.link(dve.tensor_scalar(acc[0:1, 0, 0:T], acc[0:1, 0, 0:T], float(E - 1), None, ALU.min))
        ch.link(dve.tensor_scalar(acc[0:1, 1, 0:T], acc[0:1, 1, 0:T], float(E * REGION), None, ALU.min))
        ch.note(dve.tensor_copy(k.tile_expert[0:1, 0:T], acc[0:1, 0, 0:T]))
        ch.link(dve.tensor_copy(k.tile_row[0:1, 0:T], acc[0:1, 1, 0:T]))
        self.plan_ops = ch.n

    def root(self, act, b):
        k, tiles = self.k, slice(b * TPB, (b + 1) * TPB)
        act.wait_ge(*self.when("add_step", (b + 1) * ROUTE_STATS))
        act.activation(k.rstd[:, tiles], k.var4[:, tiles], ACT.Sqrt, bias=k.eps5,
                       scale=0.25).then_inc(self.s["route_root"].h, 1)

    def keep_rows(self, act, b):
        k, tiles = self.k, slice(b * TPB, (b + 1) * TPB)
        act.wait_ge(*self.when("rows_turned", b + 1))
        if b:
            act.wait_ge(*self.when("logits_ready", b))
        act.activation(self.turned[:], k.ps[:, self.BANK_A:self.BANK_B + 1, :].rearrange("p a n -> p (a n)"),
                       ACT.Copy).then_inc(self.s["rows_kept"].h, 1)
        if self.K == 2:
            act.activation(k.rows1[:, tiles, 0:C], k.rows0[:, tiles, 0:C], ACT.Copy).then_inc(self.s["rows_copied"].h, 1)

    def exp(self, act, b):
        act.wait_ge(*self.when("choose_step", (b + 1) * self.choose_ops))
        if b:
            act.wait_ge(*self.when("slots_ready", self.K * b))
        act.activation(self.exo[:], self.ex[:], ACT.Exp).then_inc(self.s["exp_ready"].h, 1)

    def send(self, pool, b):
        K = self.K
        pool.wait_ge(*self.when("slots_ready", K * (b + 1)))
        if K == 2:
            pool.wait_ge(*self.when("rows_copied", b + 1))
        for t in range(TPB):
            for c in range(K):
                pool.indirect_dma_start(
                    out=self.k.dispatched,
                    out_offset=bass.IndirectOffsetOnAxis(ap=self.slot[:, b % 2, c, t:t + 1], axis=0),
                    in_=self.rows[c][:, b * TPB + t, :], in_offset=None).then_inc(self.s["rows_sent"].h, 16)
        pool.wait_ge(*self.when("rows_sent", 16 * TPB * K * (b + 1)))

    def send_pads(self, pool):
        pool.wait_ge(*self.when("pads_ready", 1))
        for e in range(self.E):
            pool.indirect_dma_start(
                out=self.k.dispatched, out_offset=bass.IndirectOffsetOnAxis(ap=self.padi[:, e:e + 1], axis=0),
                in_=self.k.pad_rows[:], in_offset=None).then_inc(self.s["rows_sent"].h, 16)
        pool.wait_ge(*self.when("rows_sent", 16 * (NT * self.K + self.E)))

    def finish_tensor(self, pe):
        for part in (self.turn_back, self.turn_rows, self.gate, self.rank):
            part(pe, B - 1)

    def finish_vector(self, dve):
        for part in (self.add, self.norm, self.choose, self.place):
            part(dve, B - 1)
        self.make_plan(dve)

    def finish_scalar(self, act):
        for part in (self.root, self.keep_rows, self.exp):
            part(act, B - 1)

    def send_all(self, pool):
        for b in range(B):
            self.send(pool, b)
        self.send_pads(pool)

    def tensor_between(self, pe, b, n, of):
        if b:
            between(n, of, (2, 7, 9, 12), (self.turn_back, self.turn_rows, self.gate, self.rank), pe, b - 1)

    def vector_between(self, dve, b, n, of):
        if b:
            between(n, of, (3, 5, 10, 14), (self.add, self.norm, self.choose, self.place), dve, b - 1)

    def scalar_between(self, act, b, n, of):
        if b:
            between(n, of, (4, 8, 12), (self.root, self.keep_rows, self.exp), act, b - 1)

    def done(self):
        E, K = self.E, self.K
        self.k.advance(mix_turned=B, add_step=B * ROUTE_STATS, route_root=B, route_rstd=B, rows_ready=B, rows_turned=B,
                       rows_kept=B, rows_copied=B if K == 2 else 0, gate_loaded=32, logits_ready=B,
                       choose_step=B * self.choose_ops, chosen=B, exp_ready=B, ranked=B,
                       place_step=B * self.place_ops, slots_ready=K * B, rows_sent=16 * (NT * K + E), pads_ready=1,
                       plan_step=self.plan_ops, route_reset=2)


def between(n, of, marks, parts, eng, b):
    for mark, part in zip(marks, parts):
        if n == mark * of // 16:
            part(eng, b)


def expert_weight_loads(k, layer):
    f = FFN[layer]
    E, F = f["E"], f["F"]
    _, _, w1, b1, w2, b2 = ffn_inputs(k, layer)
    first, second = expert_weight_views(k, layer)
    if not f["gated"]:
        return [(first, w1.rearrange("e c f -> c e f")),
                (second, w2.rearrange("e (j h) c -> h e j c", h=P))]
    w3 = w2
    return [(first[:, :, 0:F], w1.rearrange("e c f -> c e f")),
            (first[:, :, F:2 * F], b1.rearrange("e c f -> c e f")),
            (second, w3.rearrange("e (j h) c -> h e j c", h=P))]


def expert_weight_views(k, layer):
    f = FFN[layer]
    E, F = f["E"], f["F"]
    wide = 2 * F if f["gated"] else F
    first = k.wts[:, 0:E * wide].rearrange("p (e f) -> p e f", e=E)
    second = k.wts[:, E * wide:E * wide + E * F].rearrange("p (e j c) -> p e j c", e=E, j=F // P)
    return first, second


RING = 16


def experts(k, layer):
    nc, f = k.nc, FFN[layer]
    E, K, F = f["E"], f["K"], f["F"]
    T = N * K // P + E
    J = F // P
    gated = f["gated"]
    wide = 2 * F if gated else F
    _, _, w1, b1, w2, b2 = ffn_inputs(k, layer)
    first, second = expert_weight_views(k, layer)
    names = ("x_turned", "x_copied", "w_copied", "hidden_ready", "act_ready", "gated_ready",
             "y_ready", "y_scaled", "bias_split", "bias_turned", "bias_kept", "guard_step", "bias_loaded")
    s = {n: k.sem(n) for n in names}
    s_row = [k.sem(f"slot_rows{r}") for r in range(RING)]
    s_out = [k.sem(f"results_sent{r}") for r in range(RING)]
    loads = 16 * len(expert_weight_loads(k, layer))
    uses = [len(range(r, T, RING)) for r in range(RING)]
    PSX, PSH, PSY = 0, 2, 4
    HB = 4

    def when(name, n):
        return s[name].h, s[name].base + n

    with ExitStack() as ctx, nc.Block() as block:
        def sb(name, shape, dt=F32):
            return ctx.enter_context(nc.sbuf_tensor(f"{name}_{layer}", shape, dt))

        sizes = (RING * ROW, RING * C, 2 * C, 2 * wide, HB * F, HB * F)
        starts = [sum(sizes[:j]) for j in range(len(sizes))]

        def room(j, n):
            return k.ch[:, starts[j]:starts[j] + sizes[j]].rearrange("p (a n) -> p a n", n=n)

        rt, ys, xt, wc, hs = room(0, ROW), room(1, C), room(2, C), room(3, wide), room(4, F)
        gs = room(5, F) if gated else hs
        if f["guard"]:
            gm = sb("guard", [P, 3, C])
            carry = sb("guard_carry", [P, 2])
        if b2 is not None:
            brows = sb("bias_rows", [E * J, P])
            bcol = sb("bias_columns", [P, E * J])
            n2 = E * C
            bp2 = sb("bias_parts", [3, E, C], BF16)
            brow = k.flat(k.rows1)[0:1, 0:n2]
            bpart = k.flat(k.rows0).bitcast(BF16)[0:1, 0:3 * n2].rearrange("p (a n) -> p a n", a=3)

        @block.sync
        def _(sp):
            if b2 is not None:
                sp.dma_start(brows[:], b1.rearrange("e (j h) -> (e j) h", h=P)).then_inc(s["bias_loaded"].h, 16)
                sp.dma_start(brow, b2.rearrange("(a e) f -> a (e f)", a=1)).then_inc(s["bias_loaded"].h, 16)
                sp.wait_ge(*when("bias_split", 5))
                for part in range(3):
                    sp.dma_start(bp2[part:part + 1, :, :].rearrange("p e c -> p (e c)"),
                                 bpart[0:1, part, :]).then_inc(s["bias_loaded"].h, 16)

            def load(t, u):
                row = sp.value_load(k.tile_row[0:1, bass.ds(t, 1)], min_val=0, max_val=E * REGION)
                if past(t, RING):
                    sp.wait_ge(s_out[u].h, s_out[u].base + (t - u) * (16 // RING))
                sp.dma_start(rt[:, u, :], k.dispatched[bass.ds(row, P), :]).then_inc(s_row[u].h, 16)
            steps(sp, T, RING, load)

        @block.tensor
        def _(pe):
            if b2 is not None:
                pe.wait_ge(*when("bias_loaded", 16 * 5))
                pe.transpose(k.ps[:, PSY, 0:E * J], brows[:], k.ident[0:E * J, 0:E * J]).then_inc(s["bias_turned"].h, 1)
                pe.wait_ge(*when("bias_kept", 1))
            pe.wait_ge(k.sem("weights_loaded").h, k.sem("weights_loaded").base + loads)

            def turn_rows(t, u):
                pe.wait_ge(s_row[u].h, s_row[u].base + (t - u) * (16 // RING) + 16)
                pe.transpose(k.ps[:, PSX + u % 2, 0:P], rt[:, u, 0:C], k.ident[:]).then_inc(s["x_turned"].h, 1)

            def hidden(t, u):
                pe.wait_ge(*when("x_copied", t + 1))
                pe.wait_ge(*when("w_copied", t + 1))
                for j in range(wide // P):
                    ins = pe.matmul(k.ps[:, PSH + u % 2, j * P:(j + 1) * P], wc[:, u % 2, j * P:(j + 1) * P],
                                    xt[:, u % 2, :], start=True, stop=True)
                ins.then_inc(s["hidden_ready"].h, 1)

            def result(t, u):
                e = pe.value_load(k.tile_expert[0:1, bass.ds(t, 1)], min_val=0, max_val=E - 1)
                pe.wait_ge(*when("gated_ready" if gated else "act_ready", t + 1))
                bank = k.ps[:, PSY + u % 4, 0:C]
                if b2 is not None:
                    pe.matmul(bank, k.ones[0:3, :], bp2[:, bass.ds(e, 1), :].rearrange("p a f -> p (a f)"),
                              start=True, stop=False)
                for j in range(J):
                    ins = pe.matmul(bank, gs[:, u % HB, j * P:(j + 1) * P],
                                    second[:, bass.ds(e, 1), j, :].rearrange("p a c -> p (a c)"),
                                    start=(b2 is None and j == 0), stop=(j == J - 1))
                ins.then_inc(s["y_ready"].h, 1)

            turn_rows(0, 0)

            def step(t, u, last=False):
                if not last:
                    turn_rows(t + 1, (u + 1) % RING)
                if past(t, 2):
                    result(t - 2, (u - 2) % RING)
                hidden(t, u)

            pipelined(pe, T, RING, step)
            result(T - 2, (T - 2) % RING)
            result(T - 1, (T - 1) % RING)

        @block.scalar
        def _(act):
            if b2 is not None:
                act.wait_ge(*when("bias_turned", 1))
                act.activation(bcol[:], k.ps[:, PSY, 0:E * J], ACT.Copy).then_inc(s["bias_kept"].h, 1)
                act.wait_ge(*when("bias_kept", 1))
            act.wait_ge(k.sem("weights_loaded").h, k.sem("weights_loaded").base + loads)

            def copy_weights(t, u):
                e = act.value_load(k.tile_expert[0:1, bass.ds(t, 1)], min_val=0, max_val=E - 1)
                if past(t, 2):
                    act.wait_ge(*when("hidden_ready", t - 1))
                act.activation(wc[:, u % 2, :], first[:, bass.ds(e, 1), :].rearrange("p a f -> p (a f)"),
                               ACT.Copy).then_inc(s["w_copied"].h, 1)

            def activate(t, u):
                if not gated:
                    e = act.value_load(k.tile_expert[0:1, bass.ds(t, 1)], min_val=0, max_val=E - 1)
                act.wait_ge(*when("hidden_ready", t + 1))
                if gated:
                    if past(t, HB):
                        act.wait_ge(*when("gated_ready", t - HB + 1))
                    act.activation(hs[:, u % HB, :], k.ps[:, PSH + u % 2, 0:F], f["act"]).then_inc(s["act_ready"].h, 1)
                    return
                if past(t, HB):
                    act.wait_ge(*when("y_ready", t - HB + 1))
                for j in range(J):
                    cols = slice(j * P, (j + 1) * P)
                    ins = act.activation(hs[:, u % HB, cols], k.ps[:, PSH + u % 2, cols], f["act"],
                                         bias=bcol[:, bass.ds(e * J + j, 1)])
                ins.then_inc(s["act_ready"].h, 1)

            def step(t, u, last=False):
                if not last:
                    copy_weights(t + 1, (u + 1) % RING)
                activate(t, u)

            copy_weights(0, 0)
            pipelined(act, T, RING, step)

        @block.vector
        def _(dve):
            if b2 is not None:
                dve.wait_ge(*when("bias_loaded", 32))
                ch = Chain(dve, s["bias_split"], s["bias_split"].base)
                for part in range(3):
                    ch.link(dve.tensor_copy(bpart[0:1, part, :], brow))
                    if part < 2:
                        ch.link(dve.tensor_tensor(brow, brow, bpart[0:1, part, :], ALU.subtract))

            def copy_rows(t, u):
                dve.wait_ge(*when("x_turned", t + 1))
                if past(t, 2):
                    dve.wait_ge(*when("hidden_ready", t - 1))
                dve.tensor_copy(xt[:, u % 2, :], k.ps[:, PSX + u % 2, 0:P]).then_inc(s["x_copied"].h, 1)

            def gate(t, u):
                dve.wait_ge(*when("act_ready", t + 1))
                if past(t, HB):
                    dve.wait_ge(*when("y_ready", t - HB + 1))
                dve.tensor_tensor(gs[:, u % HB, :], hs[:, u % HB, :], k.ps[:, PSH + u % 2, F:2 * F],
                                  ALU.mult).then_inc(s["gated_ready"].h, 1)

            def scale(t, u):
                dve.wait_ge(*when("y_ready", t + 1))
                if past(t, RING):
                    dve.wait_ge(s_out[u].h, s_out[u].base + (t - u) * (16 // RING))
                y = ys[:, u, :]
                weight = rt[:, u, C + 1:C + 2]
                if not f["guard"]:
                    dve.tensor_scalar(y, k.ps[:, PSY + u % 4, 0:C], weight, None, ALU.mult).then_inc(s["y_scaled"].h, 1)
                    return
                ch = Chain(dve, s["guard_step"], s["guard_step"].base + t * 7)
                ch.link(dve.tensor_scalar(y, k.ps[:, PSY + u % 4, 0:C], weight, None, ALU.mult))
                ch.note(dve.tensor_scalar(gm[:, 0, :], y, 1e4, -1e4, ALU.min, ALU.max))
                ch.note(dve.scalar_tensor_tensor(out=gm[:, 1, :], in0=y, scalar=0.0, in1=k.zeros[:],
                                                 op0=ALU.mult, op1=ALU.not_equal))
                ch.note(dve.tensor_tensor(gm[:, 2, :], y, y, ALU.not_equal))
                ch.settle()
                ch.note(dve.tensor_copy(carry[:, 0:1], k.zeros[:, 0:1]))
                ch.link(dve.copy_predicated(y, gm[:, 1, :].bitcast(I32), gm[:, 0, :]))
                ch.note(dve.tensor_copy(carry[:, 1:2], k.zeros[:, 0:1]))
                dve.copy_predicated(y, gm[:, 2, :].bitcast(I32), k.zeros[:]).then_inc(s["y_scaled"].h, 1)

            copy_rows(0, 0)

            def step(t, u, last=False):
                if not last:
                    copy_rows(t + 1, (u + 1) % RING)
                if gated:
                    gate(t, u)
                if past(t, 2):
                    scale(t - 2, (u - 2) % RING)

            pipelined(dve, T, RING, step)
            scale(T - 2, (T - 2) % RING)
            scale(T - 1, (T - 1) % RING)

        @block.gpsimd
        def _(pool):
            last = pool.to_reg(N * K - 1)

            def send(t, u):
                pool.wait_ge(*when("y_scaled", t + 1))
                pool.indirect_dma_start(
                    out=k.returned[0:N * K, :],
                    out_offset=bass.IndirectOffsetOnAxis(ap=rt[:, u, C:C + 1].bitcast(I32), axis=0),
                    in_=ys[:, u, :], in_offset=None, bounds_check=last, oob_is_err=False).then_inc(s_out[u].h, 16)
            spelled_out(T, RING, send)
            for u in range(RING):
                pool.wait_ge(s_out[u].h, s_out[u].base + 16 * uses[u])

    k.advance(x_turned=T, x_copied=T, w_copied=T, hidden_ready=T, act_ready=T,
              y_ready=T, y_scaled=T, weights_loaded=loads)
    if gated:
        k.advance(gated_ready=T)
    if f["guard"]:
        k.advance(guard_step=7 * T)
    if b2 is not None:
        k.advance(bias_split=5, bias_loaded=16 * 5, bias_turned=1, bias_kept=1)
    for r in range(RING):
        s_row[r].base += 16 * uses[r]
        s_out[r].base += 16 * uses[r]


def load_columns(sp, sem, dst, vectors):
    for j, v in enumerate(vectors):
        sp.dma_start(dst[:, j:j + 1], v.rearrange("(c a) -> c a", a=1)).then_inc(sem.h, 16)


def mixer_fractal(k):
    nc, i = k.nc, k.ins
    RED = i["L0_conv_w1"].shape[1]
    names = ("mix_loaded", "mix_v", "mix_range", "mix_allmax", "mix_pad", "mix_boxes", "mix_logs", "mix_pool",
             "mix_slope", "mix_squares", "mix_energy", "mix_sq1", "mix_sq2", "mix_prep", "mix_mm", "mix_excite",
             "mix_root", "mix_sig", "mix_sim", "mix_out", "mix_pool2", "mix_used")
    s = {n: k.sem(n) for n in names}

    def when(name, n):
        return s[name].h, s[name].base + n

    SIDE = 47
    slope_scale = 0.1 / LN2
    norm_scale = slope_scale * float(np.sqrt(5.0) * LN2)
    xch = k.ch[:, 0:N].rearrange("p (b n) -> p b n", b=B)
    slope = k.flat(k.rows0).rearrange("p (b n) -> p b n", b=B)[:, :, 0:IMG]
    energy = k.mixed.rearrange("p (b n) -> p b n", b=B)
    with ExitStack() as ctx, nc.Block() as block:
        def sb(name, shape, dt=F32):
            return ctx.enter_context(nc.sbuf_tensor(name, shape, dt))

        w = k.wts[:]
        pad = w[:, 0:SIDE * SIDE].rearrange("p (h w) -> p h w", w=SIDE)
        tmp = w[:, 2210:2210 + 47 * 46]
        s2 = w[:, 4372:4372 + 46 * 46].rearrange("p (h w) -> p h w", w=46)
        s4 = w[:, 6488:6488 + 44 * 44].rearrange("p (h w) -> p h w", w=44)
        s8 = w[:, 8424:8424 + 40 * 40].rearrange("p (h w) -> p h w", w=40)
        logs = sb("logs", [P, 4, IMG])
        s16 = logs[:, 3, :].rearrange("p (h w) -> p h w", w=WW)
        con = [w[:, 10024:11048], w[:, 11048:12072], k.ch[:, N:N + IMG]]
        vec = sb("mix_vectors", [P, 8])
        w1 = sb("squeeze_w", [P, RED])
        w2 = sb("excite_w", [RED, P])
        b1 = sb("squeeze_b", [RED, 1])
        rng = sb("range", [P, 2, B])
        rngall = sb("range_all", [P, 2, B])
        inv = sb("range_inverse", [P, B])
        lowest = sb("lowest", [P, B])
        sums = sb("slope_sums", [P, B])
        sq = sb("squeezed", [P, B])
        hid = sb("squeeze_hidden", [RED, B])
        exc = sb("excite", [P, B])
        gain = sb("gain", [P, B])
        bn = sb("bn_scale", [P, 4])
        route = Router(k, 0, ctx, lambda b: energy[:, b, :], lambda b: (s["mix_used"], s["mix_used"].base + b + 1),
                       room=w[:, 8192:10024])

        @block.sync
        def _(sp):
            load_columns(sp, s["mix_loaded"], vec, [i["L0_conv_b2"], i["L0_conv_gamma"], i["L0_conv_beta"],
                                                    i["L0_conv_moving_mean"], i["L0_conv_moving_var"]])
            sp.dma_start(w1[:], i["L0_conv_w1"]).then_inc(s["mix_loaded"].h, 16)
            sp.dma_start(w2[:], i["L0_conv_w2"]).then_inc(s["mix_loaded"].h, 16)
            sp.dma_start(b1[:], i["L0_conv_b1"].rearrange("(c a) -> c a", a=1)).then_inc(s["mix_loaded"].h, 16)
            sp.wait_ge(*when("mix_loaded", 16 * 8))
            sp.wait_ge(*when("mix_logs", B))
            route.load_gate(sp)
            route.load_weights(sp)

        BOX = 10

        @block.vector
        def _(dve):
            ch = Chain(dve, s["mix_v"], s["mix_v"].base)
            ch.note(dve.memset(pad, 0.0))
            ch.note(dve.tensor_reduce(rng[:, 0, :], xch, AX.X, ALU.max))
            ch.link(dve.tensor_reduce(rng[:, 1, :], xch, AX.X, ALU.min))
            dve.tensor_scalar(rng[:, 1, :], rng[:, 1, :], -1.0, None, ALU.mult).then_inc(s["mix_range"].h, 1)
            dve.wait_ge(*when("mix_allmax", 1))
            ch.link(dve.tensor_tensor(inv[:], rngall[:, 0, :], rngall[:, 1, :], ALU.add))
            ch.link(dve.tensor_scalar(inv[:], inv[:], 1e-7, None, ALU.add))
            ch.link(dve.reciprocal(inv[:], inv[:]))
            ch.link(dve.tensor_scalar(lowest[:], rngall[:, 1, :], -1.0, None, ALU.mult))
            pre = k.fractal_pre = ch.n

            def boxes(b, u):
                ch = Chain(dve, s["mix_v"], s["mix_v"].base + pre + b * BOX)
                one = bass.ds(b, 1)
                src = xch[:, one, :].rearrange("p a (h w) -> p (a h) w", w=WW)
                ch.link(dve.tensor_scalar(pad[:, 7:39, 7:39], src, lowest[:, one], inv[:, one], ALU.subtract, ALU.mult))
                if past(b, 1):
                    dve.wait_ge(*when("mix_logs", b))

                def double(out, src, rows, cols, shift):
                    t = tmp[:, 0:rows * (cols - shift)].rearrange("p (h w) -> p h w", h=rows)
                    ch.link(dve.tensor_tensor(t, src[:, :, 0:cols - shift], src[:, :, shift:cols], ALU.add))
                    ins = dve.tensor_tensor(out, t[:, 0:rows - shift, :], t[:, shift:rows, :], ALU.add)
                    ch.link(ins)

                double(s2, pad, 47, 47, 1)
                double(s4, s2, 46, 46, 2)
                double(s8, s4, 44, 44, 4)
                if past(b, 1):
                    dve.wait_ge(*when("mix_pool", 5 * b))
                double(s16, s8, 40, 40, 8)
                dve.wait_ge(*when("mix_pool", b * 5 + 2))
                ch.link(dve.scalar_tensor_tensor(out=slope[:, one, :].rearrange("p a n -> p (a n)"), in0=con[0],
                                                 scalar=3.0, in1=con[1], op0=ALU.mult, op1=ALU.add,
                                                 accum_out=sums[:, one]))
            spelled_out(B, 1, boxes)

            ch = Chain(dve, s["mix_prep"], s["mix_prep"].base)
            dve.wait_ge(*when("mix_v", pre + B * BOX))
            dve.wait_ge(*when("mix_loaded", 16 * 8))
            ch.note(dve.tensor_scalar(sq[:], sums[:], slope_scale / IMG, None, ALU.mult))
            dve.wait_ge(s["mix_prep"].h, s["mix_prep"].base + 1)
            dve.wait_ge(*when("mix_sq1", 1))
            ch.link(dve.reciprocal(bn[:, 1:2], bn[:, 0:1]))
            ch.link(dve.tensor_tensor(bn[:, 1:2], bn[:, 1:2], vec[:, 1:2], ALU.mult))
            ch.link(dve.tensor_tensor(bn[:, 2:3], bn[:, 1:2], vec[:, 3:4], ALU.mult))
            ch.link(dve.tensor_tensor(bn[:, 2:3], vec[:, 2:3], bn[:, 2:3], ALU.subtract))
            ch.link(dve.tensor_scalar(bn[:, 3:4], bn[:, 1:2], slope_scale, None, ALU.mult))
            dve.wait_ge(*when("mix_excite", 2))
            ch.link(dve.tensor_tensor(gain[:], inv[:], exc[:], ALU.mult))

            def blend(b, u):
                one = bass.ds(b, 1)
                at = energy[:, one, :].rearrange("p a n -> p (a n)")
                dve.wait_ge(*when("mix_root", 2 * (b + 1)))
                c2 = Chain(dve, s["mix_sim"], s["mix_sim"].base + b * 6)
                c2.link(dve.tensor_scalar(logs[:, 0, :], at, 1e-7, None, ALU.add))
                if b:
                    route.add(dve, b - 1)
                c2.link(dve.reciprocal(logs[:, 0, :], logs[:, 0, :]))
                if b:
                    route.norm(dve, b - 1)
                c2.note(dve.tensor_tensor(logs[:, 0, :], con[2], logs[:, 0, :], ALU.mult))
                c2.link(dve.tensor_scalar(logs[:, 1, :], xch[:, b, :], lowest[:, one], gain[:, one],
                                          ALU.subtract, ALU.mult))
                if b:
                    route.choose(dve, b - 1)
                dve.wait_ge(*when("mix_sig", b + 1))
                c2.link(dve.tensor_tensor(logs[:, 2, :], logs[:, 1, :], con[0], ALU.subtract))
                c2.link(dve.tensor_tensor(logs[:, 3, :], logs[:, 0, :], logs[:, 2, :], ALU.mult))
                if b:
                    route.place(dve, b - 1)
                dve.tensor_tensor(at, logs[:, 1, :], logs[:, 3, :], ALU.subtract).then_inc(s["mix_used"].h, 1)
            route.reset(dve)
            spelled_out(B, 1, blend)
            route.finish_vector(dve)

        @block.gpsimd
        def _(pool):
            pool.wait_ge(*when("mix_range", 1))
            pool.partition_all_reduce(rngall[:].rearrange("p a b -> p (a b)"), rng[:].rearrange("p a b -> p (a b)"), P,
                                      bass.bass_isa.ReduceOp.max).then_inc(s["mix_allmax"].h, 1)

            def contrasts(b, u):
                ch = Chain(pool, s["mix_pool"], s["mix_pool"].base + b * 5)
                pool.wait_ge(*when("mix_logs", b + 1))
                if past(b, 1):
                    pool.wait_ge(*when("mix_squares", 4 * b))
                L = [logs[:, j, :] for j in range(4)]
                ch.note(pool.tensor_tensor(con[0], L[3], L[0], ALU.subtract))
                ch.note(pool.tensor_tensor(con[1], L[2], L[1], ALU.subtract))
                ch.note(pool.tensor_tensor(L[3], L[3], L[0], ALU.add))
                ch.note(pool.tensor_tensor(L[2], L[2], L[1], ALU.add))
                ch.settle()
                ch.note(pool.tensor_tensor(con[2], L[3], L[2], ALU.subtract))
                at = energy[:, bass.ds(b, 1), :].rearrange("p a n -> p (a n)")
                c2 = Chain(pool, s["mix_energy"], s["mix_energy"].base + b * 3)
                pool.wait_ge(*when("mix_squares", 4 * (b + 1)))
                c2.link(pool.tensor_tensor(con[0], con[0], con[1], ALU.add))
                c2.link(pool.tensor_tensor(con[0], con[0], con[2], ALU.add))
                c2.link(pool.tensor_tensor(at, con[0], at, ALU.mult))
            spelled_out(B, 1, contrasts)
            route.send_all(pool)

        @block.scalar
        def _(act):
            def logs_of(b, u):
                one = bass.ds(b, 1)
                act.wait_ge(s["mix_v"].h, s["mix_v"].base + k.fractal_pre + b * BOX + BOX - 1)
                if past(b, 1):
                    act.wait_ge(*when("mix_pool", 5 * b))
                for j, view in enumerate((s2[:, 7:39, 7:39], s4[:, 6:38, 6:38], s8[:, 4:36, 4:36], s16)):
                    ins = act.activation(logs[:, j, :].rearrange("p (h w) -> p h w", w=WW), view, ACT.Ln, bias=k.eps7)
                ins.then_inc(s["mix_logs"].h, 1)
                act.wait_ge(*when("mix_pool", 5 * (b + 1)))
                act.wait_ge(s["mix_v"].h, s["mix_v"].base + k.fractal_pre + (b + 1) * BOX)
                for j, scale in ((0, 0.5 ** 0.5), (1, 0.5 ** 0.5), (2, 0.5)):
                    act.activation(con[j], con[j], ACT.Square, scale=scale).then_inc(s["mix_squares"].h, 1)
                act.activation(energy[:, one, :].rearrange("p a n -> p (a n)"), slope[:, one, :].rearrange("p a n -> p (a n)"), ACT.Square,
                               scale=norm_scale).then_inc(s["mix_squares"].h, 1)
            spelled_out(B, 1, logs_of)
            act.wait_ge(*when("mix_loaded", 16 * 8))
            act.activation(bn[:, 0:1], vec[:, 4:5], ACT.Sqrt, bias=k.eps3).then_inc(s["mix_sq1"].h, 1)
            act.wait_ge(*when("mix_mm", 1))
            act.activation(hid[:], k.ps[0:RED, 0, 0:B], ACT.Relu, bias=b1[:]).then_inc(s["mix_excite"].h, 1)
            act.wait_ge(*when("mix_mm", 2))
            act.activation(exc[:], k.ps[:, 1, 0:B], ACT.Sigmoid, bias=vec[:, 0:1]).then_inc(s["mix_excite"].h, 1)
            act.wait_ge(*when("mix_energy", 3 * B))
            act.wait_ge(*when("mix_prep", 6))

            def roots(b, u):
                one = bass.ds(b, 1)
                at = energy[:, one, :].rearrange("p a n -> p (a n)")
                sl = slope[:, one, :].rearrange("p a n -> p (a n)")
                if past(b, 1):
                    act.wait_ge(*when("mix_used", b))
                act.activation(at, at, ACT.Sqrt).then_inc(s["mix_root"].h, 1)
                act.activation(con[2], sl, ACT.Square, scale=norm_scale).then_inc(s["mix_root"].h, 1)
                if b:
                    route.root(act, b - 1)
                act.activation(con[0], sl, ACT.Sigmoid, scale=bn[:, 3:4], bias=bn[:, 2:3]).then_inc(s["mix_sig"].h, 1)
                if b:
                    route.keep_rows(act, b - 1)
                    route.exp(act, b - 1)
            spelled_out(B, 1, roots)
            route.finish_scalar(act)

        @block.tensor
        def _(pe):
            pe.wait_ge(*when("mix_loaded", 16 * 8))
            pe.wait_ge(*when("mix_prep", 1))
            pe.matmul(k.ps[0:RED, 0, 0:B], w1[:], sq[:], start=True, stop=True).then_inc(s["mix_mm"].h, 1)
            pe.wait_ge(*when("mix_excite", 1))
            pe.matmul(k.ps[:, 1, 0:B], w2[:], hid[:], start=True, stop=True).then_inc(s["mix_mm"].h, 1)
            for b in range(B - 1):
                route.turn_back(pe, b)
                route.turn_rows(pe, b)
                route.gate(pe, b)
                route.rank(pe, b)
            route.finish_tensor(pe)
    route.done()


def mixer_involution(k):
    nc, i = k.nc, k.ins
    RED = i["L1_conv_W1"].shape[1]
    TAPS = 9
    GROUPS = i["L1_conv_W2"].shape[1] // TAPS
    GC = C // GROUPS
    PER = 2 * TAPS
    names = ("inv_loaded", "inv_prep", "inv_bias", "inv_ones", "inv_hidden", "inv_biased", "inv_kernel", "inv_product",
             "inv_sum", "inv_stored")
    s = {n: k.sem(n) for n in names}
    loads = 16 * (4 * 2 + 2)

    def when(name, n):
        return s[name].h, s[name].base + n

    ch4 = k.ch[:].rearrange("p (b h w) -> p b h w", b=B, h=34)
    with ExitStack() as ctx, nc.Block() as block:
        def sb(name, shape, dt=F32):
            return ctx.enter_context(nc.sbuf_tensor(name, shape, dt))

        tail = slice(7 * TPB * ROW, 7 * TPB * ROW + 2 * BANK)
        hid = k.flat(k.rows0)[:, tail].rearrange("p (a n) -> p a n", a=2)
        prods = [k.flat(k.rows1)[:, tail][:, 0:BANK], k.flat(k.rows1)[:, tail][:, BANK:2 * BANK]]
        used = 2 * FFN[1]["E"] * FFN[1]["F"]
        w2x = k.wts[:, used:used + TAPS * C]
        gather = k.wts[:, used + TAPS * C:used + 2 * TAPS * C].rearrange("p (t c) -> p t c", t=TAPS)
        left = used + 2 * TAPS * C
        mixed_first = k.wts[:, left:left + IMG]
        prods.append(k.wts[:, left + IMG:left + IMG + BANK])
        bias_row = k.flat(k.rows1)[0:1, 0:TAPS * C]

        def mixed(b):
            return mixed_first if b == 0 else k.ch[:, (b - 1) * 34 * 34:(b - 1) * 34 * 34 + IMG]

        route = Router(k, 1, ctx, mixed, lambda b: (s["inv_stored"], s["inv_stored"].base + 2 * (b + 1)))
        w1 = sb("reduce_w", [P, RED])
        w1r = sb("reduce_w_four_times", [P, 4, RED])
        w2 = sb("span_w", [P, GROUPS * TAPS])
        b2row = sb("span_b_row", [1, GROUPS * TAPS])
        b1 = sb("reduce_b", [P, 1])
        b2 = sb("span_b", [P, TAPS])

        @block.sync
        def _(sp):
            for g in range(4):
                rows = slice(RED * g, RED * (g + 1))
                sp.dma_start(w2[rows, :], i["L1_conv_W2"]).then_inc(s["inv_loaded"].h, 16)
                sp.dma_start(b1[rows, :], i["L1_conv_b1"].rearrange("(c a) -> c a", a=1)).then_inc(s["inv_loaded"].h, 16)
            sp.dma_start(w1[:], i["L1_conv_W1"]).then_inc(s["inv_loaded"].h, 16)
            sp.dma_start(b2row[:], i["L1_conv_b2"].rearrange("(a c) -> a c", a=1)).then_inc(s["inv_loaded"].h, 16)
            sp.wait_ge(*when("inv_loaded", loads))
            route.load_gate(sp)
            route.load_weights(sp)

        def window(b, half, dy, dx):
            return ch4[:, bass.ds(b, 1), 16 * half + dy:16 * half + dy + 16, dx:dx + WW].rearrange("p a h w -> p (a h) w")

        @block.gpsimd
        def _(pool):
            pool.memset(gather, 1.0).then_inc(s["inv_ones"].h, 1)
            pool.wait_ge(*when("inv_ones", 1))
            pool.affine_select(out=gather, in_=gather, compare_op=ALU.is_ge, fill=0.0, base=0,
                               pattern=[[P, TAPS], [-TAPS, C]], channel_multiplier=1).then_inc(s["inv_ones"].h, 1)
            pool.wait_ge(*when("inv_ones", 2))
            pool.affine_select(out=gather, in_=gather, compare_op=ALU.is_ge, fill=0.0, base=TAPS - 1,
                               pattern=[[-P, TAPS], [TAPS, C]], channel_multiplier=-1).then_inc(s["inv_ones"].h, 1)
            route.send_all(pool)

        @block.tensor
        def _(pe):
            pe.wait_ge(*when("inv_prep", 3))
            for tap in range(TAPS):
                ins = pe.matmul(k.ps[:, 0, tap:tap + 1], bias_row[:, tap * P:(tap + 1) * P], k.ident[0:1, 0:1],
                                start=True, stop=True)
            ins.then_inc(s["inv_bias"].h, 1)
            pe.wait_ge(*when("inv_ones", 3))
            pe.wait_ge(*when("inv_prep", 4))

            def hidden(b, half):
                if 2 * b + half:
                    pe.wait_ge(*when("inv_biased", 2 * b + half))
                pe.matmul(k.ps[:, 0, :].rearrange("p (h w) -> p h w", w=WW), w1r[:].rearrange("p a r -> p (a r)"),
                          window(b, half, 1, 1), start=True, stop=True).then_inc(s["inv_hidden"].h, 1)

            def kernel_entries(b, n):
                half, tap = n // TAPS, n % TAPS
                if tap == 0:
                    pe.wait_ge(*when("inv_biased", 2 * b + half + 1))
                if b * PER + n >= 3:
                    pe.wait_ge(*when("inv_product", b * PER + n - 2))
                rows = slice(RED * (tap % 4), RED * (tap % 4 + 1))
                pe.matmul(k.ps[:, 1 + n % 3, :], w2x[rows, tap * P:(tap + 1) * P], hid[rows, half, :],
                          start=True, stop=True).then_inc(s["inv_kernel"].h, 1)

            def add_up(b, n):
                half, tap = n // TAPS, n % TAPS
                if tap == 0 and b:
                    pe.wait_ge(*when("inv_stored", 2 * b + half - 1))
                pe.wait_ge(*when("inv_product", b * PER + n + 1))
                pe.matmul(k.ps[:, 4 + half, :], gather[:, tap, :], prods[n % 3], start=(tap == 0),
                          stop=(tap == TAPS - 1)).then_inc(s["inv_sum"].h, 1)

            hidden(0, 0)
            for b in range(B):
                for n in range(PER):
                    if n == 5:
                        hidden(b, 1)
                    if n == 14 and b + 1 < B:
                        hidden(b + 1, 0)
                    kernel_entries(b, n)
                    if n >= 2:
                        add_up(b, n - 2)
                    route.tensor_between(pe, b, n, PER)
                add_up(b, PER - 2)
                add_up(b, PER - 1)
            route.finish_tensor(pe)

        @block.scalar
        def _(act):
            act.wait_ge(*when("inv_loaded", loads))

            def bias(b, half):
                act.wait_ge(*when("inv_hidden", 2 * b + half + 1))
                if b:
                    act.wait_ge(*when("inv_kernel", (b - 1) * PER + (half + 1) * TAPS))
                act.activation(hid[:, half, :], k.ps[:, 0, :], ACT.Identity, bias=b1[:]).then_inc(s["inv_biased"].h, 1)

            def store(b, half):
                act.wait_ge(*when("inv_sum", b * PER + (half + 1) * TAPS))
                act.activation(mixed(b)[:, half * BANK:(half + 1) * BANK], k.ps[:, 4 + half, :],
                               ACT.Copy).then_inc(s["inv_stored"].h, 1)

            bias(0, 0)
            for b in range(B):
                if b:
                    route.root(act, b - 1)
                bias(b, 1)
                if b:
                    route.keep_rows(act, b - 1)
                store(b, 0)
                if b:
                    route.exp(act, b - 1)
                if b + 1 < B:
                    bias(b + 1, 0)
                store(b, 1)
            route.finish_scalar(act)

        @block.vector
        def _(dve):
            dve.wait_ge(*when("inv_loaded", loads))
            dve.tensor_copy(w1r[:], w1[:].unsqueeze(1).to_broadcast([P, 4, RED])).then_inc(s["inv_prep"].h, 1)
            for p, dst, src in ((P, w2x, w2[:]), (1, bias_row, b2row[:])):
                for g in range(GROUPS):
                    ins = dve.tensor_copy(
                        dst[:, g * GC * TAPS:(g + 1) * GC * TAPS].rearrange("p (c t) -> p c t", t=TAPS),
                        src[:, g * TAPS:(g + 1) * TAPS].unsqueeze(1).to_broadcast([p, GC, TAPS]))
                ins.then_inc(s["inv_prep"].h, 1)
            dve.wait_ge(*when("inv_bias", 1))
            dve.tensor_copy(b2[:], k.ps[:, 0, 0:TAPS]).then_inc(s["inv_prep"].h, 1)
            dve.wait_ge(*when("inv_prep", 4))

            route.reset(dve)
            for b in range(B):
                for n in range(PER):
                    half, tap = n // TAPS, n % TAPS
                    dve.wait_ge(*when("inv_kernel", b * PER + n + 1))
                    if b * PER + n >= 3:
                        dve.wait_ge(*when("inv_sum", b * PER + n - 2))
                    dve.scalar_tensor_tensor(
                        out=prods[n % 3].rearrange("p (h w) -> p h w", w=WW),
                        in0=k.ps[:, 1 + n % 3, :].rearrange("p (h w) -> p h w", w=WW), scalar=b2[:, tap:tap + 1],
                        in1=window(b, half, tap // 3, tap % 3), op0=ALU.add, op1=ALU.mult).then_inc(s["inv_product"].h, 1)
                    route.vector_between(dve, b, n, PER)
            route.finish_vector(dve)
    route.done()


def mixer_spline(k):
    nc, i = k.nc, k.ins
    KN = i["L2_conv_spline_weight"].shape[2]
    knots = [float(v) for v in np.linspace(-1.0, 1.0, KN, dtype=np.float32)]
    CHUNKS = N // BANK
    names = ("spl_loaded", "spl_v", "spl_scaled", "spl_wturned", "spl_wcopied", "spl_root", "spl_abs", "spl_basis",
             "spl_base", "spl_basis_used", "spl_silu", "spl_bn", "spl_out", "spl_range")
    s = {n: k.sem(n) for n in names}

    def when(name, n):
        return s[name].h, s[name].base + n

    with ExitStack() as ctx, nc.Block() as block:
        def sb(name, shape, dt=F32):
            return ctx.enter_context(nc.sbuf_tensor(name, shape, dt))

        base_w = sb("base_w", [P, C])
        spw = sb("spline_w", [P, C, KN])
        scl = sb("spline_scaler", [P, C])
        spt = sb("spline_w_turned", [P, KN, C])
        vec = sb("spline_vectors", [P, 8])
        bn = sb("spline_bn", [P, 2, 4])
        rng = sb("channel_range", [P, 3])
        used = 2 * FFN[2]["E"] * FFN[2]["F"]
        room = k.wts[:, used:used + 10 * BANK].rearrange("p (a n) -> p a n", n=BANK)
        xu, dist, hat, silu = (room[:, a:b, :] for a, b in ((0, 2), (2, 5), (5, 8), (8, 10)))
        kn = sb("minus_knots", [P, KN])
        route = Router(k, 2, ctx, lambda b: k.ch[:, b * IMG:(b + 1) * IMG],
                       lambda b: (s["spl_bn"], s["spl_bn"].base + 2 * (b + 1)))

        @block.sync
        def _(sp):
            load_columns(sp, s["spl_loaded"], vec, [i[f"L2_conv_bn_{a}_{b}"] for a in ("base", "spline")
                                                    for b in ("gamma", "beta", "mean", "var")])
            sp.dma_start(base_w[:], i["L2_conv_base_weight"]).then_inc(s["spl_loaded"].h, 16)
            sp.dma_start(spw[:], i["L2_conv_spline_weight"]).then_inc(s["spl_loaded"].h, 16)
            sp.dma_start(scl[:], i["L2_conv_spline_scaler"]).then_inc(s["spl_loaded"].h, 16)
            sp.wait_ge(*when("spl_loaded", 16 * 11))
            route.load_gate(sp)
            route.load_weights(sp)

        @block.gpsimd
        def _(pool):
            route.send_all(pool)

        @block.vector
        def _(dve):
            ch = Chain(dve, s["spl_v"], s["spl_v"].base)
            for j, v in enumerate(knots):
                ins = dve.memset(kn[:, j:j + 1], -v)
            ins.then_inc(s["spl_range"].h, 1)
            dve.wait_ge(*when("spl_loaded", 16 * 11))
            dve.tensor_tensor(spw[:], spw[:], scl[:].unsqueeze(2).to_broadcast([P, C, KN]),
                              ALU.mult).then_inc(s["spl_scaled"].h, 1)
            ch.note(dve.tensor_reduce(rng[:, 0:1], k.ch[:, 0:N], AX.X, ALU.min))
            ch.link(dve.tensor_reduce(rng[:, 1:2], k.ch[:, 0:N], AX.X, ALU.max))
            ch.link(dve.tensor_tensor(rng[:, 1:2], rng[:, 1:2], rng[:, 0:1], ALU.subtract))
            ch.link(dve.tensor_scalar(rng[:, 1:2], rng[:, 1:2], 1e-7, None, ALU.add))
            ch.link(dve.reciprocal(rng[:, 2:3], rng[:, 1:2]))
            dve.wait_ge(*when("spl_root", 2))
            for j in range(2):
                g, bt, mn = (vec[:, 4 * j + a:4 * j + a + 1] for a in range(3))
                ch.link(dve.reciprocal(bn[:, j, 1:2], bn[:, j, 0:1]))
                ch.link(dve.tensor_tensor(bn[:, j, 1:2], bn[:, j, 1:2], g, ALU.mult))
                ch.link(dve.tensor_tensor(bn[:, j, 2:3], bn[:, j, 1:2], mn, ALU.mult))
                ch.link(dve.tensor_tensor(bn[:, j, 2:3], bt, bn[:, j, 2:3], ALU.subtract))
                ch.link(dve.tensor_scalar(bn[:, j, 3:4], bn[:, j, 1:2], -1.0, None, ALU.mult))

            k.spline_pre = ch.n

            def chunk(c, u):
                if past(c, 2):
                    dve.wait_ge(*when("spl_abs", KN * (c - 1)))
                dve.tensor_scalar(xu[:, u, :], k.ch[:, bass.ds(c * BANK, BANK)], rng[:, 0:1], rng[:, 2:3],
                                  ALU.subtract, ALU.mult).then_inc(s["spl_v"].h, 1)
                for j in range(KN):
                    dve.wait_ge(*when("spl_abs", c * KN + j + 1))
                    if past(c, 1) or j >= 3:
                        dve.wait_ge(*when("spl_basis_used", c * KN + j - 2))
                    dve.tensor_scalar(hat[:, j % 3, :], dist[:, j % 3, :], 1.0, 1.0, ALU.min,
                                      ALU.subtract).then_inc(s["spl_basis"].h, 1)
                    route.vector_between(dve, c // 2, u * KN + j, 2 * KN)
                dve.wait_ge(*when("spl_basis_used", (c + 1) * KN))
                dve.wait_ge(*when("spl_silu", 2 * (c + 1)))
                dve.scalar_tensor_tensor(out=k.ch[:, bass.ds(c * BANK, BANK)], in0=k.ps[:, 2 + u, :],
                                         scalar=bn[:, 1, 3:4], in1=silu[:, u, :], op0=ALU.mult,
                                         op1=ALU.add).then_inc(s["spl_bn"].h, 1)
            route.reset(dve)
            spelled_out(CHUNKS, 2, chunk)
            route.finish_vector(dve)

        @block.scalar
        def _(act):
            act.wait_ge(*when("spl_loaded", 16 * 11))
            for j in range(2):
                act.activation(bn[:, j, 0:1], vec[:, 4 * j + 3:4 * j + 4], ACT.Sqrt, bias=k.eps3).then_inc(s["spl_root"].h, 1)
            for t in range(KN):
                act.wait_ge(*when("spl_wturned", t + 1))
                act.activation(spt[:, t, :], k.ps[:, 4 + t % 2, 0:P], ACT.Copy).then_inc(s["spl_wcopied"].h, 1)
            act.wait_ge(*when("spl_range", 1))

            def chunk(c, u):
                act.wait_ge(s["spl_v"].h, s["spl_v"].base + k.spline_pre + c + 1)
                for j in range(KN):
                    if past(c, 1) or j >= 3:
                        act.wait_ge(*when("spl_basis", c * KN + j - 2))
                    act.activation(dist[:, j % 3, :], xu[:, u, :], ACT.Abs, bias=kn[:, j:j + 1]).then_inc(s["spl_abs"].h, 1)
                    route.scalar_between(act, c // 2, u * KN + j, 2 * KN)
                act.wait_ge(*when("spl_base", c + 1))
                if past(c, 2):
                    act.wait_ge(*when("spl_bn", c - 1))
                act.activation(silu[:, u, :], k.ps[:, u, :], ACT.Silu, scale=bn[:, 0, 1:2],
                               bias=bn[:, 0, 2:3]).then_inc(s["spl_silu"].h, 1)
                act.wait_ge(*when("spl_silu", 2 * c + 1))
                act.activation(silu[:, u, :], silu[:, u, :], ACT.Identity, bias=bn[:, 1, 2:3]).then_inc(s["spl_silu"].h, 1)
            spelled_out(CHUNKS, 2, chunk)
            route.finish_scalar(act)

        @block.tensor
        def _(pe):
            pe.wait_ge(*when("spl_scaled", 1))
            for t in range(KN):
                if t >= 2:
                    pe.wait_ge(*when("spl_wcopied", t - 1))
                pe.transpose(k.ps[:, 4 + t % 2, 0:P], spw[:, :, t], k.ident[:]).then_inc(s["spl_wturned"].h, 1)
            pe.wait_ge(*when("spl_wcopied", KN))

            def chunk(c, u):
                if past(c, 2):
                    pe.wait_ge(*when("spl_silu", 2 * (c - 1)))
                pe.matmul(k.ps[:, u, :], base_w[:], k.ch[:, bass.ds(c * BANK, BANK)], start=True,
                          stop=True).then_inc(s["spl_base"].h, 1)
                if past(c, 2):
                    pe.wait_ge(*when("spl_bn", c - 1))
                for j in range(KN):
                    pe.wait_ge(*when("spl_basis", c * KN + j + 1))
                    ins = pe.matmul(k.ps[:, 2 + u, :], spt[:, j, :], hat[:, j % 3, :], start=(j == 0), stop=(j == KN - 1))
                    ins.then_inc(s["spl_basis_used"].h, 1)
                    route.tensor_between(pe, c // 2, u * KN + j, 2 * KN)
            spelled_out(CHUNKS, 2, chunk)
            route.finish_tensor(pe)
    route.done()


def mixer_attention(k):
    nc, i = k.nc, k.ins
    names = ("att_loaded", "att_sq", "att_norm", "att_root", "att_unit", "att_turned", "att_copied", "att_value",
             "att_vcopied", "att_sim", "att_relu", "att_square", "att_y", "att_out", "att_xt")
    s = {n: k.sem(n) for n in names}

    def when(name, n):
        return s[name].h, s[name].base + n

    xft = k.ch[:, 0:N]
    with ExitStack() as ctx, nc.Block() as block:
        def sb(name, shape, dt=F32):
            return ctx.enter_context(nc.sbuf_tensor(name, shape, dt))

        w = sb("att_w", [P, C])
        ssq = sb("att_norms", [P, NT])
        val = k.flat(k.rows1).rearrange("p (b n) -> p b n", b=B)[:, :, 0:IMG]

        def mixed(b):
            at = (b - 1) * IMG if b else N
            return k.ch[:, at:at + IMG]

        route = Router(k, 3, ctx, mixed, lambda b: (s["att_out"], s["att_out"].base + 2 * (b + 1)))
        rel = sb("att_relu_buf", [P, 2, BANK])
        r2 = sb("att_weights", [P, 2, BANK])

        @block.sync
        def _(sp):
            sp.dma_start(w[:], i["L3_conv_W"]).then_inc(s["att_loaded"].h, 16)
            sp.wait_ge(*when("att_loaded", 16))
            route.load_gate(sp)
            route.load_weights(sp)

        @block.gpsimd
        def _(pool):
            route.send_all(pool)

        KEYS = TPB

        @block.scalar
        def _(act):
            def norms(t, u):
                one = bass.ds(t, 1)
                act.activation(k.mixed[:, bass.ds(t * P, P)], k.xn[:, one, :].rearrange("p a c -> p (a c)"), ACT.Square,
                               accum_out=ssq[:, one]).then_inc(s["att_sq"].h, 1)
            steps(act, NT, 2, norms)
            act.wait_ge(s["att_norm"].h, s["att_norm"].base + 1)
            act.activation(ssq[:], ssq[:], ACT.Sqrt).then_inc(s["att_root"].h, 1)

            def values(b, u):
                act.wait_ge(*when("att_value", b + 1))
                act.activation(val[:, b, :],
                               k.ps[:, 4 + 2 * u:6 + 2 * u, :].rearrange("p a n -> p (a n)"),
                               ACT.Copy).then_inc(s["att_vcopied"].h, 1)
                act.wait_ge(*when("att_turned", b + 1))
                act.activation(xft[:, bass.ds(b * IMG, IMG)], k.ps[:, 2 * u:2 * u + 2, :].rearrange("p a n -> p (a n)"),
                               ACT.Copy).then_inc(s["att_copied"].h, 1)
            spelled_out(B, 2, values)

            def relus(b, u):
                for h in range(2):
                    for j in range(KEYS):
                        n = h * KEYS + j
                        act.wait_ge(*when("att_sim", b * 2 * KEYS + n + 1))
                        if past(b, 1) or n >= 2:
                            act.wait_ge(*when("att_square", b * 2 * KEYS + n - 1))
                        act.activation(rel[:, n % 2, :], k.ps[:, n % 4, :], ACT.Relu).then_inc(s["att_relu"].h, 1)
                        route.scalar_between(act, b, n, 2 * KEYS)
            spelled_out(B, 1, relus)
            route.finish_scalar(act)

        @block.vector
        def _(dve):
            dve.wait_ge(*when("att_sq", NT))
            dve.tensor_scalar(ssq[:], ssq[:], 1e-12, None, ALU.max).then_inc(s["att_norm"].h, 1)
            dve.wait_ge(*when("att_root", 1))
            dve.reciprocal(ssq[:], ssq[:]).then_inc(s["att_norm"].h, 1)
            dve.wait_ge(*when("att_norm", 2))

            def unit(b, u):
                for t in range(TPB):
                    one = bass.ds(b * TPB + t, 1)
                    v = k.xn[:, one, :].rearrange("p a c -> p (a c)")
                    ins = dve.tensor_scalar(v, v, ssq[:, one], None, ALU.mult)
                ins.then_inc(s["att_unit"].h, 1)
            steps(dve, B, 1, unit)

            def squares(b, u):
                for h in range(2):
                    for j in range(KEYS):
                        n = h * KEYS + j
                        dve.wait_ge(*when("att_relu", b * 2 * KEYS + n + 1))
                        if past(b, 1) or n >= 2:
                            dve.wait_ge(*when("att_y", b * 2 * KEYS + n - 1))
                        dve.tensor_tensor(r2[:, n % 2, :], rel[:, n % 2, :], rel[:, n % 2, :],
                                          ALU.mult).then_inc(s["att_square"].h, 1)
                        route.vector_between(dve, b, n, 2 * KEYS)
                    dve.wait_ge(*when("att_y", b * 2 * KEYS + (h + 1) * KEYS))
                    dve.tensor_copy(mixed(b)[:, h * BANK:(h + 1) * BANK], k.ps[:, 4 + h, :]).then_inc(s["att_out"].h, 1)
            route.reset(dve)
            spelled_out(B, 1, squares)
            route.finish_vector(dve)

        @block.tensor
        def _(pe):
            pe.wait_ge(*when("att_loaded", 16))

            def values(b, u):
                if past(b, 2):
                    pe.wait_ge(*when("att_copied", b - 1))
                for t in range(TPB):
                    bank, at = 4 + 2 * u + t // 4, (t % 4) * P
                    ins = pe.matmul(k.ps[:, bank, at:at + P], xft[:, bass.ds(b * IMG + t * P, P)], w[:],
                                    start=True, stop=True)
                ins.then_inc(s["att_value"].h, 1)
                pe.wait_ge(*when("att_unit", b + 1))
                for t in range(TPB):
                    bank, at = 2 * u + t // 4, (t % 4) * P
                    ins = pe.transpose(k.ps[:, bank, at:at + P],
                                       k.xn[:, bass.ds(b * TPB + t, 1), :].rearrange("p a c -> p (a c)"), k.ident[:])
                ins.then_inc(s["att_turned"].h, 1)
            spelled_out(B, 2, values)
            pe.wait_ge(*when("att_copied", B))

            def attend(b, u):
                def sim(n):
                    h, j = n // KEYS, n % KEYS
                    if past(b, 1) or n >= 4:
                        pe.wait_ge(*when("att_relu", b * 2 * KEYS + n - 3))
                    pe.matmul(k.ps[:, n % 4, :], xft[:, bass.ds(b * IMG + j * P, P)],
                              xft[:, bass.ds(b * IMG + h * BANK, BANK)], start=True, stop=True).then_inc(s["att_sim"].h, 1)

                def gather(n):
                    h, j = n // KEYS, n % KEYS
                    pe.wait_ge(*when("att_square", b * 2 * KEYS + n + 1))
                    if j == 0 and past(b, 1):
                        pe.wait_ge(*when("att_out", 2 * b + h - 1))
                    pe.matmul(k.ps[:, 4 + h, :], val[:, b, j * P:(j + 1) * P],
                              r2[:, n % 2, :], start=(j == 0), stop=(j == KEYS - 1)).then_inc(s["att_y"].h, 1)

                sim(0)
                sim(1)
                for n in range(2 * KEYS):
                    if n + 2 < 2 * KEYS:
                        sim(n + 2)
                    gather(n)
                    route.tensor_between(pe, b, n, 2 * KEYS)
            spelled_out(B, 1, attend)
            route.finish_tensor(pe)
    route.done()


def finish(k):
    nc = k.nc
    s_in, s_add, s_out = k.sem("last_rows"), k.sem("last_added"), k.sem("stored")
    src = k.returned[:].rearrange("(t p k) c -> p t (k c)", p=P, k=2)
    dst = k.out.rearrange("b h w c -> (b h w) c").rearrange("(t p) c -> p t c", p=P)
    with ExitStack() as ctx, nc.Block() as block:
        buf = [k.flat(k.rows0)[:, 0:4 * TPB * 2 * C].rearrange("p (b t c) -> p b t c", b=4, t=TPB),
               k.flat(k.rows1)[:, 0:4 * TPB * 2 * C].rearrange("p (b t c) -> p b t c", b=4, t=TPB)]
        s_each = [k.sem(f"last_rows{b}") for b in range(B)]

        @block.sync
        def _(sp):
            for b in range(B):
                sp.dma_start(buf[b // 4][:, b % 4], src[:, b * TPB:(b + 1) * TPB, :]).then_inc(s_each[b].h, 16)
            for b in range(B):
                sp.wait_ge(s_add.h, 2 * (b + 1))
                sp.dma_start(dst[:, b * TPB:(b + 1) * TPB, :], k.x[:, b * TPB:(b + 1) * TPB, :]).then_inc(s_out.h, 16)
            sp.wait_ge(s_out.h, 16 * B)

        @block.vector
        def _(dve):
            for b in range(B):
                dve.wait_ge(s_each[b].h, 16)
                xs = k.x[:, b * TPB:(b + 1) * TPB, :]
                for c in range(2):
                    dve.tensor_tensor(xs, xs, buf[b // 4][:, b % 4, :, c * C:(c + 1) * C], ALU.add).then_inc(s_add.h, 1)
                    dve.wait_ge(s_add.h, 2 * b + c + 1)


def build(nc, ins, out, upto=99):
    with ExitStack() as ctx:
        k = Core(nc, ctx, ins, out)
        constants(k)
        mixers = [mixer_fractal, mixer_involution, mixer_spline, mixer_attention]
        for layer in range(4):
            norm_mixer(k, layer)
            mixers[layer](k)
            experts(k, layer)
        finish(k)



NAMES = ["x",
         "L0_conv_w1", "L0_conv_b1", "L0_conv_w2", "L0_conv_b2", "L0_conv_gamma", "L0_conv_beta",
         "L0_conv_moving_mean", "L0_conv_moving_var",
         "L0_ffn_gate_w", "L0_ffn_gate_b", "L0_ffn_w1", "L0_ffn_b1", "L0_ffn_w2", "L0_ffn_b2",
         "L1_conv_W1", "L1_conv_b1", "L1_conv_W2", "L1_conv_b2",
         "L1_ffn_Wg", "L1_ffn_bg", "L1_ffn_W1", "L1_ffn_b1", "L1_ffn_W2", "L1_ffn_b2",
         "L2_conv_base_weight", "L2_conv_spline_weight", "L2_conv_spline_scaler",
         "L2_conv_bn_base_gamma", "L2_conv_bn_base_beta", "L2_conv_bn_base_mean", "L2_conv_bn_base_var",
         "L2_conv_bn_spline_gamma", "L2_conv_bn_spline_beta", "L2_conv_bn_spline_mean", "L2_conv_bn_spline_var",
         "L2_ffn_gate_w", "L2_ffn_gate_b", "L2_ffn_W1", "L2_ffn_b1", "L2_ffn_W2", "L2_ffn_b2",
         "L3_conv_W", "L3_ffn_gate_w", "L3_ffn_gate_b", "L3_ffn_w1", "L3_ffn_w2", "L3_ffn_w3"]


def kernel(**inputs):
    import concourse.bacc as bacc
    from concourse.bass_utils import run_bass_kernel_spmd

    nc = bacc.Bacc("TRN2", target_bir_lowering=False, num_devices=1)
    arrays, ins = {}, {}
    for name in NAMES:
        a = np.ascontiguousarray(inputs[name])
        arrays[f"in_{name}"] = a
        ins[name] = nc.dram_tensor(f"in_{name}", a.shape, F32, kind="ExternalInput").ap()
    out = nc.dram_tensor("out", (B, HH, WW, C), F32, kind="ExternalOutput").ap()
    build(nc, ins, out)
    r = run_bass_kernel_spmd(nc, [arrays], core_ids=[0])
    return r.results[0]["out"]
```

```python
from contextlib import ExitStack

import numpy as np

import concourse.bass as bass
from concourse import mybir

ALU = mybir.AluOpType
ACT = mybir.ActivationFunctionType
AX = mybir.AxisListType
F32 = mybir.dt.float32
BF16 = mybir.dt.bfloat16
I32 = mybir.dt.int32

P = 128
C = 128
B, HH, WW = 8, 32, 32
IMG = HH * WW
N = B * IMG
NT = N // P
TPB = IMG // P
BANK = 512
ROW = C + 2
REGION = N + P
NOWHERE = 1 << 20
EMAX = 16
LN2 = float(np.log(2.0))

FFN = [
    dict(E=8, F=512, K=1, over_chosen=False, act=ACT.Relu, gated=False, capacity=1280, guard=True),
    dict(E=8, F=512, K=2, over_chosen=True, act=ACT.Gelu, gated=False, capacity=None, guard=False),
    dict(E=8, F=256, K=2, over_chosen=False, act=ACT.Gelu, gated=False, capacity=None, guard=False),
    dict(E=16, F=256, K=2, over_chosen=True, act=ACT.Silu, gated=True, capacity=None, guard=False),
]


class Sem:

    def __init__(self, handle):
        self.h = handle
        self.base = 0


class Chain:

    def __init__(self, eng, sem, before):
        self.eng, self.sem, self.before, self.n = eng, sem, before, 0

    def note(self, ins):
        self.n += 1
        ins.then_inc(self.sem.h, 1)

    def settle(self):
        self.eng.wait_ge(self.sem.h, self.before + self.n)

    def link(self, ins):
        self.note(ins)
        self.settle()


def past(i, k):
    return not isinstance(i, int) or i >= k


def steps(eng, n, unroll, body):
    for u in range(unroll):
        body(u, u)
    if n // unroll > 1:
        with eng.Fori(1, n // unroll) as g:
            for u in range(unroll):
                body(g * unroll + u, u)
    for i in range(n // unroll * unroll, n):
        body(i, i % unroll)


def pipelined(eng, n, unroll, body):
    for u in range(unroll):
        body(u, u, False)
    with eng.Fori(1, n // unroll - 1) as g:
        for u in range(unroll):
            body(g * unroll + u, u, False)
    for i in range((n // unroll - 1) * unroll, n):
        body(i, i % unroll, i == n - 1)


def spelled_out(n, unroll, body):
    for i in range(n):
        body(i, i % unroll)


class Core:

    def __init__(self, nc, ctx, ins, out):
        self.nc, self.ctx, self.ins, self.out = nc, ctx, ins, out
        self.sems = {}

        def sb(name, shape, dt=F32):
            return ctx.enter_context(nc.sbuf_tensor(name, shape, dt))

        self.sb = sb
        self.x = sb("residual", [P, NT, C])
        self.ch = sb("channel_major", [P, B * 34 * 34])
        self.rows0 = sb("rows_first_choice", [P, NT, ROW])
        self.rows1 = sb("rows_second_choice", [P, NT, ROW])
        self.wts = sb("expert_weights", [P, 12288])
        self.ps = ctx.enter_context(nc.psum_tensor("psum", [P, 8, BANK], F32))
        self.xn = self.flat(self.rows0)[:, 0:N].rearrange("p (t c) -> p t c", c=C)
        self.mixed = self.flat(self.rows1)[:, 0:N]

        self.ident = sb("identity", [P, P])
        self.tri = sb("upper_triangle", [P, P], BF16)
        self.ones = sb("ones_square", [P, P], BF16)
        self.rank = sb("expert_rank", [P, EMAX])
        self.region = sb("region_start", [P, EMAX])
        self.partition = sb("partition_index", [P, 1])
        self.tile_no = sb("tile_number", [P, 144])
        self.token_id = sb("token_id", [P, NT, 2], I32)
        self.token_id1 = sb("token_id_one_choice", [P, NT], I32)
        self.pad_rows = sb("pad_rows", [P, ROW])
        self.zeros = sb("zeros", [P, C])
        self.eps = sb("epsilons", [P, 4])
        self.eps3, self.eps5, self.eps6, self.eps7 = (self.eps[:, j:j + 1] for j in range(4))
        self.stats = sb("bn_stats", [P, NT, 6])
        self.mean = sb("mean", [P, NT])
        self.var4 = sb("four_variances", [P, NT])
        self.rstd = sb("rstd", [P, NT])
        self.counts = sb("expert_counts", [P, EMAX])
        self.tile_expert = sb("tile_expert", [1, 144], I32)
        self.tile_row = sb("tile_row", [1, 144], I32)

        self.dispatched = nc.dram_tensor("dispatched", (EMAX * REGION + P, ROW), F32, kind="Internal").ap()
        self.returned = nc.dram_tensor("returned", (N * 2, C), F32, kind="Internal").ap()

    @staticmethod
    def flat(t):
        return t[:].rearrange("p t c -> p (t c)")

    def sem(self, name):
        if name not in self.sems:
            self.sems[name] = Sem(self.ctx.enter_context(self.nc.semaphore(name)))
        return self.sems[name]

    def advance(self, **counts):
        for name, n in counts.items():
            self.sems[name].base += n


def constants(k):
    nc = k.nc
    s_set = k.sem("const_set")
    s_made = k.sem("const_made")
    s_x = k.sem("x_loaded")
    x_dram = k.ins["x"].rearrange("b h w c -> (b h w) c").rearrange("(t p) c -> p t c", p=P)
    with ExitStack() as ctx, nc.Block() as block:
        int_rank = ctx.enter_context(nc.sbuf_tensor("int_rank", [P, EMAX], I32))
        int_region = ctx.enter_context(nc.sbuf_tensor("int_region", [P, EMAX], I32))
        int_part = ctx.enter_context(nc.sbuf_tensor("int_part", [P, 1], I32))
        int_tile = ctx.enter_context(nc.sbuf_tensor("int_tile", [P, 144], I32))

        @block.sync
        def _(sp):
            for b in range(B):
                sp.dma_start(k.x[:, b * TPB:(b + 1) * TPB, :], x_dram[:, b * TPB:(b + 1) * TPB, :]).then_inc(s_x.h, 16)
            sp.wait_ge(s_x.h, 16 * B)
            sp.wait_ge(s_made.h, 4)
            sp.dma_start(k.dispatched[EMAX * REGION:EMAX * REGION + P, :], k.pad_rows[:]).then_inc(s_x.h, 16)
            sp.dma_start(k.dispatched[8 * REGION:8 * REGION + P, :], k.pad_rows[:]).then_inc(s_x.h, 16)
            sp.wait_ge(s_x.h, 16 * (B + 2))

        @block.vector
        def _(dve):
            dve.memset(k.ident[:], 0.0).then_inc(s_set.h, 1)
            dve.memset(k.tri[:], 1.0).then_inc(s_set.h, 1)
            dve.memset(k.ones[:], 1.0).then_inc(s_set.h, 1)
            dve.memset(k.pad_rows[:], 0.0).then_inc(s_set.h, 1)
            dve.memset(k.zeros[:], 0.0).then_inc(s_set.h, 1)
            for j, value in enumerate((1e-3, 1e-5, 1e-6, 1e-7)):
                dve.memset(k.eps[:, j:j + 1], value)
            dve.wait_ge(s_made.h, 8)
            dve.tensor_copy(k.rank[:], int_rank[:])
            dve.tensor_copy(k.region[:], int_region[:])
            dve.tensor_copy(k.partition[:], int_part[:])
            dve.tensor_copy(k.tile_no[:], int_tile[:])

        @block.gpsimd
        def _(pool):
            pool.wait_ge(s_set.h, 4)
            pool.affine_select(out=k.ident[:], in_=k.ident[:], compare_op=ALU.not_equal, fill=1.0, base=0,
                               pattern=[[-1, P]], channel_multiplier=1).then_inc(s_made.h, 1)
            pool.affine_select(out=k.tri[:], in_=k.tri[:], compare_op=ALU.is_ge, fill=0.0, base=0,
                               pattern=[[1, P]], channel_multiplier=-1).then_inc(s_made.h, 1)
            pool.iota(k.pad_rows[:].bitcast(I32)[:, C:C + 1], pattern=[[0, 1]], base=NOWHERE,
                      channel_multiplier=0).then_inc(s_made.h, 1)
            pool.iota(int_rank[:], pattern=[[-1, EMAX]], base=EMAX, channel_multiplier=0).then_inc(s_made.h, 1)
            pool.iota(int_region[:], pattern=[[REGION, EMAX]], base=-1, channel_multiplier=0).then_inc(s_made.h, 1)
            pool.iota(int_part[:], pattern=[[0, 1]], base=0, channel_multiplier=1).then_inc(s_made.h, 1)
            pool.iota(int_tile[:], pattern=[[1, 144]], base=0, channel_multiplier=0).then_inc(s_made.h, 1)
            pool.iota(k.token_id[:], pattern=[[2 * P, NT], [1, 2]], base=0, channel_multiplier=2).then_inc(s_made.h, 1)
            pool.iota(k.token_id1[:], pattern=[[P, NT]], base=0, channel_multiplier=1)
    k.advance(const_set=5, const_made=8, x_loaded=16 * (B + 2))


STAT_OPS = 6


def finish_stats(dve, k, ch, tiles=slice(0, NT)):
    mean, var4, spare = k.mean[:, tiles], k.var4[:, tiles], k.rstd[:, tiles]

    def col(j):
        return k.stats[:, tiles, j]
    ch.note(dve.tensor_tensor(mean, col(1), col(4), ALU.add))
    ch.note(dve.tensor_tensor(var4, col(1), col(4), ALU.subtract))
    ch.note(dve.tensor_tensor(spare, col(2), col(5), ALU.add))
    ch.settle()
    ch.note(dve.tensor_scalar(mean, mean, 0.5, None, ALU.mult))
    ch.link(dve.tensor_tensor(var4, var4, var4, ALU.mult))
    ch.link(dve.scalar_tensor_tensor(out=var4, in0=spare, scalar=4.0 / C, in1=var4, op0=ALU.mult, op1=ALU.add))


def norm_mixer(k, layer):
    nc = k.nc
    choices = FFN[layer - 1]["K"] if layer else 0
    names = ("choices_added", "norm_step", "root_ready", "rstd_ready", "norm_most", "norm_rest",
             "turned", "turned_copied", "border_cleared")
    s = {n: k.sem(n) for n in names}
    s_back = [k.sem(f"rows_back{b}") for b in range(B)]
    padded = layer == 1
    per = min(choices, 1) + TPB
    ch4 = k.ch[:].rearrange("p (b h w) -> p b h w", b=B, h=34)

    def when(name, n):
        return s[name].h, s[name].base + n

    with ExitStack() as ctx, nc.Block() as block:
        if choices:
            size = TPB * choices * C
            rooms = [k.wts[:, j * size:(j + 1) * size] for j in range(B - 2)]
            rooms += [k.flat(k.rows1)[:, j * size:(j + 1) * size] for j in range(2)]
            back = [r.rearrange("p (t c) -> p t c", t=TPB) for r in rooms]
            src = k.returned[0:N * choices, :].rearrange("(t p k) c -> p t (k c)", p=P, k=choices)

            @block.sync
            def _(sp):
                for b in range(B):
                    sp.dma_start(back[b], src[:, b * TPB:(b + 1) * TPB, :]).then_inc(s_back[b].h, 16)

        if choices == 2:
            @block.gpsimd
            def _(pool):
                for b in range(B):
                    pool.wait_ge(s_back[b].h, s_back[b].base + 16)
                    pool.tensor_tensor(back[b][:, :, 0:C], back[b][:, :, 0:C], back[b][:, :, C:2 * C],
                                       ALU.add).then_inc(s["choices_added"].h, 1)

        @block.vector
        def _(dve):
            for b in range(B):
                ch = Chain(dve, s["norm_step"], s["norm_step"].base + b * per)
                tiles = slice(b * TPB, (b + 1) * TPB)
                if choices == 2:
                    dve.wait_ge(*when("choices_added", b + 1))
                elif choices:
                    dve.wait_ge(s_back[b].h, s_back[b].base + 16)
                if choices:
                    ch.link(dve.tensor_tensor(k.x[:, tiles, :], k.x[:, tiles, :], back[b][:, :, 0:C], ALU.add))
                for t in range(b * TPB, (b + 1) * TPB):
                    ch.note(dve.bn_stats(k.stats[:, t, :], k.x[:, t, :]))
            ch = Chain(dve, s["norm_step"], s["norm_step"].base + B * per)
            ch.settle()
            finish_stats(dve, k, ch)
            dve.wait_ge(*when("root_ready", 1))
            dve.reciprocal(k.rstd[:], k.rstd[:]).then_inc(s["rstd_ready"].h, 1)
            dve.wait_ge(*when("rstd_ready", 1))
            dve.scalar_tensor_tensor(out=k.var4[:], in0=k.mean[:], scalar=-1.0, in1=k.rstd[:], op0=ALU.mult,
                                     op1=ALU.mult).then_inc(s["rstd_ready"].h, 1)
            if padded:
                dve.memset(k.ch[:], 0.0).then_inc(s["border_cleared"].h, 1)
            for b in range(B):
                for t in (b * TPB + j for j in range(TPB) if j % 4 != 3):
                    ins = dve.tensor_scalar(k.xn[:, t, :], k.x[:, t, :], k.mean[:, t:t + 1], k.rstd[:, t:t + 1],
                                            ALU.subtract, ALU.mult)
                ins.then_inc(s["norm_most"].h, 1)

        @block.tensor
        def _(pe):
            for b in range(B):
                pe.wait_ge(*when("norm_most", b + 1))
                pe.wait_ge(*when("norm_rest", b + 1))
                if b >= 2:
                    pe.wait_ge(*when("turned_copied", b - 1))
                for t in range(TPB):
                    bank, at = 2 * (b % 2) + t // 4, (t % 4) * P
                    ins = pe.transpose(k.ps[:, bank, at:at + P], k.xn[:, b * TPB + t, :], k.ident[:])
                ins.then_inc(s["turned"].h, 1)

        @block.scalar
        def _(act):
            act.wait_ge(*when("norm_step", B * per + STAT_OPS))
            act.activation(k.rstd[:], k.var4[:], ACT.Sqrt, bias=k.eps6, scale=0.25).then_inc(s["root_ready"].h, 1)
            act.wait_ge(*when("rstd_ready", 2))
            if padded:
                act.wait_ge(*when("border_cleared", 1))

            def normalise(b):
                for t in range(b * TPB + 3, (b + 1) * TPB, 4):
                    ins = act.activation(k.xn[:, t, :], k.x[:, t, :], ACT.Identity, scale=k.rstd[:, t:t + 1],
                                         bias=k.var4[:, t:t + 1])
                ins.then_inc(s["norm_rest"].h, 1)

            def keep(b):
                act.wait_ge(*when("turned", b + 1))
                turned = k.ps[:, 2 * (b % 2):2 * (b % 2) + 2, :]
                if padded:
                    ins = act.activation(ch4[:, b, 1:33, 1:33], turned.rearrange("p a (h w) -> p (a h) w", w=WW), ACT.Copy)
                else:
                    ins = act.activation(k.ch[:, b * IMG:(b + 1) * IMG], turned.rearrange("p a n -> p (a n)"), ACT.Copy)
                ins.then_inc(s["turned_copied"].h, 1)

            normalise(0)
            for b in range(B):
                if b + 1 < B:
                    normalise(b + 1)
                keep(b)
    k.advance(norm_step=B * per + STAT_OPS, root_ready=1, rstd_ready=2, norm_most=B, norm_rest=B, turned=B,
              turned_copied=B)
    for b in range(B):
        s_back[b].base += 16 if choices else 0
    if choices == 2:
        k.advance(choices_added=B)
    if padded:
        k.advance(border_cleared=1)


def ffn_inputs(k, layer):
    i = k.ins
    if layer == 0:
        return i["L0_ffn_gate_w"], i["L0_ffn_gate_b"], i["L0_ffn_w1"], i["L0_ffn_b1"], i["L0_ffn_w2"], i["L0_ffn_b2"]
    if layer == 1:
        return i["L1_ffn_Wg"], i["L1_ffn_bg"], i["L1_ffn_W1"], i["L1_ffn_b1"], i["L1_ffn_W2"], i["L1_ffn_b2"]
    if layer == 2:
        return i["L2_ffn_gate_w"], i["L2_ffn_gate_b"], i["L2_ffn_W1"], i["L2_ffn_b1"], i["L2_ffn_W2"], i["L2_ffn_b2"]
    return i["L3_ffn_gate_w"], i["L3_ffn_gate_b"], i["L3_ffn_w1"], i["L3_ffn_w2"], i["L3_ffn_w3"], None


ROUTE_STATS = 1 + TPB + STAT_OPS


class Router:

    BANK_A, BANK_B = 6, 7

    def __init__(self, k, layer, ctx, mixed, mixed_ready, room=None, scalar_norm=False):
        nc, f = k.nc, FFN[layer]
        self.k, self.nc, self.layer, self.f = k, nc, layer, f
        self.mixed, self.mixed_ready, self.scalar_norm = mixed, mixed_ready, scalar_norm
        self.E, self.K = E, K = f["E"], f["K"]
        self.T = N * K // P + E
        self.G = E + K - 1
        self.choose_ops = 7 if K == 1 else 14
        self.place_ops = 3 + 3 * K + 2 + (4 if f["capacity"] else 0)
        names = ("mix_turned", "add_step", "route_root", "route_rstd", "rows_ready", "rows_turned", "rows_kept",
                 "rows_copied", "gate_loaded", "logits_ready", "choose_step", "chosen", "exp_ready", "ranked",
                 "place_step", "slots_ready", "rows_sent", "pads_ready", "pads_sent", "weights_loaded", "plan_step", "route_reset")
        self.s = {n: k.sem(n) for n in names}

        taken = 0

        def sb(name, shape, dt=F32):
            nonlocal taken
            size = int(np.prod(shape[1:]))
            if room is None or dt == BF16 or taken + size > room.shape[1]:
                return ctx.enter_context(nc.sbuf_tensor(f"{name}_{layer}", shape, dt))[:]
            view = room[:, taken:taken + size]
            taken += size
            view = view if dt == F32 else view.bitcast(dt)
            if len(shape) == 2:
                return view
            letters = "abc"[:len(shape) - 1]
            return view.rearrange(f"p ({' '.join(letters)}) -> p {' '.join(letters)}",
                                  **{x: n for x, n in zip(letters, shape[1:])})

        self.gw = sb("gate_w", [P, E])
        self.gb = sb("gate_b", [P, E])
        self.turned = sb("turned_rows", [P, IMG])
        self.lg = sb("logits", [P, TPB, E])
        self.lg2 = sb("logits_rest", [P, TPB, E])
        self.oh = [sb("choice0", [P, TPB, E]), sb("choice1", [P, TPB, E])]
        self.top = sb("top", [P, 4, TPB])
        self.ex = sb("exponents", [P, TPB, self.G])
        self.exo = sb("exponentials", [P, TPB, self.G])
        self.msk = sb("chosen_mask", [P, TPB + 1, E], BF16)
        self.pos = sb("position", [P, TPB, E])
        self.posr = sb("position_row", [P, TPB, E])
        self.tmp = sb("routing_tmp", [P, TPB, E])
        self.wsum = sb("weight_sum", [P, 3, TPB])
        self.slotf = sb("slot_float", [P, 2, TPB])
        self.slot = sb("slot", [P, 2, 2, TPB], I32)
        self.padf = sb("pad_row_float", [P, E])
        self.padi = sb("pad_row", [P, E], I32)
        self.nti = sb("tiles_int", [P, E], I32)
        self.ntf = sb("tiles", [P, 3, E])
        self.plan = self.turned[:, 0:3 * 144].rearrange("p (a n) -> p a n", a=3)
        self.rows = [k.rows0, k.rows1]

    def when(self, name, n):
        return self.s[name].h, self.s[name].base + n

    def over_e(self, v):
        return v.unsqueeze(2).to_broadcast([P, TPB, self.E])

    def over_t(self, v):
        return v.unsqueeze(1).to_broadcast([P, TPB, self.E])

    def load_gate(self, sp):
        gate_w, gate_b = ffn_inputs(self.k, self.layer)[:2]
        sp.dma_start(self.gw[:], gate_w).then_inc(self.s["gate_loaded"].h, 16)
        sp.dma_start(self.gb[:], gate_b.partition_broadcast(P)).then_inc(self.s["gate_loaded"].h, 16)
        sp.wait_ge(*self.when("gate_loaded", 32))

    def load_weights(self, sp):
        for dst, src in expert_weight_loads(self.k, self.layer):
            sp.dma_start(dst, src).then_inc(self.s["weights_loaded"].h, 16)

    def send_pads(self, sp):
        sp.wait_ge(*self.when("pads_ready", 1))
        for e in range(self.E):
            row = sp.value_load(self.padi[0:1, e:e + 1], min_val=0, max_val=self.E * REGION)
            sp.dma_start(self.k.dispatched[bass.ds(row, P), :], self.k.pad_rows[:]).then_inc(self.s["pads_sent"].h, 16)
        sp.wait_ge(*self.when("pads_sent", 16 * self.E))

    def turn_back(self, pe, b):
        sem, n = self.mixed_ready(b)
        pe.wait_ge(sem.h, n)
        if b:
            pe.wait_ge(*self.when("place_step", (b - 1) * self.place_ops + 2))
        mixed = self.mixed(b)
        for t in range(TPB):
            bank, at = (self.BANK_A, self.BANK_B)[t // 4], (t % 4) * P
            ins = pe.transpose(self.k.ps[:, bank, at:at + P], mixed[:, t * P:(t + 1) * P], self.k.ident[:])
        ins.then_inc(self.s["mix_turned"].h, 1)

    def turn_rows(self, pe, b):
        pe.wait_ge(*self.when("rows_ready", b + 1))
        for t in range(TPB):
            bank, at = (self.BANK_A, self.BANK_B)[t // 4], (t % 4) * P
            ins = pe.transpose(self.k.ps[:, bank, at:at + P], self.k.rows0[:, b * TPB + t, 0:C], self.k.ident[:])
        ins.then_inc(self.s["rows_turned"].h, 1)

    def gate(self, pe, b):
        E = self.E
        if b == 0:
            pe.wait_ge(*self.when("gate_loaded", 32))
        pe.wait_ge(*self.when("rows_kept", b + 1))
        for t in range(TPB):
            ins = pe.matmul(self.k.ps[:, self.BANK_B, t * E:(t + 1) * E], self.turned[:, t * P:(t + 1) * P], self.gw[:],
                            start=True, stop=True)
        ins.then_inc(self.s["logits_ready"].h, 1)

    def rank(self, pe, b):
        E, msk = self.E, self.msk
        pe.wait_ge(*self.when("chosen", b + 1))
        pe.matmul(self.k.ps[:, self.BANK_B, 0:(TPB + 1) * E], self.k.tri[:], msk[:].rearrange("p t e -> p (t e)"),
                  start=True, stop=True)
        for t in range(TPB):
            later = self.k.ps[:, self.BANK_B, (t + 1) * E:(TPB + 1) * E].rearrange("p (t e) -> p t e", e=E)
            ins = pe.matmul(later, self.k.ones[:], msk[:, t:t + 1, :].to_broadcast([P, TPB - t, E]),
                            start=False, stop=True, skip_group_check=True)
        ins.then_inc(self.s["ranked"].h, 1)

    def reset(self, dve):
        dve.memset(self.k.counts[:], 0.0).then_inc(self.s["route_reset"].h, 1)
        dve.memset(self.msk[:], 0.0).then_inc(self.s["route_reset"].h, 1)
        dve.wait_ge(*self.when("route_reset", 2))

    def add(self, dve, b):
        k, tiles = self.k, slice(b * TPB, (b + 1) * TPB)
        ch = Chain(dve, self.s["add_step"], self.s["add_step"].base + b * ROUTE_STATS)
        dve.wait_ge(*self.when("mix_turned", b + 1))
        xs = k.x[:, tiles, :].rearrange("p t c -> p (t c)")
        both = k.ps[:, self.BANK_A:self.BANK_B + 1, :].rearrange("p a n -> p (a n)")
        ch.link(dve.tensor_tensor(xs, xs, both, ALU.add))
        for t in range(b * TPB, (b + 1) * TPB):
            ch.note(dve.bn_stats(k.stats[:, t, :], k.x[:, t, :]))
        ch.settle()
        finish_stats(dve, k, ch, tiles)
        assert ch.n == ROUTE_STATS

    def norm(self, dve, b):
        k, tiles = self.k, slice(b * TPB, (b + 1) * TPB)
        dve.wait_ge(*self.when("route_root", b + 1))
        dve.reciprocal(k.rstd[:, tiles], k.rstd[:, tiles]).then_inc(self.s["route_rstd"].h, 1)
        dve.wait_ge(*self.when("route_rstd", b + 1))
        for t in range(b * TPB, (b + 1) * TPB):
            ins = dve.tensor_scalar(k.rows0[:, t, 0:C], k.x[:, t, :], k.mean[:, t:t + 1], k.rstd[:, t:t + 1],
                                    ALU.subtract, ALU.mult)
        ins.then_inc(self.s["rows_ready"].h, 1)
        self.address(dve, b)

    def invert(self, dve, b):
        k, tiles = self.k, slice(b * TPB, (b + 1) * TPB)
        dve.wait_ge(*self.when("route_root", b + 1))
        dve.reciprocal(k.rstd[:, tiles], k.rstd[:, tiles]).then_inc(self.s["route_rstd"].h, 1)
        dve.wait_ge(*self.when("route_rstd", 2 * b + 1))
        dve.scalar_tensor_tensor(out=k.var4[:, tiles], in0=k.mean[:, tiles], scalar=-1.0, in1=k.rstd[:, tiles],
                                 op0=ALU.mult, op1=ALU.mult).then_inc(self.s["route_rstd"].h, 1)
        self.address(dve, b)

    def address(self, dve, b):
        k, tiles = self.k, slice(b * TPB, (b + 1) * TPB)
        for c in range(self.K):
            src = k.token_id1[:, tiles] if self.K == 1 else k.token_id[:, tiles, c]
            dve.tensor_copy(self.rows[c][:].bitcast(I32)[:, tiles, C], src)

    def choose(self, dve, b):
        k, E, K = self.k, self.E, self.K
        lg, lg2, oh, top, ex, msk = self.lg, self.lg2, self.oh, self.top, self.ex, self.msk
        ch = Chain(dve, self.s["choose_step"], self.s["choose_step"].base + b * self.choose_ops)

        def best_of(logits, c):
            best, tie = top[:, 2 * c, :], top[:, 2 * c + 1, :]
            ch.link(dve.tensor_reduce(best, logits, AX.X, ALU.max))
            ch.link(dve.tensor_tensor(oh[c][:], logits, self.over_e(best), ALU.is_equal))
            ch.link(dve.tensor_tensor(oh[c][:], oh[c][:], self.over_t(k.rank[:, 0:E]), ALU.mult))
            ch.link(dve.tensor_reduce(tie, oh[c][:], AX.X, ALU.max))
            ch.link(dve.tensor_tensor(oh[c][:], oh[c][:], self.over_e(tie), ALU.is_equal))

        dve.wait_ge(*self.when("logits_ready", b + 1))
        if b == 0:
            dve.wait_ge(*self.when("gate_loaded", 32))
        logits = k.ps[:, self.BANK_B, 0:TPB * E].rearrange("p (t e) -> p t e", e=E)
        ch.link(dve.tensor_tensor(lg[:], logits, self.over_t(self.gb[:]), ALU.add))
        best_of(lg[:], 0)
        if K == 2:
            ch.link(dve.scalar_tensor_tensor(out=lg2[:], in0=oh[0][:], scalar=-1e30, in1=lg[:],
                                             op0=ALU.mult, op1=ALU.add))
            best_of(lg2[:], 1)
            dve.tensor_tensor(msk[:, 0:TPB, :], oh[0][:], oh[1][:], ALU.add).then_inc(self.s["chosen"].h, 1)
            ch.note(dve.tensor_tensor(ex[:, :, E], top[:, 2, :], top[:, 0, :], ALU.subtract))
        else:
            dve.tensor_copy(msk[:, 0:TPB, :], oh[0][:]).then_inc(self.s["chosen"].h, 1)
        ch.note(dve.tensor_tensor(ex[:, :, 0:E], lg[:], self.over_e(top[:, 0, :]), ALU.subtract))
        assert ch.n == self.choose_ops, ch.n

    def place(self, dve, b):
        k, E, K, f = self.k, self.E, self.K, self.f
        oh, pos, tmp, exo, wsum = self.oh, self.pos, self.tmp, self.exo, self.wsum
        tiles = slice(b * TPB, (b + 1) * TPB)
        ch = Chain(dve, self.s["place_step"], self.s["place_step"].base + b * self.place_ops)
        dve.wait_ge(*self.when("ranked", b + 1))
        ranks = k.ps[:, self.BANK_B, 0:(TPB + 1) * E].rearrange("p (t e) -> p t e", e=E)
        ch.link(dve.tensor_tensor(pos[:], ranks[:, 0:TPB, :], self.over_t(k.counts[:, 0:E]), ALU.add))
        ch.note(dve.tensor_tensor(k.counts[:, 0:E], k.counts[:, 0:E], ranks[:, TPB, :], ALU.add))
        ch.link(dve.tensor_tensor(self.posr[:], pos[:], self.over_t(k.region[:, 0:E]), ALU.add))
        for c in range(K):
            ch.link(dve.tensor_tensor(tmp[:], self.posr[:], oh[c][:], ALU.mult))
            ch.link(dve.tensor_reduce(self.slotf[:, c, :], tmp[:], AX.X, ALU.add))
            if b >= 2:
                dve.wait_ge(*self.when("rows_sent", 16 * TPB * K * (b - 1)))
            ch.link(dve.tensor_copy(self.slot[:, b % 2, c, :], self.slotf[:, c, :]))
        dve.wait_ge(*self.when("exp_ready", b + 1))
        w0 = wsum[:, 1, :]
        if f["over_chosen"]:
            ch.link(dve.tensor_scalar(wsum[:, 0, :], exo[:, :, E], 1.0, None, ALU.add))
        else:
            ch.link(dve.tensor_reduce(wsum[:, 0, :], exo[:, :, 0:E], AX.X, ALU.add))
        ch.link(dve.reciprocal(w0, wsum[:, 0, :]))
        if f["capacity"]:
            ch.link(dve.tensor_tensor(tmp[:], pos[:], oh[0][:], ALU.mult))
            ch.link(dve.tensor_reduce(wsum[:, 2, :], tmp[:], AX.X, ALU.add))
            ch.link(dve.tensor_scalar(wsum[:, 2, :], wsum[:, 2, :], float(f["capacity"]), None, ALU.is_le))
            ch.link(dve.tensor_tensor(w0, w0, wsum[:, 2, :], ALU.mult))
        dve.tensor_copy(k.rows0[:, tiles, C + 1], w0).then_inc(self.s["slots_ready"].h, 1)
        if K == 2:
            dve.tensor_tensor(k.rows1[:, tiles, C + 1], w0, exo[:, :, E], ALU.mult).then_inc(self.s["slots_ready"].h, 1)
        assert ch.n == self.place_ops, ch.n

    def make_plan(self, dve):
        k, E, T, ntf, acc = self.k, self.E, self.T, self.ntf, self.plan
        ch = Chain(dve, self.s["plan_step"], self.s["plan_step"].base)
        dve.wait_ge(*self.when("place_step", B * self.place_ops))
        cnt = k.counts[:, 0:E]
        ch.link(dve.tensor_tensor(self.padf[:], k.counts[:, 0:E], k.region[:, 0:E], ALU.add))
        ch.link(dve.tensor_scalar(self.padf[:], self.padf[:], 1.0, None, ALU.add))
        dve.tensor_copy(self.padi[:], self.padf[:]).then_inc(self.s["pads_ready"].h, 1)
        ch.link(dve.tensor_scalar(ntf[:, 0, :], cnt, float(P - 1), None, ALU.add))
        ch.link(dve.tensor_copy(self.nti[:], ntf[:, 0, :]))
        ch.link(dve.tensor_scalar(self.nti[:], self.nti[:], 7, None, ALU.logical_shift_right))
        ch.link(dve.tensor_copy(ntf[:, 0, :], self.nti[:]))
        ch.link(dve.memset(ntf[:, 1, :], 1.0))
        ch.link(dve.tensor_tensor_scan(ntf[:, 2, :], ntf[:, 1, :], ntf[:, 0, :], 0.0, ALU.mult, ALU.add))
        ch.link(dve.tensor_scalar(ntf[:, 1, :], ntf[:, 0, :], float(-P), float(REGION), ALU.mult, ALU.add))
        ch.note(dve.memset(acc[0:1, 0, 0:T], 0.0))
        ch.link(dve.tensor_scalar(acc[0:1, 1, 0:T], k.tile_no[0:1, 0:T], float(P), None, ALU.mult))
        for e in range(E):
            end, skip = ntf[0:1, 2, e:e + 1], ntf[0:1, 1, e:e + 1]
            ch.link(dve.tensor_scalar(acc[0:1, 2, 0:T], k.tile_no[0:1, 0:T], end, None, ALU.is_ge))
            ch.note(dve.tensor_tensor(acc[0:1, 0, 0:T], acc[0:1, 0, 0:T], acc[0:1, 2, 0:T], ALU.add))
            ch.link(dve.scalar_tensor_tensor(out=acc[0:1, 1, 0:T], in0=acc[0:1, 2, 0:T], scalar=skip,
                                             in1=acc[0:1, 1, 0:T], op0=ALU.mult, op1=ALU.add))
        ch.link(dve.tensor_scalar(acc[0:1, 0, 0:T], acc[0:1, 0, 0:T], float(E - 1), None, ALU.min))
        ch.link(dve.tensor_scalar(acc[0:1, 1, 0:T], acc[0:1, 1, 0:T], float(E * REGION), None, ALU.min))
        ch.note(dve.tensor_copy(k.tile_expert[0:1, 0:T], acc[0:1, 0, 0:T]))
        ch.link(dve.tensor_copy(k.tile_row[0:1, 0:T], acc[0:1, 1, 0:T]))
        self.plan_ops = ch.n

    def root(self, act, b):
        k, tiles = self.k, slice(b * TPB, (b + 1) * TPB)
        act.wait_ge(*self.when("add_step", (b + 1) * ROUTE_STATS))
        act.activation(k.rstd[:, tiles], k.var4[:, tiles], ACT.Sqrt, bias=k.eps5,
                       scale=0.25).then_inc(self.s["route_root"].h, 1)

    def normalise(self, act, b):
        k = self.k
        act.wait_ge(*self.when("route_rstd", 2 * b + 2))
        for t in range(b * TPB, (b + 1) * TPB):
            ins = act.activation(k.rows0[:, t, 0:C], k.x[:, t, :], ACT.Identity, scale=k.rstd[:, t:t + 1],
                                 bias=k.var4[:, t:t + 1])
        ins.then_inc(self.s["rows_ready"].h, 1)

    def keep_rows(self, act, b):
        k, tiles = self.k, slice(b * TPB, (b + 1) * TPB)
        act.wait_ge(*self.when("rows_turned", b + 1))
        if b:
            act.wait_ge(*self.when("logits_ready", b))
        act.activation(self.turned[:], k.ps[:, self.BANK_A:self.BANK_B + 1, :].rearrange("p a n -> p (a n)"),
                       ACT.Copy).then_inc(self.s["rows_kept"].h, 1)
        if self.K == 2:
            act.activation(k.rows1[:, tiles, 0:C], k.rows0[:, tiles, 0:C], ACT.Copy).then_inc(self.s["rows_copied"].h, 1)

    def exp(self, act, b):
        act.wait_ge(*self.when("choose_step", (b + 1) * self.choose_ops))
        if b:
            act.wait_ge(*self.when("slots_ready", self.K * b))
        act.activation(self.exo[:], self.ex[:], ACT.Exp).then_inc(self.s["exp_ready"].h, 1)

    def send(self, pool, b):
        K = self.K
        pool.wait_ge(*self.when("slots_ready", K * (b + 1)))
        if K == 2:
            pool.wait_ge(*self.when("rows_copied", b + 1))
        for t in range(TPB):
            for c in range(K):
                pool.indirect_dma_start(
                    out=self.k.dispatched,
                    out_offset=bass.IndirectOffsetOnAxis(ap=self.slot[:, b % 2, c, t:t + 1], axis=0),
                    in_=self.rows[c][:, b * TPB + t, :], in_offset=None).then_inc(self.s["rows_sent"].h, 16)
        pool.wait_ge(*self.when("rows_sent", 16 * TPB * K * (b + 1)))

    def finish_tensor(self, pe):
        for part in (self.turn_back, self.turn_rows, self.gate, self.rank):
            part(pe, B - 1)

    def finish_vector(self, dve):
        for part in (self.add, self.invert if self.scalar_norm else self.norm, self.choose, self.place):
            part(dve, B - 1)
        self.make_plan(dve)

    def finish_scalar(self, act):
        self.root(act, B - 1)
        if self.scalar_norm:
            self.normalise(act, B - 1)
        self.keep_rows(act, B - 1)
        self.exp(act, B - 1)

    def send_all(self, pool):
        for b in range(B):
            self.send(pool, b)

    def tensor_between(self, pe, b, n, after):
        for step, part in zip(after, (self.turn_back, self.turn_rows, self.gate, self.rank)):
            if b and n == step:
                part(pe, b - 1)

    def vector_between(self, dve, b, n, after):
        for step, part in zip(after, (self.add, self.norm, self.choose, self.place)):
            if b and n == step:
                part(dve, b - 1)

    def scalar_between(self, act, b, n, after):
        for step, part in zip(after, (self.root, self.keep_rows, self.exp)):
            if b and n == step:
                part(act, b - 1)

    def done(self):
        E, K = self.E, self.K
        self.k.advance(mix_turned=B, add_step=B * ROUTE_STATS, route_root=B,
                       route_rstd=2 * B if self.scalar_norm else B, rows_ready=B, rows_turned=B,
                       rows_kept=B, rows_copied=B if K == 2 else 0, gate_loaded=32, logits_ready=B,
                       choose_step=B * self.choose_ops, chosen=B, exp_ready=B, ranked=B,
                       place_step=B * self.place_ops, slots_ready=K * B, rows_sent=16 * NT * K, pads_ready=1, pads_sent=16 * E,
                       plan_step=self.plan_ops, route_reset=2)


def expert_weight_loads(k, layer):
    f = FFN[layer]
    E, F = f["E"], f["F"]
    _, _, w1, b1, w2, b2 = ffn_inputs(k, layer)
    first, second = expert_weight_views(k, layer)
    if not f["gated"]:
        return [(first, w1.rearrange("e c f -> c e f")),
                (second, w2.rearrange("e (j h) c -> h e j c", h=P))]
    w3 = w2
    return [(first[:, :, 0:F], w1.rearrange("e c f -> c e f")),
            (first[:, :, F:2 * F], b1.rearrange("e c f -> c e f")),
            (second, w3.rearrange("e (j h) c -> h e j c", h=P))]


def expert_weight_views(k, layer):
    f = FFN[layer]
    E, F = f["E"], f["F"]
    wide = 2 * F if f["gated"] else F
    first = k.wts[:, 0:E * wide].rearrange("p (e f) -> p e f", e=E)
    second = k.wts[:, E * wide:E * wide + E * F].rearrange("p (e j c) -> p e j c", e=E, j=F // P)
    return first, second


RING = 16


def experts(k, layer):
    nc, f = k.nc, FFN[layer]
    E, K, F = f["E"], f["K"], f["F"]
    T = N * K // P + E
    J = F // P
    gated = f["gated"]
    wide = 2 * F if gated else F
    _, _, w1, b1, w2, b2 = ffn_inputs(k, layer)
    first, second = expert_weight_views(k, layer)
    names = ("x_turned", "x_copied", "w_copied", "hidden_ready", "act_ready", "gated_ready",
             "y_ready", "y_scaled", "bias_split", "bias_turned", "bias_kept", "guard_step", "bias_loaded", "bias_rows",
             "bias_parts")
    s = {n: k.sem(n) for n in names}
    s_row = [k.sem(f"slot_rows{r}") for r in range(RING)]
    s_out = [k.sem(f"results_sent{r}") for r in range(RING)]
    loads = 16 * len(expert_weight_loads(k, layer))
    uses = [len(range(r, T, RING)) for r in range(RING)]
    PSX, PSH, PSY = 0, 2, 4
    HB = 4
    vector_copies = not gated and not f["guard"]

    def when(name, n):
        return s[name].h, s[name].base + n

    with ExitStack() as ctx, nc.Block() as block:
        def sb(name, shape, dt=F32):
            return ctx.enter_context(nc.sbuf_tensor(f"{name}_{layer}", shape, dt))

        sizes = (RING * ROW, RING * C, 2 * C, 2 * wide, HB * F, HB * F)
        starts = [sum(sizes[:j]) for j in range(len(sizes))]

        def room(j, n):
            return k.ch[:, starts[j]:starts[j] + sizes[j]].rearrange("p (a n) -> p a n", n=n)

        rt, ys, xt, wc, hs = room(0, ROW), room(1, C), room(2, C), room(3, wide), room(4, F)
        gs = room(5, F) if gated else hs
        if f["guard"]:
            gm = sb("guard", [P, 3, C])
            carry = sb("guard_carry", [P, 2])
        if b2 is not None:
            brows = sb("bias_rows", [E * J, P])
            bcol = sb("bias_columns", [P, E * J])
            bp2 = sb("bias_parts", [3, E, C], BF16)
            brow = sb("bias_row", [E, C])
            bpart = sb("bias_row_parts", [E, 3, C], BF16)

        @block.sync
        def _(sp):
            if b2 is not None:
                sp.dma_start(brows[:], b1.rearrange("e (j h) -> (e j) h", h=P)).then_inc(s["bias_rows"].h, 16)
                sp.dma_start(brow[:], b2).then_inc(s["bias_loaded"].h, 16)
                sp.wait_ge(*when("bias_split", 5))
                for part in range(3):
                    sp.dma_start(bp2[part:part + 1, :, :], bpart[:, part, :]).then_inc(s["bias_parts"].h, 16)

            def load(t, u):
                row = sp.value_load(k.tile_row[0:1, bass.ds(t, 1)], min_val=0, max_val=E * REGION)
                if past(t, RING):
                    sp.wait_ge(s_out[u].h, s_out[u].base + (t - u) * (16 // RING))
                sp.dma_start(rt[:, u, :], k.dispatched[bass.ds(row, P), :]).then_inc(s_row[u].h, 16)
            steps(sp, T, RING, load)

        @block.tensor
        def _(pe):
            if b2 is not None:
                pe.wait_ge(*when("bias_rows", 16))
                pe.transpose(k.ps[:, PSY, 0:E * J], brows[:], k.ident[0:E * J, 0:E * J]).then_inc(s["bias_turned"].h, 1)
                pe.wait_ge(*when("bias_kept", 1))
            pe.wait_ge(k.sem("weights_loaded").h, k.sem("weights_loaded").base + loads)

            def turn_rows(t, u):
                pe.wait_ge(s_row[u].h, s_row[u].base + (t - u) * (16 // RING) + 16)
                pe.transpose(k.ps[:, PSX + u % 2, 0:P], rt[:, u, 0:C], k.ident[:]).then_inc(s["x_turned"].h, 1)

            def hidden(t, u):
                pe.wait_ge(*when("x_copied", t + 1))
                if not vector_copies:
                    pe.wait_ge(*when("w_copied", t + 1))
                for j in range(wide // P):
                    ins = pe.matmul(k.ps[:, PSH + u % 2, j * P:(j + 1) * P], wc[:, u % 2, j * P:(j + 1) * P],
                                    xt[:, u % 2, :], start=True, stop=True)
                ins.then_inc(s["hidden_ready"].h, 1)

            def result(t, u):
                if b2 is not None and not past(t, 1):
                    pe.wait_ge(*when("bias_parts", 16 * 3))
                e = pe.value_load(k.tile_expert[0:1, bass.ds(t, 1)], min_val=0, max_val=E - 1)
                pe.wait_ge(*when("gated_ready" if gated else "act_ready", t + 1))
                bank = k.ps[:, PSY + u % 4, 0:C]
                if b2 is not None:
                    pe.matmul(bank, k.ones[0:3, :], bp2[:, bass.ds(e, 1), :].rearrange("p a f -> p (a f)"),
                              start=True, stop=False)
                for j in range(J):
                    ins = pe.matmul(bank, gs[:, u % HB, j * P:(j + 1) * P],
                                    second[:, bass.ds(e, 1), j, :].rearrange("p a c -> p (a c)"),
                                    start=(b2 is None and j == 0), stop=(j == J - 1))
                ins.then_inc(s["y_ready"].h, 1)

            turn_rows(0, 0)

            def step(t, u, last=False):
                if not last:
                    turn_rows(t + 1, (u + 1) % RING)
                if past(t, 2):
                    result(t - 2, (u - 2) % RING)
                hidden(t, u)

            pipelined(pe, T, RING, step)
            result(T - 2, (T - 2) % RING)
            result(T - 1, (T - 1) % RING)

        @block.scalar
        def _(act):
            if b2 is not None:
                act.wait_ge(*when("bias_turned", 1))
                act.activation(bcol[:], k.ps[:, PSY, 0:E * J], ACT.Copy).then_inc(s["bias_kept"].h, 1)
                act.wait_ge(*when("bias_kept", 1))
            act.wait_ge(k.sem("weights_loaded").h, k.sem("weights_loaded").base + loads)

            def copy_weights(t, u):
                e = act.value_load(k.tile_expert[0:1, bass.ds(t, 1)], min_val=0, max_val=E - 1)
                if past(t, 2):
                    act.wait_ge(*when("hidden_ready", t - 1))
                act.activation(wc[:, u % 2, :], first[:, bass.ds(e, 1), :].rearrange("p a f -> p (a f)"),
                               ACT.Copy).then_inc(s["w_copied"].h, 1)

            def activate(t, u):
                if not gated:
                    e = act.value_load(k.tile_expert[0:1, bass.ds(t, 1)], min_val=0, max_val=E - 1)
                act.wait_ge(*when("hidden_ready", t + 1))
                if gated:
                    if past(t, HB):
                        act.wait_ge(*when("gated_ready", t - HB + 1))
                    act.activation(hs[:, u % HB, :], k.ps[:, PSH + u % 2, 0:F], f["act"]).then_inc(s["act_ready"].h, 1)
                    return
                if past(t, HB):
                    act.wait_ge(*when("y_ready", t - HB + 1))
                for j in range(J):
                    cols = slice(j * P, (j + 1) * P)
                    ins = act.activation(hs[:, u % HB, cols], k.ps[:, PSH + u % 2, cols], f["act"],
                                         bias=bcol[:, bass.ds(e * J + j, 1)])
                ins.then_inc(s["act_ready"].h, 1)

            def step(t, u, last=False):
                if not last and not vector_copies:
                    copy_weights(t + 1, (u + 1) % RING)
                activate(t, u)

            if not vector_copies:
                copy_weights(0, 0)
            pipelined(act, T, RING, step)

        @block.vector
        def _(dve):
            if b2 is not None:
                dve.wait_ge(*when("bias_loaded", 16))
                ch = Chain(dve, s["bias_split"], s["bias_split"].base)
                for part in range(3):
                    ch.link(dve.tensor_copy(bpart[:, part, :], brow[:]))
                    if part < 2:
                        ch.link(dve.tensor_tensor(brow[:], brow[:], bpart[:, part, :], ALU.subtract))

            def copy_weights(t, u):
                e = dve.value_load(k.tile_expert[0:1, bass.ds(t, 1)], min_val=0, max_val=E - 1)
                if past(t, 2):
                    dve.wait_ge(*when("hidden_ready", t - 1))
                dve.tensor_copy(wc[:, u % 2, :], first[:, bass.ds(e, 1), :].rearrange("p a f -> p (a f)"))

            def copy_rows(t, u):
                dve.wait_ge(*when("x_turned", t + 1))
                if past(t, 2) and not vector_copies:
                    dve.wait_ge(*when("hidden_ready", t - 1))
                dve.tensor_copy(xt[:, u % 2, :], k.ps[:, PSX + u % 2, 0:P]).then_inc(s["x_copied"].h, 1)

            def gate(t, u):
                dve.wait_ge(*when("act_ready", t + 1))
                if past(t, HB):
                    dve.wait_ge(*when("y_ready", t - HB + 1))
                dve.tensor_tensor(gs[:, u % HB, :], hs[:, u % HB, :], k.ps[:, PSH + u % 2, F:2 * F],
                                  ALU.mult).then_inc(s["gated_ready"].h, 1)

            def scale(t, u):
                dve.wait_ge(*when("y_ready", t + 1))
                if past(t, RING):
                    dve.wait_ge(s_out[u].h, s_out[u].base + (t - u) * (16 // RING))
                y = ys[:, u, :]
                weight = rt[:, u, C + 1:C + 2]
                if not f["guard"]:
                    dve.tensor_scalar(y, k.ps[:, PSY + u % 4, 0:C], weight, None, ALU.mult).then_inc(s["y_scaled"].h, 1)
                    return
                ch = Chain(dve, s["guard_step"], s["guard_step"].base + t * 7)
                ch.link(dve.tensor_scalar(y, k.ps[:, PSY + u % 4, 0:C], weight, None, ALU.mult))
                ch.note(dve.tensor_scalar(gm[:, 0, :], y, 1e4, -1e4, ALU.min, ALU.max))
                ch.note(dve.scalar_tensor_tensor(out=gm[:, 1, :], in0=y, scalar=0.0, in1=k.zeros[:],
                                                 op0=ALU.mult, op1=ALU.not_equal))
                ch.note(dve.tensor_tensor(gm[:, 2, :], y, y, ALU.not_equal))
                ch.settle()
                ch.note(dve.tensor_copy(carry[:, 0:1], k.zeros[:, 0:1]))
                ch.link(dve.copy_predicated(y, gm[:, 1, :].bitcast(I32), gm[:, 0, :]))
                ch.note(dve.tensor_copy(carry[:, 1:2], k.zeros[:, 0:1]))
                dve.copy_predicated(y, gm[:, 2, :].bitcast(I32), k.zeros[:]).then_inc(s["y_scaled"].h, 1)

            if vector_copies:
                dve.wait_ge(k.sem("weights_loaded").h, k.sem("weights_loaded").base + loads)
                copy_weights(0, 0)
            copy_rows(0, 0)

            def step(t, u, last=False):
                if not last and vector_copies:
                    copy_weights(t + 1, (u + 1) % RING)
                if not last:
                    copy_rows(t + 1, (u + 1) % RING)
                if gated:
                    gate(t, u)
                if past(t, 2):
                    scale(t - 2, (u - 2) % RING)

            pipelined(dve, T, RING, step)
            scale(T - 2, (T - 2) % RING)
            scale(T - 1, (T - 1) % RING)

        @block.gpsimd
        def _(pool):
            last = pool.to_reg(N * K - 1)

            def send(t, u):
                pool.wait_ge(*when("y_scaled", t + 1))
                pool.indirect_dma_start(
                    out=k.returned[0:N * K, :],
                    out_offset=bass.IndirectOffsetOnAxis(ap=rt[:, u, C:C + 1].bitcast(I32), axis=0),
                    in_=ys[:, u, :], in_offset=None, bounds_check=last, oob_is_err=False).then_inc(s_out[u].h, 16)
            spelled_out(T, RING, send)
            for u in range(RING):
                pool.wait_ge(s_out[u].h, s_out[u].base + 16 * uses[u])

    k.advance(x_turned=T, x_copied=T, w_copied=0 if vector_copies else T, hidden_ready=T, act_ready=T,
              y_ready=T, y_scaled=T, weights_loaded=loads)
    if gated:
        k.advance(gated_ready=T)
    if f["guard"]:
        k.advance(guard_step=7 * T)
    if b2 is not None:
        k.advance(bias_split=5, bias_loaded=16, bias_rows=16, bias_parts=16 * 3, bias_turned=1, bias_kept=1)
    for r in range(RING):
        s_row[r].base += 16 * uses[r]
        s_out[r].base += 16 * uses[r]


def load_columns(sp, sem, dst, vectors):
    for j, v in enumerate(vectors):
        sp.dma_start(dst[:, j:j + 1], v.rearrange("(c a) -> c a", a=1)).then_inc(sem.h, 16)


def mixer_fractal(k):
    nc, i = k.nc, k.ins
    RED = i["L0_conv_w1"].shape[1]
    names = ("mix_loaded", "mix_v", "mix_range", "mix_allmax", "mix_logs", "mix_contrast", "mix_squares", "mix_energy",
             "mix_sq1", "mix_prep", "mix_mm", "mix_excite", "mix_sig", "mix_root", "mix_sim", "mix_used", "mix_minus")
    s = {n: k.sem(n) for n in names}

    def when(name, n):
        return s[name].h, s[name].base + n

    SIDE = 47
    slope_scale = 0.1 / LN2
    norm_scale = slope_scale * float(np.sqrt(5.0) * LN2)
    xch = k.ch[:, 0:N].rearrange("p (b n) -> p b n", b=B)
    slope = k.flat(k.rows0).rearrange("p (b n) -> p b n", b=B)[:, :, 0:IMG]
    energy = k.mixed.rearrange("p (b n) -> p b n", b=B)
    with ExitStack() as ctx, nc.Block() as block:
        def sb(name, shape, dt=F32):
            return ctx.enter_context(nc.sbuf_tensor(name, shape, dt))

        w = k.wts[:]
        pad = w[:, 0:SIDE * SIDE].rearrange("p (h w) -> p h w", w=SIDE)
        tmp = w[:, 2210:2210 + 47 * 46]
        s2 = w[:, 4372:4372 + 46 * 46].rearrange("p (h w) -> p h w", w=46)
        s4 = w[:, 6488:6488 + 44 * 44].rearrange("p (h w) -> p h w", w=44)
        s8 = w[:, 8424:8424 + 40 * 40].rearrange("p (h w) -> p h w", w=40)
        logs = sb("logs", [P, 4, IMG])
        s16 = logs[:, 3, :].rearrange("p (h w) -> p h w", w=WW)
        minus = sb("minus_identity", [P, P])
        contrast = [k.ps[:, 2 * j:2 * j + 2, :].rearrange("p a n -> p (a n)") for j in range(3)]
        sqr = [w[:, 10024:11048], w[:, 11048:12072], k.ch[:, N:N + IMG]]
        vec = sb("mix_vectors", [P, 8])
        w1 = sb("squeeze_w", [P, RED])
        w2 = sb("excite_w", [RED, P])
        b1 = sb("squeeze_b", [RED, 1])
        rng = sb("range", [P, 2, B])
        rngall = sb("range_all", [P, 2, B])
        inv = sb("range_inverse", [P, B])
        lowest = sb("lowest", [P, B])
        sums = sb("slope_sums", [P, B])
        sq = sb("squeezed", [P, B])
        hid = sb("squeeze_hidden", [RED, B])
        exc = sb("excite", [P, B])
        gain = sb("gain", [P, B])
        bn = sb("bn_scale", [P, 4])
        route = Router(k, 0, ctx, lambda b: energy[:, b, :], lambda b: (s["mix_used"], s["mix_used"].base + b + 1),
                       room=w[:, 8192:10024], scalar_norm=True)

        @block.sync
        def _(sp):
            load_columns(sp, s["mix_loaded"], vec, [i["L0_conv_b2"], i["L0_conv_gamma"], i["L0_conv_beta"],
                                                    i["L0_conv_moving_mean"], i["L0_conv_moving_var"]])
            sp.dma_start(w1[:], i["L0_conv_w1"]).then_inc(s["mix_loaded"].h, 16)
            sp.dma_start(w2[:], i["L0_conv_w2"]).then_inc(s["mix_loaded"].h, 16)
            sp.dma_start(b1[:], i["L0_conv_b1"].rearrange("(c a) -> c a", a=1)).then_inc(s["mix_loaded"].h, 16)
            sp.wait_ge(*when("mix_loaded", 16 * 8))
            sp.wait_ge(*when("mix_logs", 4 * B))
            route.load_gate(sp)
            route.load_weights(sp)
            route.send_pads(sp)

        BOX = 9
        PRE = 7

        @block.vector
        def _(dve):
            ch = Chain(dve, s["mix_v"], s["mix_v"].base)
            dve.tensor_scalar(minus[:], k.ident[:], -1.0, None, ALU.mult).then_inc(s["mix_minus"].h, 1)
            ch.note(dve.memset(pad, 0.0))
            ch.note(dve.tensor_reduce(rng[:, 0, :], xch, AX.X, ALU.max))
            ch.link(dve.tensor_reduce(rng[:, 1, :], xch, AX.X, ALU.min))
            dve.tensor_scalar(rng[:, 1, :], rng[:, 1, :], -1.0, None, ALU.mult).then_inc(s["mix_range"].h, 1)
            dve.wait_ge(*when("mix_allmax", 1))
            ch.link(dve.tensor_tensor(inv[:], rngall[:, 0, :], rngall[:, 1, :], ALU.add))
            ch.link(dve.tensor_scalar(inv[:], inv[:], 1e-7, None, ALU.add))
            ch.link(dve.reciprocal(inv[:], inv[:]))
            ch.link(dve.tensor_scalar(lowest[:], rngall[:, 1, :], -1.0, None, ALU.mult))
            assert ch.n == PRE

            def make_slope(b):
                dve.wait_ge(*when("mix_squares", 5 * b + 3))
                dve.scalar_tensor_tensor(out=slope[:, b, :], in0=contrast[0], scalar=3.0, in1=slope[:, b, :], op0=ALU.mult,
                                         op1=ALU.add, accum_out=sums[:, b:b + 1]).then_inc(s["mix_sim"].h, 1)

            for b in range(B):
                ch = Chain(dve, s["mix_v"], s["mix_v"].base + PRE + b * BOX)
                src = xch[:, b, :].rearrange("p (h w) -> p h w", w=WW)
                ch.link(dve.tensor_scalar(pad[:, 7:39, 7:39], src, lowest[:, b:b + 1], inv[:, b:b + 1],
                                          ALU.subtract, ALU.mult))

                def double(out, src, rows, cols, shift):
                    t = tmp[:, 0:rows * (cols - shift)].rearrange("p (h w) -> p h w", h=rows)
                    ch.link(dve.tensor_tensor(t, src[:, :, 0:cols - shift], src[:, :, shift:cols], ALU.add))
                    ch.link(dve.tensor_tensor(out, t[:, 0:rows - shift, :], t[:, shift:rows, :], ALU.add))

                if b:
                    dve.wait_ge(*when("mix_logs", 4 * b - 3))
                double(s2, pad, 47, 47, 1)
                if b:
                    dve.wait_ge(*when("mix_logs", 4 * b - 2))
                double(s4, s2, 46, 46, 2)
                if b:
                    make_slope(b - 1)
                    dve.wait_ge(*when("mix_logs", 4 * b - 1))
                double(s8, s4, 44, 44, 4)
                if b:
                    dve.wait_ge(*when("mix_contrast", 3 * b))
                double(s16, s8, 40, 40, 8)
                assert ch.n == BOX
            make_slope(B - 1)

            ch = Chain(dve, s["mix_prep"], s["mix_prep"].base)
            dve.wait_ge(*when("mix_sim", B))
            dve.wait_ge(*when("mix_loaded", 16 * 8))
            ch.link(dve.tensor_scalar(sq[:], sums[:], slope_scale / IMG, None, ALU.mult))
            dve.wait_ge(*when("mix_sq1", 1))
            ch.link(dve.reciprocal(bn[:, 1:2], bn[:, 0:1]))
            ch.link(dve.tensor_tensor(bn[:, 1:2], bn[:, 1:2], vec[:, 1:2], ALU.mult))
            ch.link(dve.tensor_tensor(bn[:, 2:3], bn[:, 1:2], vec[:, 3:4], ALU.mult))
            ch.link(dve.tensor_tensor(bn[:, 2:3], vec[:, 2:3], bn[:, 2:3], ALU.subtract))
            ch.link(dve.tensor_scalar(bn[:, 3:4], bn[:, 1:2], slope_scale, None, ALU.mult))
            dve.wait_ge(*when("mix_excite", 2))
            ch.link(dve.tensor_tensor(gain[:], inv[:], exc[:], ALU.mult))
            route.reset(dve)
            BLEND = 6

            for b in range(B):
                at, sig = energy[:, b, :], sqr[b % 2]
                if b:
                    route.add(dve, b - 1)
                dve.wait_ge(*when("mix_root", b + 1))
                c2 = Chain(dve, s["mix_sim"], s["mix_sim"].base + B + b * BLEND)
                c2.note(dve.tensor_scalar(logs[:, 0, :], at, 1e-7, None, ALU.add))
                c2.link(dve.tensor_scalar(logs[:, 1, :], xch[:, b, :], lowest[:, b:b + 1], gain[:, b:b + 1],
                                          ALU.subtract, ALU.mult))
                if b:
                    route.invert(dve, b - 1)
                c2.link(dve.reciprocal(logs[:, 0, :], logs[:, 0, :]))
                c2.note(dve.tensor_tensor(logs[:, 0, :], slope[:, b, :], logs[:, 0, :], ALU.mult))
                c2.link(dve.tensor_tensor(logs[:, 2, :], logs[:, 1, :], sig, ALU.subtract))
                if b:
                    route.choose(dve, b - 1)
                c2.link(dve.tensor_tensor(logs[:, 3, :], logs[:, 0, :], logs[:, 2, :], ALU.mult))
                assert c2.n == BLEND
                dve.tensor_tensor(at, logs[:, 1, :], logs[:, 3, :], ALU.subtract).then_inc(s["mix_used"].h, 1)
                if b:
                    route.place(dve, b - 1)
                dve.wait_ge(*when("mix_used", b + 1))
            route.finish_vector(dve)

        @block.gpsimd
        def _(pool):
            pool.wait_ge(*when("mix_range", 1))
            pool.partition_all_reduce(rngall[:].rearrange("p a b -> p (a b)"), rng[:].rearrange("p a b -> p (a b)"), P,
                                      bass.bass_isa.ReduceOp.max).then_inc(s["mix_allmax"].h, 1)
            for b in range(B):
                c2 = Chain(pool, s["mix_energy"], s["mix_energy"].base + b * 3)
                pool.wait_ge(*when("mix_squares", 5 * (b + 1)))
                c2.link(pool.tensor_tensor(sqr[0], sqr[0], sqr[1], ALU.add))
                c2.link(pool.tensor_tensor(sqr[0], sqr[0], sqr[2], ALU.add))
                c2.link(pool.tensor_tensor(energy[:, b, :], sqr[0], energy[:, b, :], ALU.mult))
            route.send_all(pool)

        @block.scalar
        def _(act):
            views = (s2[:, 7:39, 7:39], s4[:, 6:38, 6:38], s8[:, 4:36, 4:36], s16)

            def log(b, j):
                act.wait_ge(*when("mix_v", PRE + b * BOX + 1 + 2 * (j + 1)))
                if b and j == 0:
                    act.wait_ge(*when("mix_contrast", 3 * b))
                act.activation(logs[:, j, :].rearrange("p (h w) -> p h w", w=WW), views[j], ACT.Ln,
                               bias=k.eps7).then_inc(s["mix_logs"].h, 1)

            def squares(b):
                if b:
                    act.wait_ge(*when("mix_energy", 3 * b))
                for j, scale in ((1, 0.5 ** 0.5), (0, 0.5 ** 0.5), (2, 0.5)):
                    act.wait_ge(*when("mix_contrast", 3 * b + (1, 0, 2).index(j) + 1))
                    act.activation(sqr[j], contrast[j], ACT.Square, scale=scale).then_inc(s["mix_squares"].h, 1)
                    if j == 1:
                        act.activation(slope[:, b, :], contrast[1], ACT.Copy).then_inc(s["mix_squares"].h, 1)

            def square_slope(b):
                act.wait_ge(*when("mix_sim", b + 1))
                act.activation(energy[:, b, :], slope[:, b, :], ACT.Square, scale=norm_scale).then_inc(s["mix_squares"].h, 1)

            for b in range(B):
                if b:
                    squares(b - 1)
                for j in range(3):
                    log(b, j)
                if b:
                    square_slope(b - 1)
                log(b, 3)
            squares(B - 1)
            square_slope(B - 1)
            act.wait_ge(*when("mix_loaded", 16 * 8))
            act.activation(bn[:, 0:1], vec[:, 4:5], ACT.Sqrt, bias=k.eps3).then_inc(s["mix_sq1"].h, 1)
            act.wait_ge(*when("mix_mm", 1))
            act.activation(hid[:], k.ps[0:RED, 0, 0:B], ACT.Relu, bias=b1[:]).then_inc(s["mix_excite"].h, 1)
            act.wait_ge(*when("mix_mm", 2))
            act.activation(exc[:], k.ps[:, 1, 0:B], ACT.Sigmoid, bias=vec[:, 0:1]).then_inc(s["mix_excite"].h, 1)
            act.wait_ge(*when("mix_energy", 3 * B))
            act.wait_ge(*when("mix_prep", 6))

            def gates(b):
                if b >= 2:
                    act.wait_ge(*when("mix_used", b - 1))
                act.activation(sqr[b % 2], slope[:, b, :], ACT.Sigmoid, scale=bn[:, 3:4],
                               bias=bn[:, 2:3]).then_inc(s["mix_sig"].h, 1)
                act.wait_ge(*when("mix_sig", 2 * b + 1))
                act.activation(slope[:, b, :], slope[:, b, :], ACT.Square, scale=norm_scale).then_inc(s["mix_sig"].h, 1)
                act.activation(energy[:, b, :], energy[:, b, :], ACT.Sqrt).then_inc(s["mix_root"].h, 1)

            gates(0)
            for b in range(B):
                if b:
                    route.root(act, b - 1)
                    route.normalise(act, b - 1)
                    route.keep_rows(act, b - 1)
                if b + 1 < B:
                    gates(b + 1)
                if b:
                    route.exp(act, b - 1)
            route.finish_scalar(act)

        @block.tensor
        def _(pe):
            pe.wait_ge(*when("mix_minus", 1))
            plus = k.ident[:]
            terms = {1: ((plus, 2), (minus[:], 1)), 0: ((plus, 3), (minus[:], 0)),
                     2: ((plus, 3), (plus, 0), (minus[:], 2), (minus[:], 1))}
            for b in range(B):
                pe.wait_ge(*when("mix_logs", 4 * b + 3))
                if b:
                    pe.wait_ge(*when("mix_squares", 5 * b))
                    pe.wait_ge(*when("mix_sim", b))
                for n, (j, parts) in enumerate(terms.items()):
                    if n == 1:
                        pe.wait_ge(*when("mix_logs", 4 * b + 4))
                    for half in range(2):
                        for m, (weights, scale) in enumerate(parts):
                            ins = pe.matmul(k.ps[:, 2 * j + half, :], weights,
                                            logs[:, scale, half * BANK:(half + 1) * BANK],
                                            start=(m == 0), stop=(m == len(parts) - 1))
                    ins.then_inc(s["mix_contrast"].h, 1)
            pe.wait_ge(*when("mix_loaded", 16 * 8))
            pe.wait_ge(*when("mix_prep", 1))
            pe.wait_ge(*when("mix_squares", 5 * B))
            pe.matmul(k.ps[0:RED, 0, 0:B], w1[:], sq[:], start=True, stop=True).then_inc(s["mix_mm"].h, 1)
            pe.wait_ge(*when("mix_excite", 1))
            pe.matmul(k.ps[:, 1, 0:B], w2[:], hid[:], start=True, stop=True).then_inc(s["mix_mm"].h, 1)
            for b in range(B - 1):
                route.turn_back(pe, b)
                route.turn_rows(pe, b)
                route.gate(pe, b)
                route.rank(pe, b)
            route.finish_tensor(pe)
    route.done()


def mixer_involution(k):
    nc, i = k.nc, k.ins
    RED = i["L1_conv_W1"].shape[1]
    TAPS = 9
    GROUPS = i["L1_conv_W2"].shape[1] // TAPS
    GC = C // GROUPS
    PER = 2 * TAPS
    names = ("inv_loaded", "inv_prep", "inv_bias", "inv_ones", "inv_hidden", "inv_part", "inv_rest", "inv_kernel", "inv_product",
             "inv_sum", "inv_stored")
    s = {n: k.sem(n) for n in names}
    loads = 16 * (4 * 2 + 2)
    PREP = 1 + 5 + 8 + 3 + 1

    def when(name, n):
        return s[name].h, s[name].base + n

    ch4 = k.ch[:].rearrange("p (b h w) -> p b h w", b=B, h=34)
    with ExitStack() as ctx, nc.Block() as block:
        def sb(name, shape, dt=F32):
            return ctx.enter_context(nc.sbuf_tensor(name, shape, dt))

        tail = slice(7 * TPB * ROW, 7 * TPB * ROW + 2 * BANK)
        hidden_parts = k.flat(k.rows0)[:, tail].bitcast(BF16).rearrange("p (x a n) -> p x a n", x=2, a=2)
        hid_a, hid_b = hidden_parts[:, 0], hidden_parts[:, 1]
        rest = sb("hidden_rest", [P, BANK])
        prods = [k.flat(k.rows1)[:, tail][:, 0:BANK], k.flat(k.rows1)[:, tail][:, BANK:2 * BANK]]
        used = 2 * FFN[1]["E"] * FFN[1]["F"]
        spans = k.wts[:, used:used + TAPS * C].bitcast(BF16).rearrange("p (x n) -> p x n", x=2)
        span_a, span_b = spans[:, 0], spans[:, 1]
        gather = k.wts[:, used + TAPS * C:used + 2 * TAPS * C].rearrange("p (t c) -> p t c", t=TAPS)
        left = used + 2 * TAPS * C
        mixed_first = k.wts[:, left:left + IMG]
        prods.append(k.wts[:, left + IMG:left + IMG + BANK])
        prods.append(sb("last_product", [P, BANK])[:])
        bias_row = k.flat(k.rows1)[0:1, 0:TAPS * C]

        def mixed(b):
            return mixed_first if b == 0 else k.ch[:, (b - 1) * 34 * 34:(b - 1) * 34 * 34 + IMG]

        route = Router(k, 1, ctx, mixed, lambda b: (s["inv_stored"], s["inv_stored"].base + 2 * (b + 1)))
        w1 = sb("reduce_w", [P, RED])
        w1r = sb("reduce_w_four_times", [P, 4, RED])
        w2 = sb("span_w", [P, GROUPS * TAPS])
        w2p = sb("span_w_parts", [P, 5, GROUPS * TAPS], BF16)
        b2row = sb("span_b_row", [1, GROUPS * TAPS])
        b1 = sb("reduce_b", [P, 1])
        b2 = sb("span_b", [P, TAPS])

        @block.sync
        def _(sp):
            for g in range(4):
                rows = slice(RED * g, RED * (g + 1))
                sp.dma_start(w2[rows, :], i["L1_conv_W2"]).then_inc(s["inv_loaded"].h, 16)
                sp.dma_start(b1[rows, :], i["L1_conv_b1"].rearrange("(c a) -> c a", a=1)).then_inc(s["inv_loaded"].h, 16)
            sp.dma_start(w1[:], i["L1_conv_W1"]).then_inc(s["inv_loaded"].h, 16)
            sp.dma_start(b2row[:], i["L1_conv_b2"].rearrange("(a c) -> a c", a=1)).then_inc(s["inv_loaded"].h, 16)
            sp.wait_ge(*when("inv_loaded", loads))
            route.load_gate(sp)
            route.load_weights(sp)
            route.send_pads(sp)

        def window(b, half, dy, dx):
            return ch4[:, bass.ds(b, 1), 16 * half + dy:16 * half + dy + 16, dx:dx + WW].rearrange("p a h w -> p (a h) w")

        @block.gpsimd
        def _(pool):
            pool.memset(gather, 1.0).then_inc(s["inv_ones"].h, 1)
            pool.wait_ge(*when("inv_ones", 1))
            pool.affine_select(out=gather, in_=gather, compare_op=ALU.is_ge, fill=0.0, base=0,
                               pattern=[[P, TAPS], [-TAPS, C]], channel_multiplier=1).then_inc(s["inv_ones"].h, 1)
            pool.wait_ge(*when("inv_ones", 2))
            pool.affine_select(out=gather, in_=gather, compare_op=ALU.is_ge, fill=0.0, base=TAPS - 1,
                               pattern=[[-P, TAPS], [TAPS, C]], channel_multiplier=-1).then_inc(s["inv_ones"].h, 1)
            route.send_all(pool)

        @block.tensor
        def _(pe):
            pe.wait_ge(*when("inv_prep", PREP - 1))
            for tap in range(TAPS):
                ins = pe.matmul(k.ps[:, 0, tap:tap + 1], bias_row[:, tap * P:(tap + 1) * P], k.ident[0:1, 0:1],
                                start=True, stop=True)
            ins.then_inc(s["inv_bias"].h, 1)
            pe.wait_ge(*when("inv_ones", 3))
            pe.wait_ge(*when("inv_prep", PREP))

            LAG = 3

            def hidden(b, half):
                if 2 * b + half:
                    pe.wait_ge(*when("inv_rest", 3 * (2 * b + half) - 2))
                pe.matmul(k.ps[:, 0, :].rearrange("p (h w) -> p h w", w=WW), w1r[:].rearrange("p a r -> p (a r)"),
                          window(b, half, 1, 1), start=True, stop=True).then_inc(s["inv_hidden"].h, 1)

            def kernel_entries(b, n):
                half, tap = n // TAPS, n % TAPS
                if tap == 0:
                    pe.wait_ge(*when("inv_rest", 3 * (2 * b + half) + 3))
                if b * PER + n >= 3:
                    pe.wait_ge(*when("inv_product", b * PER + n - 2))
                cols = slice(tap * P, (tap + 1) * P)
                pe.matmul(k.ps[:, 1 + n % 3, :], span_a[:, cols], hid_a[:, half, :], start=True, stop=False)
                pe.matmul(k.ps[:, 1 + n % 3, :], span_b[:, cols], hid_b[:, half, :], start=False,
                          stop=True).then_inc(s["inv_kernel"].h, 1)

            def add_up(b, n):
                half, tap = n // TAPS, n % TAPS
                if tap == 0 and b:
                    pe.wait_ge(*when("inv_stored", 2 * b + half - 1))
                pe.wait_ge(*when("inv_product", b * PER + n + 1))
                pe.matmul(k.ps[:, 4 + half, :], gather[:, tap, :], prods[(b * PER + n) % 4], start=(tap == 0),
                          stop=(tap == TAPS - 1)).then_inc(s["inv_sum"].h, 1)

            hidden(0, 0)
            for b in range(B):
                for n in range(PER):
                    if n == 3:
                        hidden(b, 1)
                    if n == 11 and b + 1 < B:
                        hidden(b + 1, 0)
                    kernel_entries(b, n)
                    if n >= LAG:
                        add_up(b, n - LAG)
                    route.tensor_between(pe, b, n, (2, 7, 10, 13))
                for n in range(PER - LAG, PER):
                    add_up(b, n)
            route.finish_tensor(pe)

        @block.scalar
        def _(act):
            act.wait_ge(*when("inv_loaded", loads))

            def bias(b, half):
                h = 2 * b + half
                act.wait_ge(*when("inv_hidden", h + 1))
                if b:
                    act.wait_ge(*when("inv_kernel", (b - 1) * PER + (half + 1) * TAPS))
                act.activation(hid_a[:, half, :], k.ps[:, 0, :], ACT.Identity, bias=b1[:]).then_inc(s["inv_part"].h, 1)
                act.wait_ge(*when("inv_part", 5 * h + 1))
                act.activation(hid_b[0:RED, half, :], hid_a[0:RED, half, :], ACT.Copy).then_inc(s["inv_part"].h, 1)
                act.wait_ge(*when("inv_rest", 3 * h + 1))
                act.activation(hid_b[RED:2 * RED, half, :], rest[RED:2 * RED, :], ACT.Copy).then_inc(s["inv_part"].h, 1)
                act.activation(hid_a[2 * RED:P, half, :], rest[2 * RED:P, :], ACT.Copy).then_inc(s["inv_part"].h, 1)
                act.activation(hid_b[2 * RED:3 * RED, half, :], rest[2 * RED:3 * RED, :], ACT.Copy).then_inc(s["inv_part"].h, 1)

            def store(b, half):
                act.wait_ge(*when("inv_sum", b * PER + (half + 1) * TAPS))
                act.activation(mixed(b)[:, half * BANK:(half + 1) * BANK], k.ps[:, 4 + half, :],
                               ACT.Copy).then_inc(s["inv_stored"].h, 1)

            bias(0, 0)
            for b in range(B):
                if b:
                    route.root(act, b - 1)
                bias(b, 1)
                if b:
                    route.keep_rows(act, b - 1)
                store(b, 0)
                if b:
                    route.exp(act, b - 1)
                if b + 1 < B:
                    bias(b + 1, 0)
                store(b, 1)
            route.finish_scalar(act)

        @block.vector
        def _(dve):
            dve.wait_ge(*when("inv_loaded", loads))
            dve.tensor_copy(w1r[:], w1[:].unsqueeze(1).to_broadcast([P, 4, RED])).then_inc(s["inv_prep"].h, 1)
            ch = Chain(dve, s["inv_prep"], s["inv_prep"].base + 1)
            ch.link(dve.tensor_copy(w2p[:, 0, :], w2[:]))
            ch.link(dve.tensor_tensor(w2[:], w2[:], w2p[:, 0, :], ALU.subtract))
            ch.link(dve.tensor_copy(w2p[:, 1, :], w2[:]))
            ch.link(dve.tensor_tensor(w2[:], w2[:], w2p[:, 1, :], ALU.subtract))
            ch.link(dve.tensor_copy(w2p[:, 2, :], w2[:]))
            for x, parts in ((3, (0, 1, 0, 1)), (4, (2, 0, 2, 1))):
                for g, part in enumerate(parts):
                    rows = slice(RED * g, RED * (g + 1))
                    ch.note(dve.tensor_copy(w2p[rows, x, :], w2p[rows, part, :]))
            ch.settle()
            for p, dst, src in ((P, span_a, w2p[:, 3, :]), (P, span_b, w2p[:, 4, :]), (1, bias_row, b2row[:])):
                for g in range(GROUPS):
                    ins = dve.tensor_copy(
                        dst[:, g * GC * TAPS:(g + 1) * GC * TAPS].rearrange("p (c t) -> p c t", t=TAPS),
                        src[:, g * TAPS:(g + 1) * TAPS].unsqueeze(1).to_broadcast([p, GC, TAPS]))
                ins.then_inc(s["inv_prep"].h, 1)
            dve.wait_ge(*when("inv_bias", 1))
            dve.tensor_copy(b2[:], k.ps[:, 0, 0:TAPS]).then_inc(s["inv_prep"].h, 1)
            dve.wait_ge(*when("inv_prep", PREP))

            def leave(b, half):
                h = 2 * b + half
                dve.wait_ge(*when("inv_part", 5 * h + 1))
                if h:
                    dve.wait_ge(*when("inv_rest", 3 * h))
                dve.scalar_tensor_tensor(out=rest[:], in0=k.ps[:, 0, :], scalar=b1[:], in1=hid_a[:, half, :], op0=ALU.add,
                                         op1=ALU.subtract).then_inc(s["inv_rest"].h, 1)

            def third(b, half):
                dve.wait_ge(*when("inv_part", 5 * (2 * b + half) + 5))
                g1, g3 = slice(RED, 2 * RED), slice(3 * RED, P)
                dve.tensor_tensor(hid_b[g1, half, :], rest[g1, :], hid_b[g1, half, :], ALU.subtract).then_inc(s["inv_rest"].h, 1)
                dve.tensor_tensor(hid_b[g3, half, :], rest[g3, :], hid_a[g3, half, :], ALU.subtract).then_inc(s["inv_rest"].h, 1)

            leave(0, 0)
            third(0, 0)

            route.reset(dve)
            for b in range(B):
                for n in range(PER):
                    half, tap = n // TAPS, n % TAPS
                    dve.wait_ge(*when("inv_kernel", b * PER + n + 1))
                    if b * PER + n >= 4:
                        dve.wait_ge(*when("inv_sum", b * PER + n - 3))
                    dve.scalar_tensor_tensor(
                        out=prods[(b * PER + n) % 4].rearrange("p (h w) -> p h w", w=WW),
                        in0=k.ps[:, 1 + n % 3, :].rearrange("p (h w) -> p h w", w=WW), scalar=b2[:, tap:tap + 1],
                        in1=window(b, half, tap // 3, tap % 3), op0=ALU.add, op1=ALU.mult).then_inc(s["inv_product"].h, 1)
                    route.vector_between(dve, b, n, (3, 5, 11, 15))
                    if n in (4, 6):
                        (leave if n == 4 else third)(b, 1)
                    if n in (12, 14) and b + 1 < B:
                        (leave if n == 12 else third)(b + 1, 0)
            route.finish_vector(dve)
    route.done()


def mixer_spline(k):
    nc, i = k.nc, k.ins
    KN = i["L2_conv_spline_weight"].shape[2]
    knots = [float(v) for v in np.linspace(-1.0, 1.0, KN, dtype=np.float32)]
    CHUNKS = N // BANK
    names = ("spl_loaded", "spl_v", "spl_scaled", "spl_wturned", "spl_wcopied", "spl_root", "spl_abs", "spl_basis",
             "spl_base", "spl_basis_used", "spl_silu", "spl_bn", "spl_range")
    s = {n: k.sem(n) for n in names}

    def when(name, n):
        return s[name].h, s[name].base + n

    with ExitStack() as ctx, nc.Block() as block:
        def sb(name, shape, dt=F32):
            return ctx.enter_context(nc.sbuf_tensor(name, shape, dt))

        base_w = sb("base_w", [P, C])
        spw = sb("spline_w", [P, C, KN])
        scl = sb("spline_scaler", [P, C])
        spt = sb("spline_w_turned", [P, KN, C])
        vec = sb("spline_vectors", [P, 8])
        bn = sb("spline_bn", [P, 2, 4])
        rng = sb("channel_range", [P, 3])
        used = 2 * FFN[2]["E"] * FFN[2]["F"]
        DEEP = 6
        room = k.wts[:, used:used + (4 + 2 * DEEP) * BANK].rearrange("p (a n) -> p a n", n=BANK)
        xu, silu, dist, hat = (room[:, a:b, :] for a, b in ((0, 2), (2, 4), (4, 4 + DEEP), (4 + DEEP, 4 + 2 * DEEP)))
        kn = sb("minus_knots", [P, KN])
        route = Router(k, 2, ctx, lambda b: k.ch[:, b * IMG:(b + 1) * IMG],
                       lambda b: (s["spl_bn"], s["spl_bn"].base + 2 * (b + 1)))

        @block.sync
        def _(sp):
            load_columns(sp, s["spl_loaded"], vec, [i[f"L2_conv_bn_{a}_{b}"] for a in ("base", "spline")
                                                    for b in ("gamma", "beta", "mean", "var")])
            sp.dma_start(base_w[:], i["L2_conv_base_weight"]).then_inc(s["spl_loaded"].h, 16)
            sp.dma_start(spw[:], i["L2_conv_spline_weight"]).then_inc(s["spl_loaded"].h, 16)
            sp.dma_start(scl[:], i["L2_conv_spline_scaler"]).then_inc(s["spl_loaded"].h, 16)
            sp.wait_ge(*when("spl_loaded", 16 * 11))
            route.load_gate(sp)
            route.load_weights(sp)
            route.send_pads(sp)

        @block.gpsimd
        def _(pool):
            route.send_all(pool)

        @block.vector
        def _(dve):
            ch = Chain(dve, s["spl_v"], s["spl_v"].base)
            for j, v in enumerate(knots):
                ins = dve.memset(kn[:, j:j + 1], -v)
            ins.then_inc(s["spl_range"].h, 1)
            dve.wait_ge(*when("spl_loaded", 16 * 11))
            dve.tensor_tensor(spw[:], spw[:], scl[:].unsqueeze(2).to_broadcast([P, C, KN]),
                              ALU.mult).then_inc(s["spl_scaled"].h, 1)
            ch.note(dve.tensor_reduce(rng[:, 0:1], k.ch[:, 0:N], AX.X, ALU.min))
            ch.link(dve.tensor_reduce(rng[:, 1:2], k.ch[:, 0:N], AX.X, ALU.max))
            ch.link(dve.tensor_tensor(rng[:, 1:2], rng[:, 1:2], rng[:, 0:1], ALU.subtract))
            ch.link(dve.tensor_scalar(rng[:, 1:2], rng[:, 1:2], 1e-7, None, ALU.add))
            ch.link(dve.reciprocal(rng[:, 2:3], rng[:, 1:2]))
            dve.wait_ge(*when("spl_root", 2))
            for j in range(2):
                g, bt, mn = (vec[:, 4 * j + a:4 * j + a + 1] for a in range(3))
                ch.link(dve.reciprocal(bn[:, j, 1:2], bn[:, j, 0:1]))
                ch.link(dve.tensor_tensor(bn[:, j, 1:2], bn[:, j, 1:2], g, ALU.mult))
                ch.link(dve.tensor_tensor(bn[:, j, 2:3], bn[:, j, 1:2], mn, ALU.mult))
                ch.link(dve.tensor_tensor(bn[:, j, 2:3], bt, bn[:, j, 2:3], ALU.subtract))
                ch.link(dve.tensor_scalar(bn[:, j, 3:4], bn[:, j, 1:2], -1.0, None, ALU.mult))

            k.spline_pre = ch.n

            def to_unit_range(c, u):
                if c >= 2:
                    dve.wait_ge(*when("spl_abs", KN * (c - 1)))
                dve.tensor_scalar(xu[:, u, :], k.ch[:, c * BANK:(c + 1) * BANK], rng[:, 0:1], rng[:, 2:3],
                                  ALU.subtract, ALU.mult).then_inc(s["spl_v"].h, 1)

            def add_base(c, u):
                dve.wait_ge(*when("spl_basis_used", (c + 1) * KN))
                dve.wait_ge(*when("spl_silu", 2 * (c + 1)))
                dve.scalar_tensor_tensor(out=k.ch[:, c * BANK:(c + 1) * BANK], in0=k.ps[:, 2 + u, :],
                                         scalar=bn[:, 1, 3:4], in1=silu[:, u, :], op0=ALU.mult,
                                         op1=ALU.add).then_inc(s["spl_bn"].h, 1)

            def chunk(c, u):
                for j in range(KN):
                    n = c * KN + j
                    dve.wait_ge(*when("spl_abs", n + 1))
                    if n >= DEEP:
                        dve.wait_ge(*when("spl_basis_used", n - DEEP + 1))
                    dve.tensor_scalar(hat[:, n % DEEP, :], dist[:, n % DEEP, :], 1.0, 1.0, ALU.min,
                                      ALU.subtract).then_inc(s["spl_basis"].h, 1)
                    if j == 2 and c:
                        add_base(c - 1, 1 - u)
                    if j == 1 and c + 1 < CHUNKS:
                        to_unit_range(c + 1, 1 - u)
                    route.vector_between(dve, c // 2, u * KN + j, (6, 9, 14, 17))
            to_unit_range(0, 0)
            route.reset(dve)
            spelled_out(CHUNKS, 2, chunk)
            add_base(CHUNKS - 1, 1)
            route.finish_vector(dve)

        @block.scalar
        def _(act):
            act.wait_ge(*when("spl_loaded", 16 * 11))
            for j in range(2):
                act.activation(bn[:, j, 0:1], vec[:, 4 * j + 3:4 * j + 4], ACT.Sqrt, bias=k.eps3).then_inc(s["spl_root"].h, 1)
            for t in range(KN):
                act.wait_ge(*when("spl_wturned", t + 1))
                act.activation(spt[:, t, :], k.ps[:, 4 + t % 2, 0:P], ACT.Copy).then_inc(s["spl_wcopied"].h, 1)
            act.wait_ge(*when("spl_range", 1))

            def base(c, u):
                act.wait_ge(*when("spl_base", c + 1))
                if c >= 2:
                    act.wait_ge(*when("spl_bn", c - 1))
                act.activation(silu[:, u, :], k.ps[:, u, :], ACT.Silu, scale=bn[:, 0, 1:2],
                               bias=bn[:, 0, 2:3]).then_inc(s["spl_silu"].h, 1)
                act.wait_ge(*when("spl_silu", 2 * c + 1))
                act.activation(silu[:, u, :], silu[:, u, :], ACT.Identity, bias=bn[:, 1, 2:3]).then_inc(s["spl_silu"].h, 1)

            def chunk(c, u):
                act.wait_ge(s["spl_v"].h, s["spl_v"].base + k.spline_pre + c + 1)
                for j in range(KN):
                    n = c * KN + j
                    if n >= DEEP:
                        act.wait_ge(*when("spl_basis", n - DEEP + 1))
                    act.activation(dist[:, n % DEEP, :], xu[:, u, :], ACT.Abs, bias=kn[:, j:j + 1]).then_inc(s["spl_abs"].h, 1)
                    if j == 5:
                        base(c, u)
                    route.scalar_between(act, c // 2, u * KN + j, (8, 14, 17))
            spelled_out(CHUNKS, 2, chunk)
            route.finish_scalar(act)

        @block.tensor
        def _(pe):
            pe.wait_ge(*when("spl_scaled", 1))
            for t in range(KN):
                if t >= 2:
                    pe.wait_ge(*when("spl_wcopied", t - 1))
                pe.transpose(k.ps[:, 4 + t % 2, 0:P], spw[:, :, t], k.ident[:]).then_inc(s["spl_wturned"].h, 1)
            pe.wait_ge(*when("spl_wcopied", KN))

            def chunk(c, u):
                if past(c, 2):
                    pe.wait_ge(*when("spl_silu", 2 * (c - 1)))
                pe.matmul(k.ps[:, u, :], base_w[:], k.ch[:, bass.ds(c * BANK, BANK)], start=True,
                          stop=True).then_inc(s["spl_base"].h, 1)
                if past(c, 2):
                    pe.wait_ge(*when("spl_bn", c - 1))
                for j in range(KN):
                    pe.wait_ge(*when("spl_basis", c * KN + j + 1))
                    ins = pe.matmul(k.ps[:, 2 + u, :], spt[:, j, :], hat[:, (c * KN + j) % DEEP, :], start=(j == 0), stop=(j == KN - 1))
                    ins.then_inc(s["spl_basis_used"].h, 1)
                    route.tensor_between(pe, c // 2, u * KN + j, (1, 9, 12, 15))
            spelled_out(CHUNKS, 2, chunk)
            route.finish_tensor(pe)
    route.done()


def mixer_attention(k):
    nc, i = k.nc, k.ins
    names = ("att_loaded", "att_sq", "att_norm", "att_root", "att_unit", "att_turned", "att_copied", "att_value",
             "att_vcopied", "att_vsq", "att_sim", "att_relu", "att_square", "att_y", "att_out")
    s = {n: k.sem(n) for n in names}

    def when(name, n):
        return s[name].h, s[name].base + n

    xft = k.ch[:, 0:N]
    with ExitStack() as ctx, nc.Block() as block:
        def sb(name, shape, dt=F32):
            return ctx.enter_context(nc.sbuf_tensor(name, shape, dt))

        w = sb("att_w", [P, C])
        ssq = sb("att_norms", [P, NT])
        val = k.flat(k.rows1).rearrange("p (b n) -> p b n", b=B)[:, :, 0:IMG]

        def mixed(b):
            at = (b - 1) * IMG if b else N
            return k.ch[:, at:at + IMG]

        route = Router(k, 3, ctx, mixed, lambda b: (s["att_out"], s["att_out"].base + 2 * (b + 1)))
        work = sb("att_work", [P, 4, BANK])
        rel = work[:, 0:3, :]
        late = k.flat(k.rows0)[:, 7 * TPB * ROW:7 * TPB * ROW + 2 * BANK]
        r2 = [work[:, 3, :], late[:, 0:BANK], late[:, BANK:2 * BANK]]
        unused0, unused1 = (work[:, a:a + 2, :].rearrange("p a (t c) -> p (a t) c", c=C) for a in (0, 2))

        @block.sync
        def _(sp):
            sp.dma_start(w[:], i["L3_conv_W"]).then_inc(s["att_loaded"].h, 16)
            sp.wait_ge(*when("att_loaded", 16))
            route.load_gate(sp)
            route.load_weights(sp)
            route.send_pads(sp)

        @block.gpsimd
        def _(pool):
            route.send_all(pool)

        KEYS = TPB
        PER = 2 * KEYS
        STEPS = B * PER

        @block.scalar
        def _(act):
            def norms(b):
                for t in range(b * TPB, (b + 1) * TPB, 2):
                    ins = act.activation(unused0[:, t // 2 % 8, :], k.xn[:, t, :], ACT.Square, accum_out=ssq[:, t:t + 1])
                ins.then_inc(s["att_sq"].h, 1)

            def root(b):
                v = ssq[:, b * TPB:(b + 1) * TPB]
                act.wait_ge(*when("att_norm", 2 * b + 1))
                act.activation(v, v, ACT.Sqrt).then_inc(s["att_root"].h, 1)

            def values(b, u):
                act.wait_ge(*when("att_value", b + 1))
                act.activation(val[:, b, :], k.ps[:, 4 + 2 * u:6 + 2 * u, :].rearrange("p a n -> p (a n)"),
                               ACT.Copy).then_inc(s["att_vcopied"].h, 1)
                act.wait_ge(*when("att_turned", b + 1))
                act.activation(xft[:, b * IMG:(b + 1) * IMG], k.ps[:, 2 * u:2 * u + 2, :].rearrange("p a n -> p (a n)"),
                               ACT.Copy).then_inc(s["att_copied"].h, 1)

            norms(0)
            for b in range(B):
                if b + 1 < B:
                    norms(b + 1)
                root(b)
                if b:
                    values(b - 1, (b - 1) % 2)
            values(B - 1, 1)

            for g in range(STEPS):
                act.wait_ge(*when("att_sim", g + 1))
                if g >= 3:
                    act.wait_ge(*when("att_square", g - 2))
                act.activation(rel[:, g % 3, :], k.ps[:, g % 4, :], ACT.Relu).then_inc(s["att_relu"].h, 1)
                route.scalar_between(act, g // PER, g % PER, (6, 11, 14))
            route.finish_scalar(act)

        @block.vector
        def _(dve):
            def norms(b):
                for t in range(b * TPB + 1, (b + 1) * TPB, 2):
                    ins = dve.scalar_tensor_tensor(out=unused1[:, t // 2 % 8, :], in0=k.xn[:, t, :], scalar=1.0,
                                                   in1=k.xn[:, t, :], op0=ALU.mult, op1=ALU.mult,
                                                   accum_out=ssq[:, t:t + 1])
                ins.then_inc(s["att_vsq"].h, 1)

            norms(0)
            for b in range(B):
                v = ssq[:, b * TPB:(b + 1) * TPB]
                dve.wait_ge(*when("att_sq", b + 1))
                dve.wait_ge(*when("att_vsq", b + 1))
                dve.tensor_scalar(v, v, 1e-12, None, ALU.max).then_inc(s["att_norm"].h, 1)
                if b + 1 < B:
                    norms(b + 1)
                dve.wait_ge(*when("att_root", b + 1))
                dve.reciprocal(v, v).then_inc(s["att_norm"].h, 1)
                dve.wait_ge(*when("att_norm", 2 * b + 2))
                for t in range(b * TPB, (b + 1) * TPB):
                    ins = dve.tensor_scalar(k.xn[:, t, :], k.xn[:, t, :], ssq[:, t:t + 1], None, ALU.mult)
                ins.then_inc(s["att_unit"].h, 1)

            def store(b, h):
                dve.wait_ge(*when("att_y", b * PER + (h + 1) * KEYS))
                dve.tensor_copy(mixed(b)[:, h * BANK:(h + 1) * BANK], k.ps[:, 4 + h, :]).then_inc(s["att_out"].h, 1)

            route.reset(dve)
            for g in range(STEPS):
                b, n = g // PER, g % PER
                dve.wait_ge(*when("att_relu", g + 1))
                if g >= 3:
                    dve.wait_ge(*when("att_y", g - 2))
                dve.tensor_tensor(r2[g % 3], rel[:, g % 3, :], rel[:, g % 3, :], ALU.mult).then_inc(s["att_square"].h, 1)
                if n == 2 and b:
                    store(b - 1, 1)
                if n == 10:
                    store(b, 0)
                route.vector_between(dve, b, n, (4, 7, 12, 15))
            store(B - 1, 1)
            route.finish_vector(dve)

        @block.tensor
        def _(pe):
            pe.wait_ge(*when("att_loaded", 16))

            def values(b, u):
                if past(b, 2):
                    pe.wait_ge(*when("att_copied", b - 1))
                for t in range(TPB):
                    bank, at = 4 + 2 * u + t // 4, (t % 4) * P
                    ins = pe.matmul(k.ps[:, bank, at:at + P], xft[:, bass.ds(b * IMG + t * P, P)], w[:],
                                    start=True, stop=True)
                ins.then_inc(s["att_value"].h, 1)
                pe.wait_ge(*when("att_unit", b + 1))
                for t in range(TPB):
                    bank, at = 2 * u + t // 4, (t % 4) * P
                    ins = pe.transpose(k.ps[:, bank, at:at + P],
                                       k.xn[:, bass.ds(b * TPB + t, 1), :].rearrange("p a c -> p (a c)"), k.ident[:])
                ins.then_inc(s["att_turned"].h, 1)
            spelled_out(B, 2, values)
            pe.wait_ge(*when("att_copied", B))

            def sim(g):
                b, h, j = g // PER, g % PER // KEYS, g % KEYS
                if g >= 4:
                    pe.wait_ge(*when("att_relu", g - 3))
                pe.matmul(k.ps[:, g % 4, :], xft[:, b * IMG + j * P:b * IMG + (j + 1) * P],
                          xft[:, b * IMG + h * BANK:b * IMG + (h + 1) * BANK], start=True, stop=True).then_inc(s["att_sim"].h, 1)

            def gather(g):
                b, h, j = g // PER, g % PER // KEYS, g % KEYS
                pe.wait_ge(*when("att_square", g + 1))
                if j == 0 and b:
                    pe.wait_ge(*when("att_out", 2 * b + h - 1))
                pe.matmul(k.ps[:, 4 + h, :], val[:, b, j * P:(j + 1) * P], r2[g % 3], start=(j == 0),
                          stop=(j == KEYS - 1)).then_inc(s["att_y"].h, 1)

            for g in range(3):
                sim(g)
            for g in range(STEPS):
                if g + 3 < STEPS:
                    sim(g + 3)
                gather(g)
                route.tensor_between(pe, g // PER, g % PER, (1, 8, 10, 13))
            route.finish_tensor(pe)
    route.done()


def finish(k):
    nc = k.nc
    s_add, s_out = k.sem("last_added"), k.sem("stored")
    src = k.returned[:].rearrange("(t p k) c -> p t (k c)", p=P, k=2)
    dst = k.out.rearrange("b h w c -> (b h w) c").rearrange("(t p) c -> p t c", p=P)
    with ExitStack() as ctx, nc.Block() as block:
        buf = [k.flat(k.rows0)[:, 0:4 * TPB * 2 * C].rearrange("p (b t c) -> p b t c", b=4, t=TPB),
               k.flat(k.rows1)[:, 0:4 * TPB * 2 * C].rearrange("p (b t c) -> p b t c", b=4, t=TPB)]
        s_each = [k.sem(f"rows_back{b}") for b in range(B)]

        @block.sync
        def _(sp):
            for b in range(B):
                sp.dma_start(buf[b // 4][:, b % 4], src[:, b * TPB:(b + 1) * TPB, :]).then_inc(s_each[b].h, 16)
            for b in range(B):
                sp.wait_ge(s_add.h, 2 * (b + 1))
                sp.dma_start(dst[:, b * TPB:(b + 1) * TPB, :], k.x[:, b * TPB:(b + 1) * TPB, :]).then_inc(s_out.h, 16)
            sp.wait_ge(s_out.h, 16 * B)

        @block.vector
        def _(dve):
            for b in range(B):
                dve.wait_ge(s_each[b].h, s_each[b].base + 16)
                xs = k.x[:, b * TPB:(b + 1) * TPB, :]
                for c in range(2):
                    dve.tensor_tensor(xs, xs, buf[b // 4][:, b % 4, :, c * C:(c + 1) * C], ALU.add).then_inc(s_add.h, 1)
                    dve.wait_ge(s_add.h, 2 * b + c + 1)


def build(nc, ins, out):
    with ExitStack() as ctx:
        k = Core(nc, ctx, ins, out)
        constants(k)
        mixers = [mixer_fractal, mixer_involution, mixer_spline, mixer_attention]
        for layer in range(4):
            norm_mixer(k, layer)
            mixers[layer](k)
            experts(k, layer)
        finish(k)


NAMES = ["x",
         "L0_conv_w1", "L0_conv_b1", "L0_conv_w2", "L0_conv_b2", "L0_conv_gamma", "L0_conv_beta",
         "L0_conv_moving_mean", "L0_conv_moving_var",
         "L0_ffn_gate_w", "L0_ffn_gate_b", "L0_ffn_w1", "L0_ffn_b1", "L0_ffn_w2", "L0_ffn_b2",
         "L1_conv_W1", "L1_conv_b1", "L1_conv_W2", "L1_conv_b2",
         "L1_ffn_Wg", "L1_ffn_bg", "L1_ffn_W1", "L1_ffn_b1", "L1_ffn_W2", "L1_ffn_b2",
         "L2_conv_base_weight", "L2_conv_spline_weight", "L2_conv_spline_scaler",
         "L2_conv_bn_base_gamma", "L2_conv_bn_base_beta", "L2_conv_bn_base_mean", "L2_conv_bn_base_var",
         "L2_conv_bn_spline_gamma", "L2_conv_bn_spline_beta", "L2_conv_bn_spline_mean", "L2_conv_bn_spline_var",
         "L2_ffn_gate_w", "L2_ffn_gate_b", "L2_ffn_W1", "L2_ffn_b1", "L2_ffn_W2", "L2_ffn_b2",
         "L3_conv_W", "L3_ffn_gate_w", "L3_ffn_gate_b", "L3_ffn_w1", "L3_ffn_w2", "L3_ffn_w3"]


def kernel(**inputs):
    import concourse.bacc as bacc
    from concourse.bass_utils import run_bass_kernel_spmd

    nc = bacc.Bacc("TRN2", target_bir_lowering=False, num_devices=1)
    arrays, ins = {}, {}
    for name in NAMES:
        a = np.ascontiguousarray(inputs[name])
        arrays[f"in_{name}"] = a
        ins[name] = nc.dram_tensor(f"in_{name}", a.shape, F32, kind="ExternalInput").ap()
    out = nc.dram_tensor("out", (B, HH, WW, C), F32, kind="ExternalOutput").ap()
    build(nc, ins, out)
    r = run_bass_kernel_spmd(nc, [arrays], core_ids=[0])
    return r.results[0]["out"]
```
